# Optimizing a Trainium2 kernel written in Bass

```python
import numpy as np
import jax
import jax.numpy as jnp

def _softmax(x, axis=-1):
    return jax.nn.softmax(x, axis=axis)

def _gelu(x):
    return jax.nn.gelu(x, approximate=True)

def _silu(x):
    return jax.nn.silu(x)

def _sigmoid(x):
    return jax.nn.sigmoid(x)

def _layernorm(x, axis=-1, eps=1e-05):
    m = jnp.mean(x, axis=axis, keepdims=True)
    v = jnp.var(x, axis=axis, keepdims=True)
    return (x - m) / jnp.sqrt(v + eps)

def _scatter_add(tgt, idx, src, axis=0):
    return tgt.at[idx].add(src)

def _segment_sum(src, seg, n):
    return jax.ops.segment_sum(src, seg, n)
kernel_name = 'mk_perceiver_d1_seqx_r4_dbbf55'

def setup_inputs(seed: int=0):
    np.random.seed(seed)
    _w = jnp.asarray

    def _rec_inputs():
        import jax
        import jax.numpy as jnp
        _rk = jax.random.key(seed)
        x = 7.22e-05 + 1 * jax.random.normal(jax.random.fold_in(_rk, 1), (32, 64, 256), jnp.float32)
        _lenS = 64 - jax.random.randint(jax.random.fold_in(_rk, 7), (32,), 0, max(1, 64 // 4) + 1, jnp.int32)
        _lenS2 = 1601 - jax.random.randint(jax.random.fold_in(_rk, 8), (32,), 0, max(1, 1601 // 4) + 1, jnp.int32)
        _ctx_1024P = jax.random.normal(jax.random.fold_in(_rk, 11), (32, 16, 256), jnp.float32)
        _ctx_1024c = jax.random.dirichlet(jax.random.fold_in(_rk, 511), 0.3 * jnp.ones((16,), jnp.float32), (32, 1601))
        _ctx_1024t = jnp.einsum('bsk,bkd->bsd', _ctx_1024c, _ctx_1024P)
        _ctx_1024t = _ctx_1024t * jax.lax.rsqrt(jnp.mean(jnp.square(_ctx_1024t)) + 1e-12) * 0.953939
        ctx_1024 = 4.13588e-05 + 0.999923 * (_ctx_1024t + 0.3 * jax.random.normal(jax.random.fold_in(_rk, 611), (32, 1601, 256), jnp.float32))
        return (x, ctx_1024)
    x, ctx_1024 = _rec_inputs()

    def _L0_xattn_setup():
        import jax, jax.numpy as jnp
        import numpy as np
        LN_EPS = 1e-05
        key = jax.random.key(seed)
        ks = jax.random.split(key, 12)
        B, S, D = (4, 512, 256)
        s = 1.0 / np.sqrt(D)
        return {'query': jax.random.normal(ks[0], (B, S, D), jnp.float32), 'key_in': jax.random.normal(ks[1], (B, S, D), jnp.float32), 'value': jax.random.normal(ks[2], (B, S, D), jnp.float32), 'Wq': jax.random.normal(ks[3], (D, D), jnp.float32) * s, 'bq': jax.random.normal(ks[4], (D,), jnp.float32) * s, 'Wk': jax.random.normal(ks[5], (D, D), jnp.float32) * s, 'bk': jax.random.normal(ks[6], (D,), jnp.float32) * s, 'Wv': jax.random.normal(ks[7], (D, D), jnp.float32) * s, 'bv': jax.random.normal(ks[8], (D,), jnp.float32) * s, 'gamma': jnp.ones((D,), jnp.float32), 'beta': jnp.zeros((D,), jnp.float32)}
    _L0_xattn_all = _L0_xattn_setup()
    _L0_xattn_in = {k: v for k, v in _L0_xattn_all.items() if k in ('Wq', 'bq', 'Wk', 'bk', 'Wv', 'bv', 'gamma', 'beta')}
    del _L0_xattn_all

    def _L0_attn_setup():
        import jax, jax.numpy as jnp
        import numpy as np
        D = 256
        H = 16
        S = 2
        MAX_LEN = 512
        HEAD_DIM = D // H // S
        DV = D // H
        SCALING = (D // H) ** (-0.5)
        key = jax.random.key(seed)
        k1, k2, k3, k4, k5, k6 = jax.random.split(key, 6)
        L, B = (2046, 4)
        input_tensor = jax.random.normal(k1, (L, B, D), dtype=jnp.float32)
        w_kv = jax.random.normal(k2, (MAX_LEN // S, MAX_LEN), dtype=jnp.float32) / np.sqrt(MAX_LEN)
        w_q = jax.random.normal(k3, (D // S, D), dtype=jnp.float32) / np.sqrt(D)
        b_q = jax.random.normal(k4, (D // S,), dtype=jnp.float32) * 0.01
        w_out = jax.random.normal(k5, (D, D), dtype=jnp.float32) / np.sqrt(D)
        b_out = jax.random.normal(k6, (D,), dtype=jnp.float32) * 0.01
        return {'input_tensor': input_tensor, 'w_kv': w_kv, 'w_q': w_q, 'b_q': b_q, 'w_out': w_out, 'b_out': b_out}
    _L0_attn_all = _L0_attn_setup()
    _L0_attn_in = {k: v for k, v in _L0_attn_all.items() if k in ('w_kv', 'w_q', 'b_q', 'w_out', 'b_out')}
    del _L0_attn_all

    def _L0_ffn_setup():
        import jax, jax.numpy as jnp
        import numpy as np
        DIM = 256
        EXPERT_DIM = 128
        N_EXPERTS = 16
        TOPK = 2
        SHARED_HIDDEN = EXPERT_DIM * TOPK
        B, T = (4, 256)

        def _moe_forward(x, router_w, router_bias, up_proj, gate_proj, down_proj, sh_gate, sh_up, sh_down):
            Bb, Tt, D = x.shape
            flat = x.reshape(Bb * Tt, D)
            N = flat.shape[0]
            logits = flat @ router_w.T
            topk_scores, topk_idx = jax.lax.top_k(logits + router_bias, TOPK)
            topk_scores = jax.nn.softmax(topk_scores, axis=-1)
            combine = jnp.zeros((N, N_EXPERTS), flat.dtype)
            combine = combine.at[jnp.arange(N)[:, None], topk_idx].add(topk_scores)
            up_all = jnp.einsum('nd,kde->nke', flat, up_proj)
            gate_all = jnp.einsum('nd,kde->nke', flat, gate_proj)
            hidden = jax.nn.silu(gate_all) * up_all
            down_all = jnp.einsum('nke,ked->nkd', hidden, down_proj)
            out = jnp.einsum('nk,nkd->nd', combine, down_all)
            sh_hidden = jax.nn.silu(flat @ sh_gate.T) * (flat @ sh_up.T)
            out = out + sh_hidden @ sh_down.T
            return out.reshape(Bb, Tt, D)
        key = jax.random.key(seed)
        ks = jax.random.split(key, 9)
        std = 0.02
        return {'x': jax.random.normal(ks[0], (B, T, DIM), jnp.float32), 'router_w': jax.random.normal(ks[1], (N_EXPERTS, DIM), jnp.float32) * std, 'router_bias': jnp.zeros((N_EXPERTS,), jnp.float32), 'up_proj': jax.random.normal(ks[2], (N_EXPERTS, DIM, EXPERT_DIM), jnp.float32) * std, 'gate_proj': jax.random.normal(ks[3], (N_EXPERTS, DIM, EXPERT_DIM), jnp.float32) * std, 'down_proj': jax.random.normal(ks[4], (N_EXPERTS, EXPERT_DIM, DIM), jnp.float32) * std, 'sh_gate': jax.random.normal(ks[5], (SHARED_HIDDEN, DIM), jnp.float32) * std, 'sh_up': jax.random.normal(ks[6], (SHARED_HIDDEN, DIM), jnp.float32) * std, 'sh_down': jax.random.normal(ks[7], (DIM, SHARED_HIDDEN), jnp.float32) * std}
    _L0_ffn_all = _L0_ffn_setup()
    _L0_ffn_in = {k: v for k, v in _L0_ffn_all.items() if k in ('router_w', 'router_bias', 'up_proj', 'gate_proj', 'down_proj', 'sh_gate', 'sh_up', 'sh_down')}
    del _L0_ffn_all
    return {'x': x, 'ctx_1024': ctx_1024, 'L0_xattn_Wq': _L0_xattn_in['Wq'], 'L0_xattn_bq': _L0_xattn_in['bq'], 'L0_xattn_Wk': _L0_xattn_in['Wk'], 'L0_xattn_bk': _L0_xattn_in['bk'], 'L0_xattn_Wv': _L0_xattn_in['Wv'], 'L0_xattn_bv': _L0_xattn_in['bv'], 'L0_xattn_gamma': _L0_xattn_in['gamma'], 'L0_xattn_beta': _L0_xattn_in['beta'], 'L0_attn_w_kv': _L0_attn_in['w_kv'], 'L0_attn_w_q': _L0_attn_in['w_q'], 'L0_attn_b_q': _L0_attn_in['b_q'], 'L0_attn_w_out': _L0_attn_in['w_out'], 'L0_attn_b_out': _L0_attn_in['b_out'], 'L0_ffn_router_w': _L0_ffn_in['router_w'], 'L0_ffn_router_bias': _L0_ffn_in['router_bias'], 'L0_ffn_up_proj': _L0_ffn_in['up_proj'], 'L0_ffn_gate_proj': _L0_ffn_in['gate_proj'], 'L0_ffn_down_proj': _L0_ffn_in['down_proj'], 'L0_ffn_sh_gate': _L0_ffn_in['sh_gate'], 'L0_ffn_sh_up': _L0_ffn_in['sh_up'], 'L0_ffn_sh_down': _L0_ffn_in['sh_down']}

def reference(x, ctx_1024, L0_xattn_Wq, L0_xattn_bq, L0_xattn_Wk, L0_xattn_bk, L0_xattn_Wv, L0_xattn_bv, L0_xattn_gamma, L0_xattn_beta, L0_attn_w_kv, L0_attn_w_q, L0_attn_b_q, L0_attn_w_out, L0_attn_b_out, L0_ffn_router_w, L0_ffn_router_bias, L0_ffn_up_proj, L0_ffn_gate_proj, L0_ffn_down_proj, L0_ffn_sh_gate, L0_ffn_sh_up, L0_ffn_sh_down):
    import jax
    import jax.numpy as jnp

    def _L0_xattn_ref(query, key_in, value, Wq, bq, Wk, bk, Wv, bv, gamma, beta):
        import jax, jax.numpy as jnp
        import numpy as np
        LN_EPS = 1e-05
        q = jnp.einsum('bsd,df->bsf', query, Wq) + bq
        k = jnp.einsum('bsd,df->bsf', key_in, Wk) + bk
        v = jnp.einsum('bsd,df->bsf', value, Wv) + bv
        attn = jnp.einsum('bqd,bkd->bqk', q, k)
        probs = jax.nn.softmax(attn, axis=-1)
        result = jnp.einsum('bqk,bkd->bqd', probs, v)
        x = result + query
        mu = jnp.mean(x, axis=-1, keepdims=True)
        var = jnp.mean((x - mu) ** 2, axis=-1, keepdims=True)
        return (x - mu) * jax.lax.rsqrt(var + LN_EPS) * gamma + beta

    def _L0_attn_ref(input_tensor, w_kv, w_q, b_q, w_out, b_out):
        import jax, jax.numpy as jnp
        import numpy as np
        D = 256
        H = 16
        S = 2
        MAX_LEN = 512
        HEAD_DIM = D // H // S
        DV = D // H
        SCALING = (D // H) ** (-0.5)
        L, B, _ = input_tensor.shape
        P = L // S + 1
        X = jnp.transpose(input_tensor, (1, 0, 2))
        q = X @ w_q.T + b_q
        Wp = w_kv.T[:L, :P]
        v = jnp.einsum('bld,lp->bdp', X, Wp)
        k = jnp.einsum('blc,lp->bcp', q, Wp)
        q = q * SCALING
        qh = q.reshape(B, L, H, HEAD_DIM).transpose(0, 2, 1, 3)
        kh = k.reshape(B, HEAD_DIM, H, P).transpose(0, 2, 1, 3)
        vh = v.reshape(B, DV, H, P).transpose(0, 2, 3, 1)
        attn = jnp.einsum('bhld,bhdp->bhlp', qh, kh)
        attn = jax.nn.softmax(attn.astype(jnp.float32), axis=-1).astype(attn.dtype)
        out = jnp.einsum('bhlp,bhpd->bhld', attn, vh)
        out = out.transpose(0, 2, 3, 1).reshape(B, L, D)
        out = out @ w_out.T + b_out
        return jnp.transpose(out, (1, 0, 2))

    def _L0_ffn_ref(x, router_w, router_bias, up_proj, gate_proj, down_proj, sh_gate, sh_up, sh_down):
        import jax, jax.numpy as jnp
        import numpy as np
        DIM = 256
        EXPERT_DIM = 128
        N_EXPERTS = 16
        TOPK = 2
        SHARED_HIDDEN = EXPERT_DIM * TOPK
        B, T = (4, 256)

        def _moe_forward(x, router_w, router_bias, up_proj, gate_proj, down_proj, sh_gate, sh_up, sh_down):
            Bb, Tt, D = x.shape
            flat = x.reshape(Bb * Tt, D)
            N = flat.shape[0]
            logits = flat @ router_w.T
            topk_scores, topk_idx = jax.lax.top_k(logits + router_bias, TOPK)
            topk_scores = jax.nn.softmax(topk_scores, axis=-1)
            combine = jnp.zeros((N, N_EXPERTS), flat.dtype)
            combine = combine.at[jnp.arange(N)[:, None], topk_idx].add(topk_scores)
            up_all = jnp.einsum('nd,kde->nke', flat, up_proj)
            gate_all = jnp.einsum('nd,kde->nke', flat, gate_proj)
            hidden = jax.nn.silu(gate_all) * up_all
            down_all = jnp.einsum('nke,ked->nkd', hidden, down_proj)
            out = jnp.einsum('nk,nkd->nd', combine, down_all)
            sh_hidden = jax.nn.silu(flat @ sh_gate.T) * (flat @ sh_up.T)
            out = out + sh_hidden @ sh_down.T
            return out.reshape(Bb, Tt, D)
        return _moe_forward(x, router_w, router_bias, up_proj, gate_proj, down_proj, sh_gate, sh_up, sh_down)
    x = x + _L0_xattn_ref(_layernorm(x, axis=-1), ctx_1024, ctx_1024, L0_xattn_Wq, L0_xattn_bq, L0_xattn_Wk, L0_xattn_bk, L0_xattn_Wv, L0_xattn_bv, L0_xattn_gamma, L0_xattn_beta)
    x = x + _L0_attn_ref(_layernorm(x, axis=-1), L0_attn_w_kv, L0_attn_w_q, L0_attn_b_q, L0_attn_w_out, L0_attn_b_out)
    x = x + _L0_ffn_ref(_layernorm(x, axis=-1), L0_ffn_router_w, L0_ffn_router_bias, L0_ffn_up_proj, L0_ffn_gate_proj, L0_ffn_down_proj, L0_ffn_sh_gate, L0_ffn_sh_up, L0_ffn_sh_down)
    return x

_drawn_inputs = setup_inputs


def setup_inputs(seed=0):
    import zlib

    import numpy as np

    out = dict(_drawn_inputs(seed))
    spreads = {'L0_xattn_gamma': (1.0, 0.2),
     'L0_xattn_beta': (0.0, 0.1),
     'L0_ffn_router_bias': (0.0, 0.8)}
    factors = {'L0_xattn_bk': 8.0,
     'L0_attn_w_q': 7.409,
     'L0_attn_b_q': 8.0,
     'L0_attn_b_out': 8.0,
     'L0_ffn_router_w': 8.0,
     'L0_ffn_up_proj': 8.0,
     'L0_ffn_gate_proj': 8.0,
     'L0_ffn_down_proj': 8.0,
     'L0_ffn_sh_gate': 6.17,
     'L0_ffn_sh_up': 6.114,
     'L0_ffn_sh_down': 6.124}
    for name, (base, spread) in spreads.items():
        noise = np.random.default_rng([zlib.crc32(name.encode()), seed]).standard_normal(out[name].shape)
        drawn = base * np.exp(spread * noise) if base else spread * noise
        out[name] = jnp.asarray(drawn.astype(out[name].dtype))
    for name, factor in factors.items():
        out[name] = (out[name] * factor).astype(out[name].dtype)
    return out
```

```python
from contextlib import ExitStack

import concourse.bass as bass
from concourse import mybir


def perceiver_layer(nc, t, out):
    fp32 = mybir.dt.float32
    i32 = mybir.dt.int32
    u32 = mybir.dt.uint32
    ALU = mybir.AluOpType
    ACT = mybir.ActivationFunctionType
    AX = mybir.AxisListType

    x_in, ctx_in = t["x"], t["ctx_1024"]
    NL, NB, D = x_in.shape
    KEYS = ctx_in.shape[1]
    P = 128
    DH = D // P
    TOK = NL * NB
    PAIRS = TOK // P
    KT = KEYS // P
    TAIL = KEYS - KT * P
    KB = -(-KEYS // 512)
    KW = [min(512, KEYS - 512 * kb) for kb in range(KB)]
    LN_EPS = 1e-5
    TG = 2 * (2 * (KB - 1) + 1)
    TGH = TG // 2
    RING = 3

    QD = t["L0_attn_w_q"].shape[0]
    HEADS = 16
    HD = QD // HEADS
    DV = D // HEADS
    NP = NL // 2 + 1
    Q_SCALE = float(DV) ** -0.5
    NG = TOK // P
    GB = P // NL
    HG = 6
    GROUPS = [(h, min(HG, HEADS - h)) for h in range(0, HEADS, HG)]

    NE, _, HID = t["L0_ffn_up_proj"].shape
    TOPK = 2
    NK = NG * TOPK
    SLOTS = (TOPK * TOK + NE * (P - 1)) // P
    NOWHERE = TOPK * TOK
    ROW = D + 1

    cross = ExitStack()
    with cross:
        def sb(name, shape, dt=fp32):
            return cross.enter_context(nc.sbuf_tensor(name, shape, dt))

        def sem(name):
            return cross.enter_context(nc.semaphore(name))

        bank = [cross.enter_context(nc.psum_tensor(f"bank{n}", [P, 512], fp32)) for n in range(8)]
        mid = nc.dram_tensor("mid", [TOK, 2 * D], fp32).ap()
        rows_dram = nc.dram_tensor("rows_by_expert", [SLOTS * P, ROW], fp32).ap()
        y_dram = nc.dram_tensor("expert_out", [TOPK * TOK, D], fp32).ap()

        ident = sb("ident", [P, P])
        ones = sb("ones", [P, P])
        ring_mem = sb("ring", [P, RING * 2 * (KT + 1) * D])
        ring = ring_mem[:, :].rearrange("p (r b k c) -> p r b k c", r=RING, b=2, c=D)
        ctxT_mem = sb("ctxT", [P, 2 * DH * KEYS])
        ctxT = ctxT_mem[:, :].rearrange("p (b d k) -> p b d k", b=2, d=DH)
        prob = sb("prob", [P, KEYS])
        probT_mem = sb("probT", [P, (KT + 1) * P])
        probT = probT_mem[:, :].rearrange("p (k q) -> p k q", q=P)
        x_all = sb("x_all", [P, PAIRS, D])
        xn_mem = sb("xn_all", [P, PAIRS * ROW])
        xn_all = xn_mem[:, 0:PAIRS * D].rearrange("p (i c) -> p i c", c=D)
        qT_mem = sb("qT_all", [P, DH * TOK])
        qT_all = qT_mem[:, :].rearrange("p (d s) -> p d s", d=DH)
        q_now = sb("q_now", [P, DH, P])

        def views(mem, *shapes):
            at, got = 0, []
            for shape in shapes:
                size = 1
                for n in shape[1:]:
                    size *= n
                piece = mem[0:shape[0], at:at + size]
                if len(shape) > 2:
                    names = "abcd"[:len(shape) - 1]
                    piece = piece.rearrange(f"p ({' '.join(names)}) -> p {' '.join(names)}",
                                            **dict(zip(names[1:], shape[2:])))
                got.append(piece)
                at += size
            return got

        third = ring_mem[:, 2 * 2 * (KT + 1) * D:]
        wq, wk, w_q, w_out, sh_gate, sh_up, sh_down, router_w, w_kv4, bq_rep, xnT = views(
            third, [P, DH, D], [P, DH, D], [P, D], [P, DH, D], [P, DH, D], [P, DH, D], [P, DH, D],
            [NE, D], [NP, P], [NL, QD], [P, DH, 512])
        wv = sb("wv", [P, DH, D])
        wqT = sb("wqT", [P, DH, D])
        wkT = sb("wkT", [P, DH, D])
        wqk = sb("wqk", [P, DH, D])
        bq_col = sb("bq_col", [P, DH])
        bk_col = sb("bk_col", [P, DH])
        bk_rep = sb("bk_rep", [P, DH, P])
        bqk_col = sb("bqk_col", [P, DH])
        bk_row = sb("bk_row", [P, D + 1])
        gamma_b = sb("gamma_b", [P, D])
        beta_b = sb("beta_b", [P, D])
        bv_b = sb("bv_b", [P, D])
        x_stats = sb("x_stats", [P, PAIRS, 6])
        x_mv = sb("x_mv", [P, PAIRS, 2])
        x_rstd = sb("x_rstd", [P, PAIRS])
        x_var = sb("x_var", [P, PAIRS])
        shift = sb("shift", [P, PAIRS])
        dotted = sb("dotted", [P, D])
        eps = sb("eps", [P, 1])
        seen = sb("seen", [P, 1])
        m_half = sb("m_half", [P, PAIRS])
        blockmax = sb("blockmax", [P, KB])
        rowmax = sb("rowmax", [P, 1])
        topped = sb("topped", [P, 1])
        negmax = sb("negmax", [P, 1])
        sums = sb("sums", [P, KB])
        rowsum = sb("rowsum", [P, 1])
        rinv = sb("rinv", [P, 1])
        Un = sb("Un", [P, D])
        UT = sb("UT", [P, DH, P])
        res = sb("res", [P, D])
        scaled = sb("scaled", [P, D])
        stats = sb("stats", [P, 2, 6])
        mv = sb("mv", [P, 2, 2])
        var = sb("var", [P, 2])
        rstd = sb("rstd", [P, 2])
        stage = sb("stage", [P, 2, D])

        w_qT = sb("w_qT", [P, DH, QD])
        w_kT = sb("w_kT", [P, DH, QD])
        w_outT = sb("w_outT", [P, DH, D])
        bout_b = sb("bout_b", [P, D])
        bq_scaled = sb("bq_scaled", [P, 1])
        bq_perm = sb("bq_perm", [NL, QD])
        w_pick = sb("w_pick", [P, GB, NP])
        w_rep = sb("w_rep", [P, GB, HG, NP])
        k_bias = sb("k_bias", [P, NP])
        k_mask = sb("k_mask", [P, HEADS])
        v_mask = sb("v_mask", [P, HEADS])
        (kv_in, x_nT, vT, q_T, k_T, k_blk, v_blk, attn, attnT, o_sb, oT) = views(
            ctxT_mem, [P, 3, D], [P, DH, P], [P, DH, GB * NP], [P, P], [P, GB, NP], [P, GB, HEADS, NP],
            [P, GB, HEADS, DV], [P, HEADS, NP], [P, len(GROUPS), P], [P, D], [P, DH, P])
        head_max = sb("head_max", [P, HEADS])
        head_sum = sb("head_sum", [P, HEADS])
        head_inv = sb("head_inv", [P, HEADS])
        x1_all = qT_mem[:, :].rearrange("p (g c) -> p g c", c=D)
        x2_all = x_all
        router_T = sb("router_T", [P, DH, NE])
        rbias_b = sb("rbias_b", [P, NE])
        sh_gateT = sb("sh_gateT", [P, DH, D])
        sh_upT = sb("sh_upT", [P, DH, D])
        sh_downT = sb("sh_downT", [P, DH, D])
        below = sb("below", [P, P])
        lane = sb("lane", [P, NE])
        tile_no = sb("tile_no", [1, SLOTS + 1])
        blank = sb("blank", [P, ROW])
        w_gu, w_down, n2_first, passed = views(ring_mem, [P, NE, DH, 2 * HID], [P, NE, D], [P, NG, ROW], [1, SLOTS + 1, NE])
        n2_second = xn_mem[:, :].rearrange("p (g c) -> p g c", c=ROW)
        n2 = [n2_first, n2_second]
        n2T_all = qT_all
        y_all = [qT_mem[:, :].rearrange("p (g c) -> p g c", c=D), xn_all]
        logits, count_a = views(prob, [P, NG, NE], [P, 2 * NK, NE])
        count_b, chosen = views(probT_mem, [P, 2 * NK, NE], [P, NK, NE])
        (sh_silu, sh_hid, place, best, best_at, row_in, rowT, silu_g, hid, hidT, y_sb) = views(
            ctxT_mem, [P, DH, 512], [P, 2, DH, 512], [P, NK, NE], [P, NG, 8], [P, NG, 8], [P, 2, ROW], [P, 2, DH, P],
            [P, 2, HID], [P, 2, HID], [P, 2, P], [P, 2, D])
        best_at = best_at.bitcast(u32)
        best_f = sb("best_f", [P, NG, TOPK])
        gap_w = sb("gap_w", [P, NG])
        gap_e = sb("gap_e", [P, NG])
        gap_s = sb("gap_s", [P, NG])
        mix = sb("mix", [P, TOPK, NG])
        tiles_f = sb("tiles_f", [P, NE])
        tiles_i = sb("tiles_i", [P, NE], i32)
        tiles_h = sb("tiles_h", [P, NE], i32)
        tiles_n = sb("tiles_n", [P, NE])
        cum_a = sb("cum_a", [P, 2 * NE])
        cum_b = sb("cum_b", [P, 2 * NE])
        first_row = sb("first_row", [P, NE])
        place_f = sb("place_f", [P, NK])
        place_i = sb("place_i", [P, NK], u32)
        expert_f = sb("expert_f", [1, SLOTS + 1])
        expert_m = sb("expert_m", [1, SLOTS + 1])
        expert_i = sb("expert_i", [1, SLOTS + 1], i32)
        dest = sb("dest", [P, 2], u32)

        S = bank[0:KB]
        T = bank[4:6]
        U = bank[6]
        M = bank[7]

        x_loaded = [sem(f"x_loaded{n}") for n in range(4)]
        qk_loaded = sem("qk_loaded")
        rest_loaded = sem("rest_loaded")
        ctx_loaded = [sem(f"ctx_loaded{r}") for r in range(RING)]
        stored = sem("stored")
        const_step = sem("const_step")
        wT_done = sem("wT_done")
        wT_copied = sem("wT_copied")
        bk_rep_ready = sem("bk_rep_ready")
        wqk_done = sem("wqk_done")
        wqk_copied = sem("wqk_copied")
        bk_row_copied = sem("bk_row_copied")
        x_stat_ready = sem("x_stat_ready")
        x_mv_ready = sem("x_mv_ready")
        x_var_ready = sem("x_var_ready")
        x_rstd_ready = sem("x_rstd_ready")
        xn_ready = sem("xn_ready")
        dot_ready = sem("dot_ready")
        shift_ready = sem("shift_ready")
        xnT_done = sem("xnT_done")
        xnT_copied = sem("xnT_copied")
        qT_done = sem("qT_done")
        qT_copied = sem("qT_copied")
        xnb_ready = sem("xnb_ready")
        q_now_ready = sem("q_now_ready")
        t_done = sem("t_done")
        t_act = sem("t_act")
        t_dve = sem("t_dve")
        scores_done = sem("scores_done")
        blockmax_ready = sem("blockmax_ready")
        rowmax_ready = sem("rowmax_ready")
        topped_ready = sem("topped_ready")
        negmax_ready = sem("negmax_ready")
        exp_done = sem("exp_done")
        probT_done = sem("probT_done")
        probT_copied = sem("probT_copied")
        pv_done = sem("pv_done")
        rowsum_ready = sem("rowsum_ready")
        rinv_ready = sem("rinv_ready")
        Un_ready = sem("Un_ready")
        UT_done = sem("UT_done")
        UT_copied = sem("UT_copied")
        res_done = sem("res_done")
        res_ready = sem("res_ready")
        stat_ready = sem("stat_ready")
        mv_ready = sem("mv_ready")
        var_ready = sem("var_ready")
        rstd_ready = sem("rstd_ready")
        scaled_ready = sem("scaled_ready")
        x1_ready = sem("x1_ready")
        n1_ready = sem("n1_ready")
        prep_loaded = sem("prep_loaded")
        bconst_loaded = sem("bconst_loaded")
        masks_ready = sem("masks_ready")
        prep_done = sem("prep_done")
        prep_copied = sem("prep_copied")
        small_copied = sem("small_copied")
        kbias_done = sem("kbias_done")
        kbias_copied = sem("kbias_copied")
        perm_ready = sem("perm_ready")
        wp_ready = sem("wp_ready")
        zeroed = sem("zeroed")
        mid_loaded = sem("mid_loaded")
        x1b_ready = sem("x1b_ready")
        xnT2_done = sem("xnT2_done")
        xnT2_copied = sem("xnT2_copied")
        vT_done = sem("vT_done")
        vT_copied = sem("vT_copied")
        vrep_done = sem("vrep_done")
        v_blk_ready = sem("v_blk_ready")
        q2_done = sem("q2_done")
        q2_copied = sem("q2_copied")
        k2_done = sem("k2_done")
        k2_copied = sem("k2_copied")
        k_blk_ready = sem("k_blk_ready")
        s2_done = sem("s2_done")
        head_max_ready = sem("head_max_ready")
        shifted_ready = sem("shifted_ready")
        exp2_done = sem("exp2_done")
        head_sum_ready = sem("head_sum_ready")
        head_inv_ready = sem("head_inv_ready")
        attn_ready = sem("attn_ready")
        attnT_done = sem("attnT_done")
        attnT_copied = sem("attnT_copied")
        pv2_done = sem("pv2_done")
        o_copied = sem("o_copied")
        oT_done = sem("oT_done")
        oT_copied = sem("oT_copied")
        proj_done = sem("proj_done")
        x2_ready = sem("x2_ready")
        stat2_ready = sem("stat2_ready")
        mv2_ready = sem("mv2_ready")
        var2_ready = sem("var2_ready")
        rstd2_ready = sem("rstd2_ready")
        n2_ready = sem("n2_ready")
        n2b_ready = sem("n2b_ready")
        experts_loaded = sem("experts_loaded")
        blank_ready = sem("blank_ready")
        blanked = sem("blanked")
        n2T_done = sem("n2T_done")
        n2T_act = sem("n2T_act")
        n2T_dve = sem("n2T_dve")
        logits_done = sem("logits_done")
        logits_ready = sem("logits_ready")
        best_ready = sem("best_ready")
        best_at_ready = sem("best_at_ready")
        best_f_ready = sem("best_f_ready")
        chosen_ready = sem("chosen_ready")
        before_done = sem("before_done")
        gap_ready = sem("gap_ready")
        gap_exp = sem("gap_exp")
        gap_sum_ready = sem("gap_sum_ready")
        mix_ready = sem("mix_ready")
        count_step = sem("count_step")
        tiles_step = sem("tiles_step")
        first_ready = sem("first_ready")
        place_step = sem("place_step")
        place_ready = sem("place_ready")
        expert_step = sem("expert_step")
        dest_ready = sem("dest_ready")
        scattered = sem("scattered")
        shared_up_done = sem("shared_up_done")
        shared_silu = sem("shared_silu")
        shared_hid_ready = sem("shared_hid_ready")
        shared_done = sem("shared_done")
        shared_added = sem("shared_added")
        rowT_done = sem("rowT_done")
        rowT_copied = sem("rowT_copied")
        dest_copied = sem("dest_copied")
        gu_done = sem("gu_done")
        silu_done = sem("silu_done")
        hid_ready = sem("hid_ready")
        hidT_done = sem("hidT_done")
        hidT_copied = sem("hidT_copied")
        down_done = sem("down_done")
        y_ready = sem("y_ready")
        mixed_ready = sem("mixed_ready")
        out_ready = sem("out_ready")
        written = sem("written")
        kv_loaded = [sem(f"kv_loaded{r}") for r in range(3)]
        row_loaded = [sem(f"row_loaded{r}") for r in range(2)]
        y_sent = [sem(f"y_sent{r}") for r in range(2)]
        y_loaded = [sem(f"y_loaded{n}") for n in range(4)]

        block = cross.enter_context(nc.Block())

        def tgroups():
            for b in range(2):
                for kb in range(KB - 1):
                    for dh in range(DH):
                        yield b, kb, dh
                yield b, KB - 1, None

        def t_copy(n):
            b, kb, dh = list(tgroups())[n]
            if dh is None:
                return (ctxT[:, b, :, KT * P:KEYS],
                        T[n % 2][:, 0:DH * P].rearrange("p (d k) -> p d k", d=DH)[:, :, 0:TAIL])
            return ctxT[:, b, dh, kb * 512:(kb + 1) * 512], T[n % 2][:, :]

        @block.sync
        def _(sp):
            rows = x_in.rearrange("l b c -> (l b) c").rearrange("(i p) c -> p i c", p=P)
            for n in range(4):
                sp.dma_start(x_all[:, 4 * n:4 * n + 4, :], rows[:, 4 * n:4 * n + 4, :]).then_inc(x_loaded[n], 16)

            def load(i, r):
                pair = ctx_in[bass.ds(2 * i, 2)]
                sp.dma_start(ring[:, r, :, 0:KT, :].rearrange("p b k c -> p b (k c)"),
                             pair[:, 0:KT * P, :].rearrange("b (p k) c -> p b (k c)", k=KT)).then_inc(ctx_loaded[r], 16)
                sp.dma_start(ring[0:TAIL, r, :, KT, :],
                             pair[:, KT * P:KEYS, :].rearrange("b p c -> p b c")).then_inc(ctx_loaded[r], 16)

            def store(k):
                sp.wait_ge(n1_ready, k + 1)
                cols = mid.rearrange("(g q l) c -> l q g c", g=16, q=4)
                for b in range(2):
                    sp.dma_start(cols[bass.ds(2 * k + b, 1)].squeeze(0),
                                 stage[64 * b:64 * b + 64, :, :].rearrange("p a c -> p (a c)")).then_inc(stored, 16)

            sp.sem_inc(stored, 32)
            for i in range(RING):
                if i == 2:
                    sp.wait_ge(prep_done, 5)
                    sp.wait_ge(perm_ready, 1)
                    sp.wait_ge(wT_done, 2)
                    sp.wait_ge(qT_done, 8)
                load(i, i)
            sp.wait_ge(pv_done, 1)
            load(RING, 0)
            sp.wait_ge(blank_ready, 2)
            sp.dma_start(rows_dram.rearrange("(s p) c -> p s c", p=P),
                         blank[:, :].unsqueeze(1).broadcast_to([P, SLOTS, ROW])).then_inc(blanked, 16)
            store(0)
            with sp.Fori(0, (PAIRS - RING - 1) // RING) as it:
                for u in range(RING):
                    i = it * RING + (RING + 1 + u)
                    sp.wait_ge(pv_done, i - (RING - 1))
                    load(i, (RING + 1 + u) % RING)
                    store(i - RING)
            for k in range(PAIRS - RING, PAIRS):
                store(k)
            sp.wait_ge(stored, 32 * (PAIRS + 1))

            def load_group(g, r):
                sp.dma_start(kv_in[:, r, :], mid[bass.ds(g * P, P), D:2 * D]).then_inc(kv_loaded[r], 16)

            for g in range(3):
                load_group(g, g)
            sp.dma_start(x1_all, mid.rearrange("(g p) c -> p g c", p=P)[:, :, 0:D]).then_inc(mid_loaded, 16)
            with sp.Fori(0, NG // 3 - 1) as it:
                for u in range(3):
                    g = it * 3 + (3 + u)
                    sp.wait_ge(vrep_done, g - 2)
                    load_group(g, u)
            sp.wait_ge(vrep_done, NG - 3)
            load_group(NG - 1, (NG - 1) % 3)

            def load_rows(s, r):
                sp.dma_start(row_in[:, r, :], rows_dram[bass.ds(s * P, P), :]).then_inc(row_loaded[r], 16)

            sp.wait_ge(scattered, 16 * NK)
            load_rows(0, 0)
            load_rows(1, 1)
            with sp.Fori(0, (SLOTS - 3) // 2) as it:
                for u in range(2):
                    s = it * 2 + (2 + u)
                    sp.wait_ge(rowT_done, s - 1)
                    sp.wait_ge(dest_copied, s - 1)
                    load_rows(s, u)
            sp.wait_ge(rowT_done, SLOTS - 2)
            sp.wait_ge(dest_copied, SLOTS - 2)
            load_rows(SLOTS - 1, (SLOTS - 1) % 2)
            for r in range(2):
                sp.wait_ge(y_sent[r], 16 * ((SLOTS + 1 - r) // 2))
            for n in range(4):
                for k in range(TOPK):
                    sp.dma_start(y_all[k][:, 4 * n:4 * n + 4, :],
                                 y_dram[k * TOK:(k + 1) * TOK, :].rearrange("(g p) c -> p g c", p=P)[:, 4 * n:4 * n + 4, :])\
                        .then_inc(y_loaded[n], 16)
            for n in range(4):
                sp.wait_ge(out_ready, 4 * n + 4)
                for q in range(GB):
                    sp.dma_start(out.rearrange("l (q g) c -> q l g c", q=GB)[q][:, 4 * n:4 * n + 4, :],
                                 x2_all[NL * q:NL * q + NL, 4 * n:4 * n + 4, :]).then_inc(written, 16)
            sp.wait_ge(written, 16 * 4 * GB)

        @block.gpsimd
        def _(pool):
            pool.memset(ident[:, :], 0.0).then_inc(const_step, 1)
            pool.memset(m_half[:, :], -0.5).then_inc(const_step, 1)
            pool.memset(ones[:, :], 1.0).then_inc(const_step, 1)
            pool.memset(eps[:, :], LN_EPS).then_inc(const_step, 1)
            pool.wait_ge(const_step, 4)
            pool.affine_select(out=ident[:, :], in_=ident[:, :], compare_op=ALU.not_equal, fill=1.0, base=0,
                               pattern=[[-1, P]], channel_multiplier=1).then_inc(const_step, 1)
            pool.memset(blank[:, 0:D], 0.0).then_inc(blank_ready, 1)
            pool.iota(blank[:, D:ROW].bitcast(i32), pattern=[[0, 1]], base=NOWHERE, channel_multiplier=0)\
                .then_inc(blank_ready, 1)
            pool.memset(w_pick[:, :, :], 0.0).then_inc(zeroed, 1)
            pool.memset(w_rep[:, :, :, :], 0.0).then_inc(zeroed, 1)
            pool.memset(k_mask[:, :], 1.0).then_inc(zeroed, 1)
            pool.memset(v_mask[:, :], 1.0).then_inc(zeroed, 1)
            pool.memset(below[:, :], 1.0).then_inc(zeroed, 1)
            pool.wait_ge(zeroed, 5)
            pool.affine_select(out=k_mask[:, :], in_=k_mask[:, :], compare_op=ALU.is_ge, fill=0.0, base=0,
                               pattern=[[-HD, HEADS]], channel_multiplier=1).then_inc(masks_ready, 1)
            pool.affine_select(out=below[:, :], in_=below[:, :], compare_op=ALU.is_ge, fill=0.0, base=-1,
                               pattern=[[1, P]], channel_multiplier=-1).then_inc(masks_ready, 1)
            for h, n in GROUPS:
                pool.affine_select(out=v_mask[:, h:h + n], in_=v_mask[:, h:h + n], compare_op=ALU.is_ge, fill=0.0, base=0,
                                   pattern=[[-NP, n]], channel_multiplier=1).then_inc(masks_ready, 1)
            pool.wait_ge(masks_ready, 5)
            pool.affine_select(out=k_mask[:, :], in_=k_mask[:, :], compare_op=ALU.is_ge, fill=0.0, base=HD - 1,
                               pattern=[[HD, HEADS]], channel_multiplier=-1).then_inc(masks_ready, 1)
            for h, n in GROUPS:
                pool.affine_select(out=v_mask[:, h:h + n], in_=v_mask[:, h:h + n], compare_op=ALU.is_ge, fill=0.0,
                                   base=NP - 1, pattern=[[NP, n]], channel_multiplier=-1).then_inc(masks_ready, 1)
            pool.iota(lane[:, :], pattern=[[1, NE]], base=0, channel_multiplier=0,
                      allow_small_or_imprecise_dtypes=True).then_inc(masks_ready, 1)
            pool.iota(tile_no[:, :], pattern=[[1, SLOTS + 1]], base=0, channel_multiplier=0,
                      allow_small_or_imprecise_dtypes=True).then_inc(masks_ready, 1)
            pool.wait_ge(x_mv_ready, PAIRS)
            pool.tensor_scalar(x_var[:, :], x_mv[:, :, 1], LN_EPS, None, ALU.add).then_inc(x_var_ready, 1)
            pool.wait_ge(x_var_ready, 1)
            pool.tensor_tensor(x_rstd[:, :], x_var[:, :], m_half[:, :], ALU.pow).then_inc(x_rstd_ready, 1)

            def take_q(i):
                pool.wait_ge(qT_copied, 8)
                pool.tensor_copy(q_now[:, :, :], qT_all[:, :, bass.ds(i * P, P)]).then_inc(q_now_ready, 1)

            def deviations(k):
                for n in range(2):
                    pool.wait_ge(mv_ready, 2 * k + (n + 1))
                    pool.tensor_tensor(var[:, n:n + 1], mv[:, n, 1:2], eps[:, :], ALU.add).then_inc(var_ready, 1)
                    pool.wait_ge(var_ready, 2 * k + (n + 1))
                    pool.tensor_tensor(rstd[:, n:n + 1], var[:, n:n + 1], m_half[:, 0:1], ALU.pow).then_inc(rstd_ready, 1)

            take_q(0)
            pool.wait_ge(rest_loaded, 64)
            pool.wait_ge(xnT_done, 4)
            pool.wait_ge(shift_ready, PAIRS)
            pool.tensor_tensor(xn_all[:, :, :], xn_all[:, :, :],
                               bv_b[:, :].unsqueeze(1).broadcast_to([P, PAIRS, D]), ALU.add).then_inc(xnb_ready, 1)
            pool.tensor_tensor(x_all[:, :, :], x_all[:, :, :],
                               beta_b[:, :].unsqueeze(1).broadcast_to([P, PAIRS, D]), ALU.add).then_inc(xnb_ready, 1)
            pool.wait_ge(scores_done, KB)
            take_q(1)
            with pool.Fori(0, PAIRS - 2) as k:
                pool.wait_ge(scores_done, k * KB + 2 * KB)
                take_q(k + 2)
                deviations(k)
            for k in range(PAIRS - 2, PAIRS):
                deviations(k)

            def keys_by_head(g):
                pool.wait_ge(k2_copied, g + 1)
                pool.tensor_tensor(k_blk, k_T.unsqueeze(2).broadcast_to([P, GB, HEADS, NP]),
                                   k_mask[:, :].unsqueeze(1).unsqueeze(3).broadcast_to([P, GB, HEADS, NP]),
                                   ALU.mult).then_inc(k_blk_ready, 1)

            def deviation2(k):
                pool.wait_ge(mv2_ready, k + 1)
                pool.tensor_tensor(var[:, 0:1], mv[:, 0, 1:2], eps[:, :], ALU.add).then_inc(var2_ready, 1)
                pool.wait_ge(var2_ready, k + 1)
                pool.tensor_tensor(rstd[:, 0:1], var[:, 0:1], m_half[:, 0:1], ALU.pow).then_inc(rstd2_ready, 1)

            def copy_rows(k):
                pool.wait_ge(n2_ready, k + 1)
                pool.tensor_copy(n2_second[:, bass.ds(k, 1), 0:D].squeeze(1),
                                 n2_first[:, bass.ds(k, 1), 0:D].squeeze(1)).then_inc(n2b_ready, 1)

            pool.wait_ge(mid_loaded, 16)
            pool.tensor_tensor(x1_all, x1_all, bout_b[:, :].unsqueeze(1).broadcast_to([P, NG, D]), ALU.add)\
                .then_inc(x1b_ready, 1)
            for k in range(TOPK):
                pool.iota(n2[k][:, :, D].bitcast(i32), pattern=[[P, NG]], base=k * TOK, channel_multiplier=1)\
                    .then_inc(dest_ready, 1)
            pool.memset(count_a[:, 0:NK, :], 0.0).then_inc(dest_ready, 1)
            pool.memset(count_b[:, 0:NK, :], 0.0).then_inc(dest_ready, 1)
            pool.memset(cum_a[:, 0:NE], 0.0).then_inc(dest_ready, 1)
            pool.memset(cum_b[:, 0:NE], 0.0).then_inc(dest_ready, 1)
            keys_by_head(0)
            with pool.Fori(0, NG - 1) as k:
                keys_by_head(k + 1)
                deviation2(k)
                copy_rows(k)
            deviation2(NG - 1)
            copy_rows(NG - 1)

            pool.wait_ge(blanked, 16)
            pool.wait_ge(place_ready, 1)
            pool.wait_ge(n2b_ready, NG)
            pool.wait_ge(dest_ready, TOPK)
            for g in range(NG):
                for k in range(TOPK):
                    c = g * TOPK + k
                    pool.indirect_dma_start(rows_dram, bass.IndirectOffsetOnAxis(ap=place_i[:, c:c + 1], axis=0),
                                            n2[k][:, g, :], None).then_inc(scattered, 16)

            def send(s, r):
                pool.wait_ge(y_ready, s + 1)
                pool.indirect_dma_start(y_dram, bass.IndirectOffsetOnAxis(ap=dest[:, r:r + 1], axis=0), y_sb[:, r, :], None,
                                        bounds_check=TOPK * TOK - 1, oob_is_err=False).then_inc(y_sent[r], 16)

            for n in range(SLOTS):
                send(n, n % 2)

        @block.scalar
        def _(act):
            act.dma_start(wq[:, :, :], t["L0_xattn_Wq"].rearrange("(k p) f -> p k f", p=P)).then_inc(qk_loaded, 16)
            act.dma_start(wk[:, :, :], t["L0_xattn_Wk"].rearrange("(k p) f -> p k f", p=P)).then_inc(qk_loaded, 16)
            act.dma_start(bq_col[:, :], t["L0_xattn_bq"].rearrange("(k p) -> p k", p=P),
                          allow_slow_non_contiguous=True).then_inc(qk_loaded, 16)
            act.dma_start(bk_col[:, :], t["L0_xattn_bk"].rearrange("(k p) -> p k", p=P),
                          allow_slow_non_contiguous=True).then_inc(qk_loaded, 16)
            act.dma_start(wv[:, :, :], t["L0_xattn_Wv"].rearrange("(k p) f -> p k f", p=P)).then_inc(rest_loaded, 16)
            for to, of in ((bv_b, "L0_xattn_bv"), (gamma_b, "L0_xattn_gamma"), (beta_b, "L0_xattn_beta")):
                act.dma_start(to[:, :], t[of].partition_broadcast(P)).then_inc(rest_loaded, 16)
            act.dma_start(w_q, t["L0_attn_w_q"]).then_inc(prep_loaded, 16)
            for q in range(GB):
                act.dma_start(w_kv4[:, NL * q:NL * q + NL], t["L0_attn_w_kv"][0:NP, 0:NL]).then_inc(prep_loaded, 16)
            act.dma_start(router_w, t["L0_ffn_router_w"]).then_inc(prep_loaded, 16)
            act.dma_start(bq_rep, t["L0_attn_b_q"].partition_broadcast(NL)).then_inc(prep_loaded, 16)
            for to, of in ((w_out, "L0_attn_w_out"), (sh_gate, "L0_ffn_sh_gate"), (sh_up, "L0_ffn_sh_up"),
                           (sh_down, "L0_ffn_sh_down")):
                act.dma_start(to, t[of].rearrange("(k p) c -> p k c", p=P)).then_inc(prep_loaded, 16)
            act.dma_start(bq_scaled[:, :], t["L0_attn_b_q"].rearrange("(p a) -> p a", a=1)).then_inc(bconst_loaded, 16)
            act.dma_start(bout_b[:, :], t["L0_attn_b_out"].partition_broadcast(P)).then_inc(bconst_loaded, 16)
            act.dma_start(rbias_b[:, :], t["L0_ffn_router_bias"].partition_broadcast(P)).then_inc(bconst_loaded, 16)
            act.wait_ge(wT_done, 1)
            act.copy(wqT[:, :, :].rearrange("p a b -> p (a b)"), bank[0][:, :]).then_inc(wT_copied, 1)
            act.wait_ge(wT_done, 2)
            act.copy(wkT[:, :, :].rearrange("p a b -> p (a b)"), bank[1][:, :]).then_inc(wT_copied, 1)
            act.wait_ge(wqk_done, 1)
            act.copy(wqk[:, :, :].rearrange("p a b -> p (a b)"), bank[2][:, :]).then_inc(wqk_copied, 1)
            act.wait_ge(wqk_done, 2)
            act.copy(bqk_col[:, :], bank[3][:, 300:300 + DH]).then_inc(wqk_copied, 1)
            for n, to in enumerate((w_outT, sh_gateT, sh_upT, sh_downT)):
                act.wait_ge(prep_done, n + 1)
                act.copy(to[:, :, :].rearrange("p a b -> p (a b)"), bank[4 + n][:, :]).then_inc(prep_copied, 1)
            act.wait_ge(wqk_copied, 2)
            for n in range(4):
                for dc in range(DH):
                    act.wait_ge(qT_done, 2 * n + dc + 1)
                    act.activation(qT_all[:, dc, 512 * n:512 * n + 512], bank[6 + dc][:, :], ACT.Identity,
                                   bias=bqk_col[:, dc:dc + 1]).then_inc(qT_copied, 1)

            def t_evac(i, n):
                act.wait_ge(t_done, i * TG + (n + 1))
                act.copy(*t_copy(n)).then_inc(t_act, 1)

            def exps(i, kb):
                if kb == 0:
                    act.wait_ge(negmax_ready, i + 1)
                act.activation(prob[:, 512 * kb:512 * kb + KW[kb]], S[kb][:, 0:KW[kb]], ACT.Exp, bias=negmax[:, 0:1],
                               accum_out=sums[:, kb:kb + 1]).then_inc(exp_done, 1)

            def probT_evac(i):
                for kb in range(KB):
                    act.wait_ge(probT_done, i * KB + (kb + 1))
                    rows, tiles = (P, 4) if kb < KB - 1 else (TAIL, 1)
                    act.copy(probT[0:rows, 4 * kb:4 * kb + tiles, :].rearrange("p a b -> p (a b)"),
                             S[kb][0:rows, 0:tiles * P]).then_inc(probT_copied, 1)

            def UT_evac(i):
                act.wait_ge(UT_done, i + 1)
                act.copy(UT[:, :, :].rearrange("p a b -> p (a b)"), M[:, 0:D]).then_inc(UT_copied, 1)

            for n in range(0, TG, 2):
                t_evac(0, n)
            with act.Fori(1, PAIRS) as i:
                for n in range(0, TG, 2):
                    t_evac(i, n)
                    if 1 <= n // 2 <= KB:
                        exps(i - 1, n // 2 - 1)
                probT_evac(i - 1)
                UT_evac(i - 1)
            for kb in range(KB):
                exps(PAIRS - 1, kb)
            probT_evac(PAIRS - 1)
            act.wait_ge(pv_done, PAIRS)
            for k in range(DH):
                for a, of in enumerate(("gate", "up")):
                    act.dma_start(w_gu[:, :, k, a * HID:(a + 1) * HID],
                                  t[f"L0_ffn_{of}_proj"][:, k * P:(k + 1) * P, :].rearrange("e p h -> p e h"))\
                        .then_inc(experts_loaded, 16)
            act.dma_start(w_down, t["L0_ffn_down_proj"].rearrange("e p c -> p e c")).then_inc(experts_loaded, 16)
            UT_evac(PAIRS - 1)

            def group_in(g):
                act.wait_ge(xnT2_done, g + 1)
                act.copy(x_nT.rearrange("p a b -> p (a b)"), bank[0][:, 0:D]).then_inc(xnT2_copied, 1)

            def exp2(g):
                act.wait_ge(shifted_ready, g + 1)
                act.activation(attn, attn, ACT.Exp).then_inc(exp2_done, 1)

            def v_and_q(g):
                act.wait_ge(vT_done, g + 1)
                act.copy(vT.rearrange("p a b -> p (a b)"), bank[1][:, 0:DH * GB * NP]).then_inc(vT_copied, 1)
                act.wait_ge(q2_done, g + 1)
                act.activation(q_T, bank[4][:, 0:P], ACT.Identity, bias=bq_scaled[:, 0:1], scale=Q_SCALE).then_inc(q2_copied, 1)

            def weighted(g):
                act.wait_ge(attnT_done, g + 1)
                act.copy(attnT[0:HG * NP].rearrange("p a b -> p (a b)"), bank[6][0:HG * NP, 0:len(GROUPS) * P])\
                    .then_inc(attnT_copied, 1)
                act.wait_ge(pv2_done, g + 1)
                act.copy(o_sb.rearrange("p (v h) -> p h v", h=HEADS),
                         bank[7][:, 0:D].rearrange("p (h v) -> p h v", v=DV)).then_inc(o_copied, 1)
                act.wait_ge(oT_done, g + 1)
                act.copy(oT.rearrange("p a b -> p (a b)"), bank[0][:, D:2 * D]).then_inc(oT_copied, 1)

            act.wait_ge(perm_ready, 2)
            group_in(0)
            v_and_q(0)
            with act.Fori(1, NG) as g:
                group_in(g)
                exp2(g - 1)
                v_and_q(g)
                weighted(g - 1)
            exp2(NG - 1)
            weighted(NG - 1)

            for n in range(0, 8, 2):
                act.wait_ge(n2T_done, n + 1)
                act.copy(n2T_all[:, 0, 512 * (n // 2):512 * (n // 2) + 512], bank[n][:, :]).then_inc(n2T_act, 1)
            act.wait_ge(gap_ready, 1)
            act.activation(gap_e[:, :], gap_w[:, :], ACT.Exp).then_inc(gap_exp, 1)
            for q in range(4):
                for hc in range(DH):
                    act.wait_ge(shared_up_done, 2 * DH * q + hc + 1)
                    if q >= 1:
                        act.wait_ge(shared_hid_ready, DH * (q - 1) + hc + 1)
                    act.activation(sh_silu[:, hc, :], bank[1 + hc][:, :], ACT.Silu).then_inc(shared_silu, 1)

            def rows_in(s, r):
                act.wait_ge(rowT_done, s + 1)
                act.copy(rowT[:, r].rearrange("p a b -> p (a b)"), bank[r][:, 0:D]).then_inc(rowT_copied, 1)

            def hidden_T(s, r):
                act.wait_ge(hidT_done, s + 1)
                act.copy(hidT[:, r, :], bank[4 + r][:, 0:P]).then_inc(hidT_copied, 1)

            def gate(s, r):
                act.wait_ge(gu_done, s + 1)
                act.activation(silu_g[:, r, :], bank[2 + r][:, 0:HID], ACT.Silu).then_inc(silu_done, 1)

            rows_in(0, 0)
            gate(0, 0)
            with act.Fori(0, (SLOTS - 1) // 2) as it:
                for u in range(2):
                    s = it * 2 + (u + 1)
                    rows_in(s, (u + 1) % 2)
                    hidden_T(s - 1, u)
                    gate(s, (u + 1) % 2)
            hidden_T(SLOTS - 1, (SLOTS - 1) % 2)

        @block.tensor
        def _(pe):
            pe.wait_ge(const_step, 5)
            pe.wait_ge(qk_loaded, 64)
            for of, to in ((wq, 0), (wk, 1)):
                for kd in range(DH):
                    for fc in range(DH):
                        last = pe.transpose(bank[to][:, fc * D + kd * P:fc * D + kd * P + P],
                                            of[:, kd, fc * P:fc * P + P], ident[:, :])
                last.then_inc(wT_done, 1)
            pe.wait_ge(wT_copied, 2)
            for kd in range(DH):
                for fc in range(DH):
                    last = pe.matmul(bank[2][:, kd * D:kd * D + D], wqT[:, fc, kd * P:kd * P + P], wkT[:, fc, :],
                                     start=fc == 0, stop=fc == DH - 1)
            last.then_inc(wqk_done, 1)
            for dc in range(DH):
                for fc in range(DH):
                    pe.matmul(bank[3][:, 300 + dc:301 + dc], wkT[:, fc, dc * P:dc * P + P], bq_col[:, fc:fc + 1],
                              start=fc == 0, stop=fc == DH - 1)
            pe.wait_ge(bk_rep_ready, 1)
            for fc in range(DH):
                pe.matmul(bank[3][:, 0:D], bk_rep[:, fc, :], wqT[:, fc, :], start=fc == 0, stop=fc == DH - 1)
            for fc in range(DH):
                last = pe.matmul(bank[3][:, D:D + 1], bk_rep[:, fc, :], bq_col[:, fc:fc + 1],
                                 start=fc == 0, stop=fc == DH - 1)
            last.then_inc(wqk_done, 1)
            pe.wait_ge(prep_loaded, 16 * (GB + 7))
            for n, of in enumerate((w_out, sh_gate, sh_up, sh_down)):
                for kd in range(DH):
                    for fc in range(DH):
                        last = pe.transpose(bank[4 + n][:, fc * D + kd * P:fc * D + kd * P + P],
                                            of[:, kd, fc * P:fc * P + P], ident[:, :])
                last.then_inc(prep_done, 1)
            for k in range(DH):
                pe.transpose(bank[0][:, k * QD:k * QD + QD], w_q[:, k * P:k * P + P], ident[:, :])
                pe.transpose(bank[0][:, 256 + k * NE:256 + k * NE + NE], router_w[:, k * P:k * P + P], ident[0:NE, 0:NE])
            pe.transpose(bank[0][:, 300:300 + NP], w_kv4, ident[0:NP, 0:NP]).then_inc(prep_done, 1)
            pe.wait_ge(perm_ready, 1)
            pe.wait_ge(wp_ready, 2 * GB)
            pe.matmul(bank[1][:, 0:NP], bq_perm[:, :], w_pick[0:NL, 0, :], start=True, stop=True).then_inc(kbias_done, 1)
            pe.wait_ge(wqk_copied, 1)
            pe.wait_ge(prep_copied, 4)

            def transposes(i, r, round_):
                pe.wait_ge(ctx_loaded[r], round_ * 32 + 32)
                for n, (b, kb, dh) in enumerate(tgroups()):
                    if n >= 2:
                        pe.wait_ge(t_dve if n % 2 else t_act, i * TGH + n // 2)
                    if dh is None:
                        for d in range(DH):
                            last = pe.transpose(T[n % 2][:, d * P:d * P + TAIL], ring[0:TAIL, r, b, KT, d * P:d * P + P],
                                                ident[0:TAIL, 0:TAIL])
                    else:
                        for a in range(4):
                            last = pe.transpose(T[n % 2][:, a * P:a * P + P], ring[:, r, b, 4 * kb + a, dh * P:dh * P + P],
                                                ident[:, :])
                    last.then_inc(t_done, 1)

            def scores(i, kb):
                if kb == 0:
                    pe.wait_ge(t_act, i * TGH + TGH)
                    pe.wait_ge(t_dve, i * TGH + TGH)
                    pe.wait_ge(q_now_ready, i + 1)
                for dh in range(DH):
                    for b in range(2):
                        last = pe.matmul(S[kb][64 * b:64 * b + 64, 0:KW[kb]], q_now[:, dh, 64 * b:64 * b + 64],
                                         ctxT[:, b, dh, 512 * kb:512 * kb + KW[kb]], start=dh == 0, stop=dh == DH - 1)
                last.then_inc(scores_done, 1)

            def weigh(i, r):
                for kb in range(KB):
                    pe.wait_ge(exp_done, i * KB + (kb + 1))
                    if kb < KB - 1:
                        for a in range(4):
                            last = pe.transpose(S[kb][:, a * P:a * P + P], prob[:, 512 * kb + a * P:512 * kb + a * P + P],
                                                ident[:, :])
                    else:
                        last = pe.transpose(S[kb][0:TAIL, 0:P], prob[:, KT * P:KEYS], ident[:, :])
                    last.then_inc(probT_done, 1)
                for k in range(KT + 1):
                    rows = P if k < KT else TAIL
                    if k % 4 == 0:
                        pe.wait_ge(probT_copied, i * KB + (k // 4 + 1))
                    for b in range(2):
                        last = pe.matmul(U[64 * b:64 * b + 64, 0:D], probT[0:rows, k, 64 * b:64 * b + 64],
                                         ring[0:rows, r, b, k, :], start=k == 0, stop=k == KT)
                last.then_inc(pv_done, 1)

            def turn(i):
                pe.wait_ge(Un_ready, i + 1)
                for dh in range(DH):
                    last = pe.transpose(M[:, dh * P:dh * P + P], Un[:, dh * P:dh * P + P], ident[:, :])
                last.then_inc(UT_done, 1)

            def project(i):
                pe.wait_ge(UT_copied, i + 1)
                for k in range(DH):
                    last = pe.matmul(M[:, D:2 * D], UT[:, k, :], wv[:, k, :], start=k == 0, stop=k == DH - 1)
                last.then_inc(res_done, 1)

            for n in range(4):
                pe.wait_ge(xn_ready, 4 * n + 4)
                if n >= 1:
                    pe.wait_ge(xnT_copied, 2 * n)
                for dh in range(DH):
                    for a in range(4):
                        last = pe.transpose(T[dh][:, a * P:a * P + P], xn_all[:, 4 * n + a, dh * P:dh * P + P], ident[:, :])
                last.then_inc(xnT_done, 1)
                pe.wait_ge(xnT_copied, 2 * n + 2)
                if n >= 1:
                    pe.wait_ge(qT_copied, 2 * n)
                for dc in range(DH):
                    for k in range(DH):
                        last = pe.matmul(bank[6 + dc][:, :], wqk[:, k, dc * P:dc * P + P], xnT[:, k, :],
                                         start=k == 0, stop=k == DH - 1)
                    last.then_inc(qT_done, 1)
            transposes(0, 0, 0)
            pe.wait_ge(bk_row_copied, 1)
            for kb in range(KB):
                scores(0, kb)
            pe.wait_ge(rest_loaded, 64)
            with pe.Fori(0, (PAIRS - 1) // RING) as it:
                for u in range(RING):
                    i = it * RING + (u + 1)
                    transposes(i, (u + 1) % RING, it + (u + 1) // RING)
                    weigh(i - 1, u)
                    for kb in range(KB):
                        if kb == 0:
                            pe.wait_ge(probT_copied, i * KB)
                        if kb == KB - 1:
                            turn(i - 1)
                        scores(i, kb)
                    project(i - 1)
            weigh(PAIRS - 1, (PAIRS - 1) % RING)
            turn(PAIRS - 1)
            project(PAIRS - 1)

            def group_keys(g, r, round_):
                pe.wait_ge(kv_loaded[r], round_ * 16 + 16)
                for dh in range(DH):
                    last = pe.transpose(bank[0][:, dh * P:dh * P + P], kv_in[:, r, dh * P:dh * P + P], ident[:, :])
                last.then_inc(xnT2_done, 1)
                for dh in range(DH):
                    last = pe.matmul(bank[1][:, dh * GB * NP:(dh + 1) * GB * NP], kv_in[:, r, dh * P:dh * P + P],
                                     w_pick[:, :, :].rearrange("p b n -> p (b n)"), start=True, stop=True)
                last.then_inc(vT_done, 1)
                pe.wait_ge(v_blk_ready, g * 2)
                by_head = kv_in[:, r, :].rearrange("p (v h) -> p h v", h=HEADS)
                for b in range(GB):
                    last = pe.matmul(bank[2 + b // 2][0:HG * NP, (b % 2) * D:(b % 2) * D + D],
                                     w_rep[:, b, :, :].rearrange("p h n -> p (h n)"), by_head, start=True, stop=True)
                last.then_inc(vrep_done, 1)
                pe.wait_ge(xnT2_copied, g + 1)
                for k in range(DH):
                    last = pe.matmul(bank[4][:, 0:P], w_qT[:, k, :], x_nT[:, k, :], start=k == 0, stop=k == DH - 1)
                last.then_inc(q2_done, 1)
                pe.wait_ge(vT_copied, g + 1)
                for k in range(DH):
                    last = pe.matmul(bank[1][:, 256:256 + GB * NP], w_kT[:, k, :], vT[:, k, :], start=k == 0, stop=k == DH - 1)
                last.then_inc(k2_done, 1)

            def group_scores(g):
                pe.wait_ge(q2_copied, g + 1)
                pe.wait_ge(k_blk_ready, g + 1)
                for b in range(GB):
                    last = pe.matmul(bank[5][NL * b:NL * b + NL, 0:HEADS * NP], q_T[:, NL * b:NL * b + NL],
                                     k_blk[:, b].rearrange("p h n -> p (h n)"), start=True, stop=True)
                last.then_inc(s2_done, 1)

            def group_weigh(g):
                pe.wait_ge(attn_ready, g + 1)
                flat = attn.rearrange("p h n -> p (h n)")
                for j, (h, n) in enumerate(GROUPS):
                    last = pe.transpose(bank[6][0:n * NP, j * P:j * P + P], flat[:, h * NP:(h + n) * NP], ident[:, :])
                last.then_inc(attnT_done, 1)
                pe.wait_ge(attnT_copied, g + 1)
                pe.wait_ge(v_blk_ready, g * 2 + 2)
                pe.wait_ge(x2_ready, g + 1)
                for b in range(GB):
                    for j, (h, n) in enumerate(GROUPS):
                        last = pe.matmul(bank[7][NL * b:NL * b + NL, h * DV:(h + n) * DV], attnT[0:n * NP, j, NL * b:NL * b + NL],
                                         v_blk[0:n * NP, b, h:h + n, :].rearrange("p h v -> p (h v)"), start=True, stop=True)
                last.then_inc(pv2_done, 1)

            def group_out(g):
                pe.wait_ge(o_copied, g + 1)
                for dh in range(DH):
                    last = pe.transpose(bank[0][:, D + dh * P:D + dh * P + P], o_sb[:, dh * P:dh * P + P], ident[:, :])
                last.then_inc(oT_done, 1)
                pe.wait_ge(oT_copied, g + 1)
                for k in range(DH):
                    last = pe.matmul(bank[7][:, D:2 * D], oT[:, k, :], w_outT[:, k, :], start=k == 0, stop=k == DH - 1)
                last.then_inc(proj_done, 1)

            pe.wait_ge(res_ready, PAIRS)
            pe.wait_ge(kbias_copied, 1)
            pe.wait_ge(small_copied, DH + 2)
            group_keys(0, 0, 0)
            group_scores(0)
            with pe.Fori(0, (NG - 1) // 3) as it:
                for u in range(3):
                    g = it * 3 + (u + 1)
                    group_keys(g, (u + 1) % 3, it + (u + 1) // 3)
                    group_weigh(g - 1)
                    group_scores(g)
                    group_out(g - 1)
            group_weigh(NG - 1)
            group_out(NG - 1)

            for n in range(8):
                q, dh = n // 2, n % 2
                pe.wait_ge(n2_ready, 4 * q + 4)
                for a in range(4):
                    last = pe.transpose(bank[n][:, a * P:a * P + P], n2_first[:, 4 * q + a, dh * P:dh * P + P], ident[:, :])
                last.then_inc(n2T_done, 1)
            pe.wait_ge(n2T_act, 4)
            pe.wait_ge(n2T_dve, 4)
            for g in range(NG):
                for k in range(DH):
                    last = pe.matmul(bank[0][:, g * NE:g * NE + NE], n2T_all[:, k, g * P:g * P + P], router_T[:, k, :],
                                     start=k == 0, stop=k == DH - 1)
            last.then_inc(logits_done, 1)

            def shared_up(q):
                for a, w in enumerate((sh_gateT, sh_upT)):
                    for hc in range(DH):
                        if q >= 1:
                            pe.wait_ge(shared_hid_ready if a else shared_silu, DH * (q - 1) + hc + 1)
                        for k in range(DH):
                            last = pe.matmul(bank[1 + DH * a + hc][:, :], w[:, k, hc * P:hc * P + P],
                                             n2T_all[:, k, 512 * q:512 * q + 512], start=k == 0, stop=k == DH - 1)
                        last.then_inc(shared_up_done, 1)

            def shared_down(q):
                pe.wait_ge(shared_hid_ready, DH * q + DH)
                for a in range(4):
                    m = 4 * q + a
                    if m >= 2:
                        pe.wait_ge(shared_added, m - 1)
                    for hc in range(DH):
                        last = pe.matmul(bank[5 + m % 2][:, 0:D], sh_hid[:, q % 2, hc, a * P:a * P + P], sh_downT[:, hc, :],
                                         start=hc == 0, stop=hc == DH - 1)
                    last.then_inc(shared_done, 1)

            shared_up(0)
            pe.wait_ge(chosen_ready, 1)
            flat = chosen.rearrange("p c e -> p (c e)")
            pe.matmul(bank[7][:, :], below[:, :], flat, start=True, stop=True)
            pe.matmul(bank[0][:, :], ones[:, :], flat, start=True, stop=True).then_inc(before_done, 1)
            for q in range(1, 4):
                shared_up(q)
                shared_down(q - 1)
            shared_down(3)

            def rows_T(s, r, round_):
                pe.wait_ge(row_loaded[r], round_ * 16 + 16)
                for dh in range(DH):
                    last = pe.transpose(bank[r][:, dh * P:dh * P + P], row_in[:, r, dh * P:dh * P + P], ident[:, :])
                last.then_inc(rowT_done, 1)

            def expert_of(s):
                return pe.value_load(expert_i[0:1, bass.ds(s, 1)], min_val=0, max_val=NE - 1)

            def gate_up(s, r):
                e = expert_of(s)
                pe.wait_ge(rowT_copied, s + 1)
                for k in range(DH):
                    last = pe.matmul(bank[2 + r][:, 0:2 * HID], rowT[:, r, k, :], w_gu[:, bass.ds(e, 1), k, :].squeeze(1),
                                     start=k == 0, stop=k == DH - 1)
                last.then_inc(gu_done, 1)

            def hidden_T(s, r):
                pe.wait_ge(hid_ready, s + 1)
                pe.transpose(bank[4 + r][:, 0:P], hid[:, r, :], ident[:, :]).then_inc(hidT_done, 1)

            def back(s, r):
                e = expert_of(s)
                pe.wait_ge(hidT_copied, s + 1)
                pe.matmul(bank[6 + r][:, 0:D], hidT[:, r, :], w_down[:, bass.ds(e, 1), :].squeeze(1), start=True, stop=True)\
                    .then_inc(down_done, 1)

            pe.wait_ge(expert_step, 4)
            pe.wait_ge(experts_loaded, 16 * (2 * DH + 1))
            pe.wait_ge(shared_added, NG)
            pe.wait_ge(place_ready, 1)
            rows_T(0, 0, 0)
            gate_up(0, 0)
            with pe.Fori(0, (SLOTS - 1) // 2) as it:
                for u in range(2):
                    s = it * 2 + (u + 1)
                    r = (u + 1) % 2
                    rows_T(s, r, it + (u + 1) // 2)
                    hidden_T(s - 1, u)
                    gate_up(s, r)
                    back(s - 1, u)
            hidden_T(SLOTS - 1, (SLOTS - 1) % 2)
            back(SLOTS - 1, (SLOTS - 1) % 2)

        @block.vector
        def _(dve):
            dve.wait_ge(qk_loaded, 64)
            dve.tensor_copy(bk_rep[:, :, :], bk_col[:, :].unsqueeze(2).broadcast_to([P, DH, P])).then_inc(bk_rep_ready, 1)
            for n in range(4):
                dve.wait_ge(x_loaded[n], 16)
                for a in range(4 * n, 4 * n + 4):
                    dve.bn_stats(x_stats[:, a, :], x_all[:, a, :]).then_inc(x_stat_ready, 1)
                for a in range(4 * n, 4 * n + 4):
                    dve.wait_ge(x_stat_ready, a + 1)
                    dve.bn_aggr(x_mv[:, a, :], x_stats[:, a, :]).then_inc(x_mv_ready, 1)
            dve.wait_ge(prep_loaded, 16 * (GB + 7))
            dve.tensor_copy(bq_perm[:, :].rearrange("p (h d) -> p h d", h=HEADS),
                            bq_rep.rearrange("p (d h) -> p h d", h=HEADS)).then_inc(perm_ready, 1)
            dve.wait_ge(bconst_loaded, 48)
            dve.tensor_scalar(bq_scaled[:, :], bq_scaled[:, :], Q_SCALE, None, ALU.mult).then_inc(perm_ready, 1)
            dve.wait_ge(prep_done, 5)
            dve.wait_ge(zeroed, 5)
            for b in range(GB):
                mine = slice(NL * b, NL * b + NL)
                dve.tensor_copy(w_pick[mine, b, :], bank[0][mine, 300:300 + NP]).then_inc(wp_ready, 1)
                dve.tensor_copy(w_rep[mine, b, :, :], bank[0][mine, 300:300 + NP].unsqueeze(1).broadcast_to([NL, HG, NP]))\
                    .then_inc(wp_ready, 1)
            dve.tensor_copy(w_qT[:, :, :].rearrange("p a b -> p (a b)"), bank[0][:, 0:DH * QD])\
                .then_inc(small_copied, 1)
            for k in range(DH):
                dve.tensor_copy(w_kT[:, k, :].rearrange("p (h d) -> p h d", h=HEADS),
                                bank[0][:, k * QD:k * QD + QD].rearrange("p (d h) -> p h d", h=HEADS))\
                    .then_inc(small_copied, 1)
            dve.tensor_copy(router_T[:, :, :].rearrange("p a b -> p (a b)"), bank[0][:, 256:256 + DH * NE])\
                .then_inc(small_copied, 1)
            dve.wait_ge(kbias_done, 1)
            dve.tensor_copy(k_bias[:, :], bank[1][:, 0:NP]).then_inc(kbias_copied, 1)
            dve.wait_ge(x_rstd_ready, 1)
            for n in range(4):
                for a in range(4 * n, 4 * n + 4):
                    dve.tensor_scalar(xn_all[:, a, :], x_all[:, a, :], x_mv[:, a, 0:1], x_rstd[:, a:a + 1],
                                      ALU.subtract, ALU.mult).then_inc(xn_ready, 1)
                for dh in range(DH):
                    dve.wait_ge(xnT_done, n + 1)
                    if n >= 1:
                        dve.wait_ge(qT_done, 2 * n)
                    dve.tensor_copy(xnT[:, dh, :], T[dh][:, :]).then_inc(xnT_copied, 1)
            dve.wait_ge(wqk_done, 2)
            dve.tensor_copy(bk_row[:, :], bank[3][:, 0:D + 1]).then_inc(bk_row_copied, 1)
            dve.wait_ge(bk_row_copied, 1)

            def t_evac(i):
                for n in range(1, TG, 2):
                    dve.wait_ge(t_done, i * TG + (n + 1))
                    dve.tensor_copy(*t_copy(n)).then_inc(t_dve, 1)

            def row_max(i):
                for kb in range(KB):
                    dve.wait_ge(scores_done, i * KB + (kb + 1))
                    dve.tensor_reduce(blockmax[:, kb:kb + 1], S[kb][:, 0:KW[kb]], AX.X, ALU.max).then_inc(blockmax_ready, 1)
                dve.wait_ge(blockmax_ready, i * KB + KB)
                dve.tensor_reduce(rowmax[:, :], blockmax[:, :], AX.X, ALU.max).then_inc(rowmax_ready, 1)
                dve.wait_ge(rowmax_ready, i + 1)
                dve.tensor_tensor(topped[:, :], rowmax[:, :], shift[:, bass.ds(i, 1)], ALU.add).then_inc(topped_ready, 1)
                dve.wait_ge(topped_ready, i + 1)
                dve.tensor_tensor(negmax[:, :], shift[:, bass.ds(i, 1)], topped[:, :], ALU.subtract).then_inc(negmax_ready, 1)

            def normalise(k):
                dve.wait_ge(exp_done, k * KB + KB)
                dve.tensor_reduce(rowsum[:, :], sums[:, :], AX.X, ALU.add).then_inc(rowsum_ready, 1)
                dve.wait_ge(rowsum_ready, k + 1)
                dve.reciprocal(rinv[:, :], rowsum[:, :]).then_inc(rinv_ready, 1)
                dve.wait_ge(pv_done, k + 1)
                dve.wait_ge(rinv_ready, k + 1)
                dve.tensor_scalar(Un[:, :], U[:, 0:D], rinv[:, 0:1], None, ALU.mult).then_inc(Un_ready, 1)

            def layer_norms(k):
                dve.wait_ge(res_done, k + 1)
                dve.tensor_tensor(res[:, :], M[:, D:2 * D], xn_all[:, bass.ds(k, 1), :].squeeze(1), ALU.add).then_inc(res_ready, 1)
                dve.wait_ge(res_ready, k + 1)
                dve.bn_stats(stats[:, 0, :], res[:, :]).then_inc(stat_ready, 1)
                dve.wait_ge(stat_ready, 2 * k + 1)
                dve.tensor_copy(seen[:, :], stats[:, 0, 0:1])
                dve.bn_aggr(mv[:, 0, :], stats[:, 0, :]).then_inc(mv_ready, 1)
                dve.wait_ge(mv_ready, 2 * k + 1)
                dve.scalar_tensor_tensor(scaled[:, :], res[:, :], mv[:, 0, 0:1], gamma_b[:, :],
                                         ALU.subtract, ALU.mult).then_inc(scaled_ready, 1)
                dve.wait_ge(scaled_ready, k + 1)
                dve.wait_ge(rstd_ready, 2 * k + 1)
                dve.wait_ge(stored, k * 32 + 32)
                dve.scalar_tensor_tensor(stage[:, 0, :], scaled[:, :], rstd[:, 0:1], x_all[:, bass.ds(k, 1), :].squeeze(1),
                                         ALU.mult, ALU.add).then_inc(x1_ready, 1)
                dve.wait_ge(x1_ready, k + 1)
                dve.bn_stats(stats[:, 1, :], stage[:, 0, :]).then_inc(stat_ready, 1)
                dve.wait_ge(stat_ready, 2 * k + 2)
                dve.tensor_copy(seen[:, :], stats[:, 1, 0:1])
                dve.bn_aggr(mv[:, 1, :], stats[:, 1, :]).then_inc(mv_ready, 1)
                dve.wait_ge(rstd_ready, 2 * k + 2)
                dve.tensor_scalar(stage[:, 1, :], stage[:, 0, :], mv[:, 1, 0:1], rstd[:, 1:2],
                                  ALU.subtract, ALU.mult).then_inc(n1_ready, 1)

            t_evac(0)
            for a in range(PAIRS):
                if a >= 1:
                    dve.wait_ge(dot_ready, a)
                dve.tensor_tensor_reduce(out=dotted[:, :], in0=xn_all[:, a, :], in1=bk_row[:, 0:D], scale=1.0,
                                         scalar=bk_row[:, D:D + 1], op0=ALU.mult, op1=ALU.add,
                                         accum_out=shift[:, a:a + 1]).then_inc(dot_ready, 1)
            dve.wait_ge(dot_ready, PAIRS)
            dve.sem_inc(shift_ready, PAIRS)
            row_max(0)
            t_evac(1)
            dve.wait_ge(rest_loaded, 64)
            dve.wait_ge(xnb_ready, 2)
            with dve.Fori(0, PAIRS - 2) as k:
                normalise(k)
                row_max(k + 1)
                t_evac(k + 2)
                layer_norms(k)
            normalise(PAIRS - 2)
            row_max(PAIRS - 1)
            layer_norms(PAIRS - 2)
            normalise(PAIRS - 1)
            layer_norms(PAIRS - 1)

            def keys_out(g):
                dve.wait_ge(k2_done, g + 1)
                dve.tensor_tensor(k_T, bank[1][:, 256:256 + GB * NP].rearrange("p (b n) -> p b n", b=GB),
                                  k_bias[:, :].unsqueeze(1).broadcast_to([P, GB, NP]), ALU.add).then_inc(k2_copied, 1)

            def values_by_head(g):
                rows = HG * NP
                dve.wait_ge(vrep_done, g + 1)
                for a in range(2):
                    dve.tensor_tensor(v_blk[0:rows, 2 * a:2 * a + 2],
                                      bank[2 + a][0:rows, :].rearrange("p (b h v) -> p b h v", b=2, h=HEADS),
                                      v_mask[0:rows, :].unsqueeze(1).unsqueeze(3).broadcast_to([rows, 2, HEADS, DV]),
                                      ALU.mult).then_inc(v_blk_ready, 1)

            def softmax(g):
                scores_ = bank[5][:, 0:HEADS * NP].rearrange("p (h n) -> p h n", h=HEADS)
                wide = [P, HEADS, NP]
                dve.wait_ge(s2_done, g + 1)
                dve.tensor_reduce(head_max[:, :], scores_, AX.X, ALU.max).then_inc(head_max_ready, 1)
                dve.wait_ge(head_max_ready, g + 1)
                dve.tensor_tensor(attn, scores_, head_max[:, :].unsqueeze(2).broadcast_to(wide), ALU.subtract)\
                    .then_inc(shifted_ready, 1)
                dve.wait_ge(exp2_done, g + 1)
                dve.tensor_reduce(head_sum[:, :], attn, AX.X, ALU.add).then_inc(head_sum_ready, 1)
                dve.wait_ge(head_sum_ready, g + 1)
                dve.reciprocal(head_inv[:, :], head_sum[:, :]).then_inc(head_inv_ready, 1)
                dve.wait_ge(head_inv_ready, g + 1)
                dve.tensor_tensor(attn, attn, head_inv[:, :].unsqueeze(2).broadcast_to(wide), ALU.mult).then_inc(attn_ready, 1)

            def group_norm(g):
                dve.wait_ge(proj_done, g + 1)
                dve.tensor_tensor(x2_all[:, bass.ds(g, 1), :].squeeze(1), bank[7][:, D:2 * D],
                                  x1_all[:, bass.ds(g, 1), :].squeeze(1), ALU.add).then_inc(x2_ready, 1)
                dve.wait_ge(x2_ready, g + 2)
                dve.tensor_copy(seen[:, :], mv[:, 0, 0:1])
                dve.bn_stats(stats[:, 0, :], x2_all[:, bass.ds(g, 1), :].squeeze(1)).then_inc(stat2_ready, 1)
                dve.wait_ge(stat2_ready, g + 1)
                dve.tensor_copy(seen[:, :], stats[:, 0, 0:1])
                dve.bn_aggr(mv[:, 0, :], stats[:, 0, :]).then_inc(mv2_ready, 1)
                dve.wait_ge(rstd2_ready, g + 1)
                dve.tensor_scalar(n2_first[:, bass.ds(g, 1), 0:D].squeeze(1), x2_all[:, bass.ds(g, 1), :].squeeze(1),
                                  mv[:, 0, 0:1], rstd[:, 0:1], ALU.subtract, ALU.mult).then_inc(n2_ready, 1)

            dve.wait_ge(x1b_ready, 1)
            dve.wait_ge(masks_ready, 11)
            dve.sem_inc(x2_ready, 1)
            keys_out(0)
            values_by_head(0)
            with dve.Fori(0, NG - 1) as k:
                softmax(k)
                keys_out(k + 1)
                dve.wait_ge(pv2_done, k + 1)
                values_by_head(k + 1)
                group_norm(k)
            softmax(NG - 1)
            group_norm(NG - 1)

            for n in range(1, 8, 2):
                dve.wait_ge(n2T_done, n + 1)
                dve.tensor_copy(n2T_all[:, 1, 512 * (n // 2):512 * (n // 2) + 512], bank[n][:, :]).then_inc(n2T_dve, 1)
            dve.wait_ge(logits_done, 1)
            dve.tensor_tensor(logits, bank[0][:, 0:NG * NE].rearrange("p (g e) -> p g e", g=NG),
                              rbias_b[:, :].unsqueeze(1).broadcast_to([P, NG, NE]), ALU.add).then_inc(logits_ready, 1)
            dve.wait_ge(logits_ready, 1)
            for g in range(NG):
                dve.max(best[:, g, :], logits[:, g, :]).then_inc(best_ready, 1)
            for g in range(NG):
                dve.wait_ge(best_ready, g + 1)
                dve.max_index(best_at[:, g, :], best[:, g, :], logits[:, g, :]).then_inc(best_at_ready, 1)
            dve.wait_ge(best_at_ready, NG)
            dve.tensor_copy(best_f[:, :, :], best_at[:, :, 0:TOPK]).then_inc(best_f_ready, 1)
            dve.wait_ge(best_f_ready, 1)
            wide = [P, NK, NE]
            dve.tensor_tensor(chosen, best_f[:, :, :].rearrange("p g k -> p (g k)").unsqueeze(2).broadcast_to(wide),
                              lane[:, :].unsqueeze(1).broadcast_to(wide), ALU.is_equal).then_inc(chosen_ready, 1)
            dve.tensor_tensor(gap_w[:, :], best[:, :, 1], best[:, :, 0], ALU.subtract).then_inc(gap_ready, 1)
            dve.wait_ge(before_done, 1)
            dve.wait_ge(dest_ready, TOPK + 4)
            in_tile = bank[0][:, :].rearrange("p (c e) -> p c e", e=NE)
            earlier = bank[7][:, :].rearrange("p (c e) -> p c e", e=NE)
            dve.tensor_copy(count_a[:, NK:, :], in_tile).then_inc(count_step, 1)
            of, to, step, n = count_a, count_b, 1, 1
            while step < NK:
                dve.wait_ge(count_step, n)
                dve.tensor_tensor(to[:, NK:, :], of[:, NK:, :], of[:, NK - step:2 * NK - step, :], ALU.add).then_inc(count_step, 1)
                of, to, step, n = to, of, 2 * step, n + 1
            dve.wait_ge(count_step, n)
            counted, spare = of, to
            dve.tensor_scalar(tiles_f[:, :], counted[:, 2 * NK - 1, :], float(P - 1), None, ALU.add).then_inc(tiles_step, 1)
            dve.wait_ge(tiles_step, 1)
            dve.tensor_copy(tiles_i[:, :], tiles_f[:, :]).then_inc(tiles_step, 1)
            dve.wait_ge(tiles_step, 2)
            dve.tensor_single_scalar(tiles_h[:, :], tiles_i[:, :], P.bit_length() - 1, ALU.logical_shift_right).then_inc(tiles_step, 1)
            dve.wait_ge(tiles_step, 3)
            dve.tensor_copy(tiles_n[:, :], tiles_h[:, :]).then_inc(tiles_step, 1)
            dve.tensor_copy(cum_a[:, NE:], tiles_h[:, :]).then_inc(tiles_step, 1)
            cum, nxt, step, n = cum_a, cum_b, 1, 5
            while step < NE:
                dve.wait_ge(tiles_step, n)
                dve.tensor_tensor(nxt[:, NE:], cum[:, NE:], cum[:, NE - step:2 * NE - step], ALU.add).then_inc(tiles_step, 1)
                cum, nxt, step, n = nxt, cum, 2 * step, n + 1
            dve.wait_ge(tiles_step, n)
            dve.tensor_tensor(first_row[:, :], cum[:, NE:], tiles_n[:, :], ALU.subtract).then_inc(first_ready, 1)
            dve.tensor_tensor(place, counted[:, NK:, :], in_tile, ALU.subtract).then_inc(place_step, 1)
            dve.wait_ge(place_step, 1)
            dve.tensor_tensor(place, place, earlier, ALU.add).then_inc(place_step, 1)
            dve.wait_ge(place_step, 2)
            dve.wait_ge(first_ready, 1)
            dve.scalar_tensor_tensor(place, first_row[:, :].unsqueeze(1).broadcast_to(wide), float(P), place,
                                     ALU.mult, ALU.add).then_inc(place_step, 1)
            dve.wait_ge(place_step, 3)
            dve.tensor_tensor(place, place, chosen, ALU.mult).then_inc(place_step, 1)
            dve.wait_ge(place_step, 4)
            dve.tensor_reduce(place_f[:, :], place, AX.X, ALU.add).then_inc(place_step, 1)
            dve.wait_ge(place_step, 5)
            dve.tensor_copy(place_i[:, :], place_f[:, :]).then_inc(place_ready, 1)
            most = [1, SLOTS + 1, NE]
            dve.tensor_tensor(passed, tile_no[:, :].unsqueeze(2).broadcast_to(most),
                              cum[0:1, NE:].unsqueeze(1).broadcast_to(most), ALU.is_ge).then_inc(expert_step, 1)
            dve.wait_ge(expert_step, 1)
            dve.tensor_reduce(expert_f[:, :], passed, AX.X, ALU.add).then_inc(expert_step, 1)
            dve.wait_ge(expert_step, 2)
            dve.tensor_scalar(expert_m[:, :], expert_f[:, :], float(NE - 1), None, ALU.min).then_inc(expert_step, 1)
            dve.wait_ge(expert_step, 3)
            dve.tensor_copy(expert_i[:, :], expert_m[:, :]).then_inc(expert_step, 1)
            dve.wait_ge(gap_exp, 1)
            dve.tensor_scalar(gap_s[:, :], gap_e[:, :], 1.0, None, ALU.add).then_inc(gap_sum_ready, 1)
            dve.wait_ge(gap_sum_ready, 1)
            dve.reciprocal(mix[:, 0, :], gap_s[:, :]).then_inc(mix_ready, 1)
            dve.wait_ge(mix_ready, 1)
            dve.tensor_tensor(mix[:, 1, :], gap_e[:, :], mix[:, 0, :], ALU.mult).then_inc(mix_ready, 1)

            def shared_hidden(q):
                for hc in range(DH):
                    dve.wait_ge(shared_silu, DH * q + hc + 1)
                    dve.wait_ge(shared_up_done, 2 * DH * q + DH + hc + 1)
                    if q >= 2:
                        dve.wait_ge(shared_done, 4 * (q - 1))
                    dve.tensor_tensor(sh_hid[:, q % 2, hc, :], bank[1 + DH + hc][:, :], sh_silu[:, hc, :], ALU.mult)\
                        .then_inc(shared_hid_ready, 1)

            def shared_add(q):
                for m in range(4 * q, 4 * q + 4):
                    dve.wait_ge(shared_done, m + 1)
                    dve.tensor_tensor(x2_all[:, m, :], x2_all[:, m, :], bank[5 + m % 2][:, 0:D], ALU.add).then_inc(shared_added, 1)

            shared_hidden(0)
            for q in range(1, 4):
                shared_hidden(q)
                shared_add(q - 1)
            shared_add(3)

            def hidden(s, r, round_):
                dve.wait_ge(row_loaded[r], round_ * 16 + 16)
                dve.tensor_copy(dest[:, r:r + 1], row_in[:, r, D:ROW].bitcast(u32)).then_inc(dest_copied, 1)
                dve.wait_ge(silu_done, s + 1)
                dve.tensor_tensor(hid[:, r, :], bank[2 + r][:, HID:2 * HID], silu_g[:, r, :], ALU.mult).then_inc(hid_ready, 1)

            def result(s, r):
                dve.wait_ge(down_done, s + 1)
                dve.tensor_copy(y_sb[:, r, :], bank[6 + r][:, 0:D]).then_inc(y_ready, 1)

            hidden(0, 0, 0)
            hidden(1, 1, 0)
            result(0, 0)
            with dve.Fori(0, (SLOTS - 2) // 2) as it:
                for r in range(2):
                    s = it * 2 + (2 + r)
                    dve.wait_ge(y_sent[r], it * 16 + 16)
                    hidden(s, r, it + 1)
                    result(s - 1, 1 - r)
            for s in range(2 + (SLOTS - 2) // 2 * 2, SLOTS):
                dve.wait_ge(y_sent[s % 2], 16 * (s // 2))
                hidden(s, s % 2, s // 2)
                result(s - 1, 1 - s % 2)
            result(SLOTS - 1, (SLOTS - 1) % 2)

            for n in range(4):
                dve.wait_ge(y_loaded[n], 32)
                dve.wait_ge(mix_ready, 2)
                for g in range(4 * n, 4 * n + 4):
                    dve.scalar_tensor_tensor(x2_all[:, g, :], y_all[0][:, g, :], mix[:, 0, g:g + 1], x2_all[:, g, :],
                                             ALU.mult, ALU.add).then_inc(mixed_ready, 1)
                for g in range(4 * n, 4 * n + 4):
                    dve.wait_ge(mixed_ready, g + 1)
                    dve.scalar_tensor_tensor(x2_all[:, g, :], y_all[1][:, g, :], mix[:, 1, g:g + 1], x2_all[:, g, :],
                                             ALU.mult, ALU.add).then_inc(out_ready, 1)


_INS = ["x", "ctx_1024", "L0_xattn_Wq", "L0_xattn_bq", "L0_xattn_Wk", "L0_xattn_bk", "L0_xattn_Wv", "L0_xattn_bv",
        "L0_xattn_gamma", "L0_xattn_beta", "L0_attn_w_kv", "L0_attn_w_q", "L0_attn_b_q", "L0_attn_w_out", "L0_attn_b_out",
        "L0_ffn_router_w", "L0_ffn_router_bias", "L0_ffn_up_proj", "L0_ffn_gate_proj", "L0_ffn_down_proj",
        "L0_ffn_sh_gate", "L0_ffn_sh_up", "L0_ffn_sh_down"]


def kernel(**inputs):
    import numpy as _np
    import concourse.bacc as _bacc
    from concourse import mybir as _mybir
    from concourse.bass_utils import run_bass_kernel_spmd as _run

    nc = _bacc.Bacc("TRN2", target_bir_lowering=False, num_devices=1)
    arrays, tensors = {}, {}
    for name in _INS:
        a = _np.ascontiguousarray(inputs[name])
        arrays[f"in_{name}_dram"] = a
        tensors[name] = nc.dram_tensor(f"in_{name}_dram", a.shape, _mybir.dt.from_np(a.dtype), kind="ExternalInput").ap()
    shape = inputs["x"].shape
    out = nc.dram_tensor("out_dram", shape, _mybir.dt.from_np(_np.dtype("float32")), kind="ExternalOutput").ap()
    perceiver_layer(nc, tensors, out)
    r = _run(nc, [arrays], core_ids=[0])
    return r.results[0]["out_dram"]
```

```python
from contextlib import ExitStack

import concourse.bass as bass
from concourse import mybir


def perceiver_layer(nc, t, out):
    fp32 = mybir.dt.float32
    i32 = mybir.dt.int32
    u32 = mybir.dt.uint32
    ALU = mybir.AluOpType
    ACT = mybir.ActivationFunctionType
    AX = mybir.AxisListType

    x_in, ctx_in = t["x"], t["ctx_1024"]
    NL, NB, D = x_in.shape
    KEYS = ctx_in.shape[1]
    P = 128
    DH = D // P
    TOK = NL * NB
    PAIRS = TOK // P
    KT = KEYS // P
    TAIL = KEYS - KT * P
    KB = -(-KEYS // 512)
    KW = [min(512, KEYS - 512 * kb) for kb in range(KB)]
    LN_EPS = 1e-5
    TG = 2 * (2 * (KB - 1) + 1)
    TGH = TG // 2
    PH = KB // 2
    PV_LATE = 6
    RING = 3

    QD = t["L0_attn_w_q"].shape[0]
    HEADS = 16
    HD = QD // HEADS
    DV = D // HEADS
    NP = NL // 2 + 1
    Q_SCALE = float(DV) ** -0.5
    NG = TOK // P
    GB = P // NL
    CHUNKS = (4, 5, 5, 2)
    ROWS = 4
    KV_RING = 4
    HG = 6
    GROUPS = [(h, min(HG, HEADS - h)) for h in range(0, HEADS, HG)]

    NE, _, HID = t["L0_ffn_up_proj"].shape
    TOPK = 2
    NK = NG * TOPK
    SLOTS = (TOPK * TOK + NE * (P - 1)) // P
    NOWHERE = TOPK * TOK
    ROW = D + 1

    cross = ExitStack()
    with cross:
        def sb(name, shape, dt=fp32):
            return cross.enter_context(nc.sbuf_tensor(name, shape, dt))

        def sem(name):
            return cross.enter_context(nc.semaphore(name))

        bank = [cross.enter_context(nc.psum_tensor(f"bank{n}", [P, 512], fp32)) for n in range(8)]
        mid = nc.dram_tensor("mid", [TOK, 2 * D], fp32).ap()
        rows_dram = nc.dram_tensor("rows_by_expert", [SLOTS * P, ROW], fp32).ap()
        y_dram = nc.dram_tensor("expert_out", [TOPK * TOK, D], fp32).ap()

        ident = sb("ident", [P, P])
        ones = sb("ones", [P, P])
        ring_mem = sb("ring", [P, RING * 2 * (KT + 1) * D])
        ring = ring_mem[:, :].rearrange("p (r b k c) -> p r b k c", r=RING, b=2, c=D)
        ctxT_mem = sb("ctxT", [P, 2 * DH * KEYS])
        ctxT = ctxT_mem[:, :].rearrange("p (b d k) -> p b d k", b=2, d=DH)
        prob_mem = sb("prob", [P, KEYS + (KT + 1) * P])
        prob = prob_mem[:, 0:KEYS]
        probT = prob_mem[:, KEYS:].rearrange("p (k q) -> p k q", q=P)
        x_all = sb("x_all", [P, PAIRS, D])
        xn_mem = sb("xn_all", [P, PAIRS * ROW])
        xn_all = xn_mem[:, 0:PAIRS * D].rearrange("p (i c) -> p i c", c=D)
        qT_mem = sb("qT_all", [P, DH * TOK])
        qT_all = qT_mem[:, :].rearrange("p (d s) -> p d s", d=DH)
        q_now = sb("q_now", [P, DH, P])

        def views(mem, *shapes):
            at, got = 0, []
            for shape in shapes:
                size = 1
                for n in shape[1:]:
                    size *= n
                piece = mem[0:shape[0], at:at + size]
                if len(shape) > 2:
                    names = "abcd"[:len(shape) - 1]
                    piece = piece.rearrange(f"p ({' '.join(names)}) -> p {' '.join(names)}",
                                            **dict(zip(names[1:], shape[2:])))
                got.append(piece)
                at += size
            return got

        third = ring_mem[:, 2 * 2 * (KT + 1) * D:]
        wq, wk, w_q, w_out, sh_gate, sh_up, sh_down, router_w, w_kv4, xnT = views(
            third, [P, DH, D], [P, DH, D], [P, D], [P, DH, D], [P, DH, D], [P, DH, D], [P, DH, D],
            [NE, D], [NP, P], [P, 2, DH, 512])
        wv = sb("wv", [P, DH, D])
        wqT = sb("wqT", [P, DH, D])
        wkT = sb("wkT", [P, DH, D])
        wqk = sb("wqk", [P, DH, D])
        bq_col = sb("bq_col", [P, DH])
        bk_col = sb("bk_col", [P, DH])
        bk_rep = sb("bk_rep", [P, DH, P])
        bqk_col = sb("bqk_col", [P, DH])
        bk_row = sb("bk_row", [P, D + 1])
        gamma_b = sb("gamma_b", [P, D])
        beta_b = sb("beta_b", [P, D])
        bv_b = sb("bv_b", [P, D])
        x_stats = sb("x_stats", [P, PAIRS, 6])
        x_mv = sb("x_mv", [P, PAIRS, 2])
        x_rstd = sb("x_rstd", [P, PAIRS])
        x_var = sb("x_var", [P, PAIRS])
        shift = sb("shift", [P, PAIRS])
        dotted = sb("dotted", [P, D])
        eps = sb("eps", [P, 1])
        seen = sb("seen", [P, 1])
        m_half = sb("m_half", [P, PAIRS])
        blockmax = sb("blockmax", [P, KB])
        rowmax = sb("rowmax", [P, 1])
        topped = sb("topped", [P, 1])
        negmax = sb("negmax", [P, 1])
        sums = sb("sums", [P, KB])
        rowsum = sb("rowsum", [P, 1])
        rinv = sb("rinv", [P, 1])
        Un = sb("Un", [P, D])
        UT = sb("UT", [P, DH, P])
        res = sb("res", [P, D])
        scaled = sb("scaled", [P, D])
        stats = sb("stats", [P, 2, 6])
        mv = sb("mv", [P, 2, 2])
        var = sb("var", [P, 2])
        rstd = sb("rstd", [P, 2])
        stage = sb("stage", [P, 2, D])

        w_qT = sb("w_qT", [P, DH, QD])
        w_outT = sb("w_outT", [P, DH, D])
        bout_b = sb("bout_b", [P, D])
        bq2_col = sb("bq2_col", [P, 1])
        w_pick = sb("w_pick", [P, GB, NP])
        w_rep = sb("w_rep", [P, GB, HG, NP])
        k_mask = sb("k_mask", [P, HEADS])
        v_mask = sb("v_mask", [P, HEADS])
        (kv_in, x_nT, q_T, q_nat, k_T, k_blk, v_blk_even, attn, attnT, o_sb, oT, n2_now) = views(
            ctxT_mem, [P, KV_RING, D], [P, DH, P], [P, 2, P], [P, P], [P, GB, NP], [P, GB, HEADS, NP],
            [P, GB, HEADS, DV], [P, HEADS, NP], [P, len(GROUPS), P], [P, D], [P, DH, P], [P, D])
        head_max = sb("head_max", [P, HEADS])
        head_sum = sb("head_sum", [P, HEADS])
        head_inv = sb("head_inv", [P, HEADS])
        x1_all = qT_mem[:, :].rearrange("p (g c) -> p g c", c=D)
        x2_all = x_all
        router_T = sb("router_T", [P, DH, NL])
        rbias_b = sb("rbias_b", [P, NE])
        sh_gateT = sb("sh_gateT", [P, DH, D])
        sh_upT = sb("sh_upT", [P, DH, D])
        sh_downT = sb("sh_downT", [P, DH, D])
        below = sb("below", [P, P])
        lane = sb("lane", [P, NE])
        tile_no = sb("tile_no", [1, SLOTS + 1])
        blank = sb("blank", [P, ROW])
        w_gu, w_down, n2_first, n2T_low, passed = views(
            ring_mem, [P, NE, DH, 2 * HID], [P, NE, D], [P, NG, ROW], [P, TOK], [1, SLOTS + 1, NE])
        n2T_high, v_blk_odd = views(prob_mem, [P, TOK], [P, GB, HEADS, DV])
        y_sb = views(prob_mem, [P, TOK], [P, ROWS, D])[1]
        n2T = [n2T_low, n2T_high]
        v_blk = [v_blk_even, v_blk_odd]
        n2_second = xn_mem[:, :].rearrange("p (g c) -> p g c", c=ROW)
        n2 = [n2_first, n2_second]
        y_all = [qT_mem[:, :].rearrange("p (g c) -> p g c", c=D), xn_all]
        logits, count_a, count_b, chosen, place, logitsT = views(
            qT_mem, [P, NG, NE], [P, 2 * NK, NE], [P, 2 * NK, NE], [P, NK, NE], [P, NK, NE], [P, 512])
        (sh_silu, sh_hid, best, best_at, row_in, rowT, silu_g, hid, hidT) = views(
            ctxT_mem, [P, DH, 512], [P, 2, DH, 512], [P, NG, 8], [P, NG, 8], [P, ROWS, ROW], [P, 2, DH, P],
            [P, 2, HID], [P, 2, HID], [P, 2, P])
        best_at = best_at.bitcast(u32)
        best_f = sb("best_f", [P, NG, TOPK])
        gap_w = sb("gap_w", [P, NG])
        gap_e = sb("gap_e", [P, NG])
        gap_s = sb("gap_s", [P, NG])
        mix = sb("mix", [P, TOPK, NG])
        tiles_f = sb("tiles_f", [P, NE])
        tiles_i = sb("tiles_i", [P, NE], i32)
        tiles_h = sb("tiles_h", [P, NE], i32)
        tiles_n = sb("tiles_n", [P, NE])
        cum_a = sb("cum_a", [P, 2 * NE])
        cum_b = sb("cum_b", [P, 2 * NE])
        first_row = sb("first_row", [P, NE])
        place_f = sb("place_f", [P, NK])
        place_i = sb("place_i", [P, NK], u32)
        expert_f = sb("expert_f", [1, SLOTS + 1])
        expert_m = sb("expert_m", [1, SLOTS + 1])
        expert_up = sb("expert_up", [1, SLOTS + 1 + ROWS], i32)
        expert_back = sb("expert_back", [1, SLOTS + 1 + ROWS], i32)
        dest = sb("dest", [P, SLOTS], u32)

        S = bank[0:KB]
        T = bank[4:6]
        U = bank[6]
        M = bank[7]

        x_loaded = [sem(f"x_loaded{n}") for n in range(4)]
        qk_loaded = sem("qk_loaded")
        rest_loaded = sem("rest_loaded")
        ctx_loaded = [sem(f"ctx_loaded{r}") for r in range(RING)]
        stored = sem("stored")
        const_step = sem("const_step")
        wT_done = sem("wT_done")
        wT_copied = sem("wT_copied")
        bk_rep_ready = sem("bk_rep_ready")
        wqk_done = sem("wqk_done")
        wqk_copied = sem("wqk_copied")
        bk_row_copied = sem("bk_row_copied")
        x_stat_ready = sem("x_stat_ready")
        x_mv_ready = sem("x_mv_ready")
        x_var_ready = sem("x_var_ready")
        x_rstd_ready = sem("x_rstd_ready")
        xn_ready = sem("xn_ready")
        dot_ready = sem("dot_ready")
        shift_ready = sem("shift_ready")
        xnT_done = sem("xnT_done")
        xnT_copied = sem("xnT_copied")
        qT_done = sem("qT_done")
        qT_copied = sem("qT_copied")
        xnb_ready = sem("xnb_ready")
        q_now_ready = sem("q_now_ready")
        t_done = sem("t_done")
        t_act = sem("t_act")
        t_dve = sem("t_dve")
        scores_done = sem("scores_done")
        blockmax_ready = sem("blockmax_ready")
        rowmax_ready = sem("rowmax_ready")
        topped_ready = sem("topped_ready")
        negmax_ready = sem("negmax_ready")
        exp_done = sem("exp_done")
        probT_done = sem("probT_done")
        probT_act = sem("probT_act")
        probT_dve = sem("probT_dve")
        pv_done = sem("pv_done")
        rowsum_ready = sem("rowsum_ready")
        rinv_ready = sem("rinv_ready")
        Un_ready = sem("Un_ready")
        UT_done = sem("UT_done")
        UT_copied = sem("UT_copied")
        res_done = sem("res_done")
        res_ready = sem("res_ready")
        stat_ready = sem("stat_ready")
        mv_ready = sem("mv_ready")
        var_ready = sem("var_ready")
        rstd_ready = sem("rstd_ready")
        scaled_ready = sem("scaled_ready")
        x1_ready = sem("x1_ready")
        n1_ready = sem("n1_ready")
        prep_loaded = sem("prep_loaded")
        qkb_loaded = sem("qkb_loaded")
        masks_ready = sem("masks_ready")
        prep_done = sem("prep_done")
        prep_copied = sem("prep_copied")
        smalls_ready = sem("smalls_ready")
        zeroed = sem("zeroed")
        x1b_ready = sem("x1b_ready")
        xnT2_done = sem("xnT2_done")
        xnT2_copied = sem("xnT2_copied")
        vrep_done = sem("vrep_done")
        v_blk_ready = sem("v_blk_ready")
        qN_done = sem("qN_done")
        qN_copied = sem("qN_copied")
        n2T_copied = sem("n2T_copied")
        q2_done = sem("q2_done")
        q2_copied = sem("q2_copied")
        k2_done = sem("k2_done")
        k2_copied = sem("k2_copied")
        k_blk_ready = sem("k_blk_ready")
        s2_done = sem("s2_done")
        head_max_ready = sem("head_max_ready")
        shifted_ready = sem("shifted_ready")
        exp2_done = sem("exp2_done")
        head_sum_ready = sem("head_sum_ready")
        head_inv_ready = sem("head_inv_ready")
        attnT_done = sem("attnT_done")
        attnT_copied = sem("attnT_copied")
        pv2_done = sem("pv2_done")
        o_copied = sem("o_copied")
        oT_done = sem("oT_done")
        oT_copied = sem("oT_copied")
        proj_done = sem("proj_done")
        x2_ready = sem("x2_ready")
        stat2_ready = sem("stat2_ready")
        mv2_ready = sem("mv2_ready")
        var2_ready = sem("var2_ready")
        rstd2_ready = sem("rstd2_ready")
        n2_ready = sem("n2_ready")
        n2a_ready = sem("n2a_ready")
        n2b_ready = sem("n2b_ready")
        experts_loaded = sem("experts_loaded")
        blank_ready = sem("blank_ready")
        blanked = sem("blanked")
        n2T_done = sem("n2T_done")
        logitsT_done = sem("logitsT_done")
        logitsT_copied = sem("logitsT_copied")
        logits_done = sem("logits_done")
        logits_ready = sem("logits_ready")
        best_ready = sem("best_ready")
        best_at_ready = sem("best_at_ready")
        best_f_ready = sem("best_f_ready")
        chosen_ready = sem("chosen_ready")
        before_done = sem("before_done")
        gap_ready = sem("gap_ready")
        gap_exp = sem("gap_exp")
        gap_sum_ready = sem("gap_sum_ready")
        mix_ready = sem("mix_ready")
        count_step = sem("count_step")
        tiles_step = sem("tiles_step")
        first_ready = sem("first_ready")
        place_step = sem("place_step")
        place_ready = sem("place_ready")
        expert_step = sem("expert_step")
        dest_ready = sem("dest_ready")
        scattered = sem("scattered")
        shared_up_done = sem("shared_up_done")
        shared_silu = sem("shared_silu")
        shared_hid_ready = sem("shared_hid_ready")
        shared_done = sem("shared_done")
        shared_added = sem("shared_added")
        rowT_done = sem("rowT_done")
        rowT_copied = sem("rowT_copied")
        dest_copied = sem("dest_copied")
        gu_done = sem("gu_done")
        silu_done = sem("silu_done")
        hid_ready = sem("hid_ready")
        hidT_done = sem("hidT_done")
        hidT_copied = sem("hidT_copied")
        down_done = sem("down_done")
        y_ready = sem("y_ready")
        mixed_ready = sem("mixed_ready")
        out_ready = sem("out_ready")
        written = sem("written")
        kv_loaded = [sem(f"kv_loaded{r}") for r in range(KV_RING)]
        row_loaded = [sem(f"row_loaded{r}") for r in range(ROWS)]
        y_sent = [sem(f"y_sent{r}") for r in range(ROWS)]
        y_loaded = [sem(f"y_loaded{n}") for n in range(len(CHUNKS))]

        block = cross.enter_context(nc.Block())

        TGROUPS = [(kb, b, dh) for kb in range(KB - 1) for b in range(2) for dh in range(DH)] \
            + [(KB - 1, b, None) for b in range(2)]
        USES = [("T", n) for n in range(6)] + [("P", 0), ("T", 6), ("T", 7), ("P", 1)] \
            + [("T", n) for n in range(8, 12)] + [("P", 2), ("T", 12), ("T", 13), ("P", 3)]

        def count_of(use, i):
            kind, n = USES[use]
            mine = sum(1 for m in range(use % 2, use + 1, 2) if USES[m][0] == kind)
            if kind == "T":
                return (t_dve if use % 2 else t_act), i * TGH + mine
            return (probT_dve if use % 2 else probT_act), (i - 1) * PH + mine

        def done_of(use, i):
            kind, n = USES[use]
            return (t_done, i * TG + (n + 1)) if kind == "T" else (probT_done, (i - 1) * KB + (n + 1))

        def copy_of(use):
            (kind, n), of = USES[use], T[use % 2]
            if kind == "P":
                rows, tiles = (P, 4) if n < KB - 1 else (TAIL, 1)
                return probT[0:rows, 4 * n:4 * n + tiles, :].rearrange("p a b -> p (a b)"), of[0:rows, 0:tiles * P]
            kb, b, dh = TGROUPS[n]
            if dh is None:
                return (ctxT[:, b, :, KT * P:KEYS],
                        of[:, 0:DH * P].rearrange("p (d k) -> p d k", d=DH)[:, :, 0:TAIL])
            return ctxT[:, b, dh, kb * 512:(kb + 1) * 512], of[:, :]

        @block.sync
        def _(sp):
            rows = x_in.rearrange("l b c -> (l b) c").rearrange("(i p) c -> p i c", p=P)
            for to, of in ((wq, "L0_xattn_Wq"), (wk, "L0_xattn_Wk")):
                sp.dma_start(to[:, :, :], t[of].rearrange("(k p) f -> p k f", p=P)).then_inc(qk_loaded, 16)
            for n in range(4):
                sp.dma_start(x_all[:, 4 * n:4 * n + 4, :], rows[:, 4 * n:4 * n + 4, :]).then_inc(x_loaded[n], 16)

            def load(i, r):
                pair = ctx_in[bass.ds(2 * i, 2)]
                sp.dma_start(ring[:, r, :, 0:KT, :].rearrange("p b k c -> p b (k c)"),
                             pair[:, 0:KT * P, :].rearrange("b (p k) c -> p b (k c)", k=KT)).then_inc(ctx_loaded[r], 16)
                sp.dma_start(ring[0:TAIL, r, :, KT, :],
                             pair[:, KT * P:KEYS, :].rearrange("b p c -> p b c")).then_inc(ctx_loaded[r], 16)

            def store(k):
                sp.wait_ge(n1_ready, k + 1)
                cols = mid.rearrange("(g q l) c -> l q g c", g=16, q=4)
                for b in range(2):
                    sp.dma_start(cols[bass.ds(2 * k + b, 1)].squeeze(0),
                                 stage[64 * b:64 * b + 64, :, :].rearrange("p a c -> p (a c)")).then_inc(stored, 16)

            sp.sem_inc(stored, 32)
            for i in range(RING):
                if i == 1:
                    sp.dma_start(w_q, t["L0_attn_w_q"]).then_inc(prep_loaded, 16)
                    for q in range(GB):
                        sp.dma_start(w_kv4[:, NL * q:NL * q + NL], t["L0_attn_w_kv"][0:NP, 0:NL]).then_inc(prep_loaded, 16)
                    sp.dma_start(router_w, t["L0_ffn_router_w"]).then_inc(prep_loaded, 16)
                    for to, of in ((w_out, "L0_attn_w_out"), (sh_gate, "L0_ffn_sh_gate"), (sh_up, "L0_ffn_sh_up"),
                                   (sh_down, "L0_ffn_sh_down")):
                        sp.dma_start(to, t[of].rearrange("(k p) c -> p k c", p=P)).then_inc(prep_loaded, 16)
                if i == 2:
                    sp.wait_ge(prep_done, 5)
                    sp.wait_ge(wT_done, 2)
                    sp.wait_ge(qT_done, 8)
                load(i, i)
            sp.wait_ge(pv_done, 1)
            load(RING, 0)
            with sp.Fori(0, (PAIRS - RING - 1) // RING) as it:
                for u in range(RING):
                    i = it * RING + (RING + 1 + u)
                    sp.wait_ge(pv_done, i - (RING - 1))
                    load(i, (RING + 1 + u) % RING)
                    store(i - RING - 1)
            for k in range(PAIRS - RING - 1, PAIRS):
                store(k)
            sp.wait_ge(stored, 32 * (PAIRS + 1))

            def load_group(g, r):
                rows = mid[bass.ds(g * P, P)]
                sp.dma_start(kv_in[:, r, :], rows[:, D:2 * D]).then_inc(kv_loaded[r], 16)
                sp.dma_start(x1_all[:, bass.ds(g, 1), :].squeeze(1), rows[:, 0:D]).then_inc(kv_loaded[r], 16)

            def load_expert(e):
                for a, of in enumerate(("gate", "up")):
                    sp.dma_start(w_gu[:, bass.ds(e, 1), :, a * HID:(a + 1) * HID].squeeze(1),
                                 t[f"L0_ffn_{of}_proj"][bass.ds(e, 1)].squeeze(0).rearrange("(k p) h -> p k h", p=P))\
                        .then_inc(experts_loaded, 16)
                sp.dma_start(w_down[:, bass.ds(e, 1), :].squeeze(1), t["L0_ffn_down_proj"][bass.ds(e, 1)].squeeze(0))\
                    .then_inc(experts_loaded, 16)

            BLANKED = SLOTS // (NG - KV_RING)

            def blank_tiles(s, n):
                sp.dma_start(rows_dram[bass.ds(s * P, n * P)].rearrange("(s p) c -> p s c", p=P),
                             blank[:, :].unsqueeze(1).broadcast_to([P, n, ROW])).then_inc(blanked, 16)

            for g in range(KV_RING):
                load_group(g, g)
            for e in range(NE - (NG - KV_RING)):
                load_expert(e)
            sp.wait_ge(blank_ready, 2)
            with sp.Fori(1, NG // KV_RING) as it:
                for u in range(KV_RING):
                    g = it * KV_RING + u
                    sp.wait_ge(vrep_done, g - (KV_RING - 1))
                    load_group(g, u)
                    load_expert(g + (NE - NG))
                    blank_tiles((g - KV_RING) * BLANKED, BLANKED)
            blank_tiles((NG - KV_RING) * BLANKED, SLOTS - (NG - KV_RING) * BLANKED)

            def load_rows(s, r):
                sp.dma_start(row_in[:, r, :], rows_dram[bass.ds(s * P, P), :]).then_inc(row_loaded[r], 16)

            sp.wait_ge(scattered, 16 * NK)
            for s in range(ROWS):
                load_rows(s, s)
            with sp.Fori(1, SLOTS // ROWS) as it:
                for r in range(ROWS):
                    s = it * ROWS + r
                    sp.wait_ge(rowT_done, s - (ROWS - 1))
                    sp.wait_ge(dest_copied, s - (ROWS - 1))
                    load_rows(s, r)
            for s in range(SLOTS // ROWS * ROWS, SLOTS):
                sp.wait_ge(rowT_done, s - (ROWS - 1))
                sp.wait_ge(dest_copied, s - (ROWS - 1))
                load_rows(s, s % ROWS)
            for r in range(ROWS):
                sp.wait_ge(y_sent[r], 16 * ((SLOTS - r + ROWS - 1) // ROWS))
            for n, size in enumerate(CHUNKS):
                first = sum(CHUNKS[:n])
                for k in range(TOPK):
                    sp.dma_start(y_all[k][:, first:first + size, :],
                                 y_dram[k * TOK:(k + 1) * TOK, :].rearrange("(g p) c -> p g c", p=P)[:, first:first + size, :])\
                        .then_inc(y_loaded[n], 16)
            for n, size in enumerate(CHUNKS):
                first = sum(CHUNKS[:n])
                sp.wait_ge(out_ready, first + size)
                for q in range(GB):
                    sp.dma_start(out.rearrange("l (q g) c -> q l g c", q=GB)[q][:, first:first + size, :],
                                 x2_all[NL * q:NL * q + NL, first:first + size, :]).then_inc(written, 16)
            sp.wait_ge(written, 16 * len(CHUNKS) * GB)

        @block.gpsimd
        def _(pool):
            pool.memset(ident[:, :], 0.0).then_inc(const_step, 1)
            pool.memset(m_half[:, :], -0.5).then_inc(const_step, 1)
            pool.memset(ones[:, :], 1.0).then_inc(const_step, 1)
            pool.memset(eps[:, :], LN_EPS).then_inc(const_step, 1)
            pool.wait_ge(const_step, 4)
            pool.affine_select(out=ident[:, :], in_=ident[:, :], compare_op=ALU.not_equal, fill=1.0, base=0,
                               pattern=[[-1, P]], channel_multiplier=1).then_inc(const_step, 1)
            pool.memset(blank[:, 0:D], 0.0).then_inc(blank_ready, 1)
            pool.iota(blank[:, D:ROW].bitcast(i32), pattern=[[0, 1]], base=NOWHERE, channel_multiplier=0)\
                .then_inc(blank_ready, 1)
            pool.memset(w_pick[:, :, :], 0.0).then_inc(zeroed, 1)
            pool.memset(w_rep[:, :, :, :], 0.0).then_inc(zeroed, 1)
            pool.memset(k_mask[:, :], Q_SCALE).then_inc(zeroed, 1)
            pool.memset(v_mask[:, :], 1.0).then_inc(zeroed, 1)
            pool.memset(below[:, :], 1.0).then_inc(zeroed, 1)
            pool.memset(router_T[:, :, :], 0.0).then_inc(zeroed, 1)
            pool.wait_ge(zeroed, 6)
            pool.affine_select(out=k_mask[:, :], in_=k_mask[:, :], compare_op=ALU.is_ge, fill=0.0, base=0,
                               pattern=[[-HD, HEADS]], channel_multiplier=1).then_inc(masks_ready, 1)
            pool.affine_select(out=below[:, :], in_=below[:, :], compare_op=ALU.is_ge, fill=0.0, base=-1,
                               pattern=[[1, P]], channel_multiplier=-1).then_inc(masks_ready, 1)
            for h, n in GROUPS:
                pool.affine_select(out=v_mask[:, h:h + n], in_=v_mask[:, h:h + n], compare_op=ALU.is_ge, fill=0.0, base=0,
                                   pattern=[[-NP, n]], channel_multiplier=1).then_inc(masks_ready, 1)
            pool.wait_ge(masks_ready, 5)
            pool.affine_select(out=k_mask[:, :], in_=k_mask[:, :], compare_op=ALU.is_ge, fill=0.0, base=HD - 1,
                               pattern=[[HD, HEADS]], channel_multiplier=-1).then_inc(masks_ready, 1)
            for h, n in GROUPS:
                pool.affine_select(out=v_mask[:, h:h + n], in_=v_mask[:, h:h + n], compare_op=ALU.is_ge, fill=0.0,
                                   base=NP - 1, pattern=[[NP, n]], channel_multiplier=-1).then_inc(masks_ready, 1)
            pool.iota(lane[:, :], pattern=[[1, NE]], base=0, channel_multiplier=0,
                      allow_small_or_imprecise_dtypes=True).then_inc(masks_ready, 1)
            pool.iota(tile_no[:, :], pattern=[[1, SLOTS + 1]], base=0, channel_multiplier=0,
                      allow_small_or_imprecise_dtypes=True).then_inc(masks_ready, 1)
            for n in range(4):
                part = slice(4 * n, 4 * n + 4)
                pool.wait_ge(x_mv_ready, 4 * n + 4)
                pool.tensor_scalar(x_var[:, part], x_mv[:, part, 1], LN_EPS, None, ALU.add).then_inc(x_var_ready, 1)
                pool.wait_ge(x_var_ready, n + 1)
                pool.tensor_tensor(x_rstd[:, part], x_var[:, part], m_half[:, part], ALU.pow).then_inc(x_rstd_ready, 1)

            def take_q(i):
                pool.wait_ge(qT_copied, 8)
                pool.tensor_copy(q_now[:, :, :], qT_all[:, :, bass.ds(i * P, P)]).then_inc(q_now_ready, 1)

            def deviation(k, n):
                pool.wait_ge(mv_ready, 2 * k + (n + 1))
                pool.tensor_tensor(var[:, n:n + 1], mv[:, n, 1:2], eps[:, :], ALU.add).then_inc(var_ready, 1)
                pool.wait_ge(var_ready, 2 * k + (n + 1))
                pool.tensor_tensor(rstd[:, n:n + 1], var[:, n:n + 1], m_half[:, 0:1], ALU.pow).then_inc(rstd_ready, 1)

            take_q(0)
            pool.wait_ge(rest_loaded, 112)
            pool.wait_ge(xnT_done, 4)
            pool.wait_ge(shift_ready, PAIRS)
            pool.tensor_tensor(xn_all[:, :, :], xn_all[:, :, :],
                               bv_b[:, :].unsqueeze(1).broadcast_to([P, PAIRS, D]), ALU.add).then_inc(xnb_ready, 1)
            pool.tensor_tensor(x_all[:, :, :], x_all[:, :, :],
                               beta_b[:, :].unsqueeze(1).broadcast_to([P, PAIRS, D]), ALU.add).then_inc(xnb_ready, 1)
            for i in (1, 2):
                pool.wait_ge(scores_done, i * KB)
                take_q(i)
            deviation(0, 0)
            with pool.Fori(3, PAIRS) as i:
                pool.wait_ge(scores_done, i * KB)
                take_q(i)
                deviation(i - 3, 1)
                deviation(i - 2, 0)
            deviation(PAIRS - 3, 1)
            deviation(PAIRS - 2, 0)
            deviation(PAIRS - 2, 1)
            deviation(PAIRS - 1, 0)
            deviation(PAIRS - 1, 1)

            def keys_by_head(g):
                pool.wait_ge(k2_copied, g + 1)
                pool.tensor_tensor(k_blk, k_T.unsqueeze(2).broadcast_to([P, GB, HEADS, NP]),
                                   k_mask[:, :].unsqueeze(1).unsqueeze(3).broadcast_to([P, GB, HEADS, NP]),
                                   ALU.mult).then_inc(k_blk_ready, 1)

            def deviation2(k):
                pool.wait_ge(mv2_ready, k + 1)
                pool.tensor_tensor(var[:, 0:1], mv[:, 0, 1:2], eps[:, :], ALU.add).then_inc(var2_ready, 1)
                pool.wait_ge(var2_ready, k + 1)
                pool.tensor_tensor(rstd[:, 0:1], var[:, 0:1], m_half[:, 0:1], ALU.pow).then_inc(rstd2_ready, 1)

            def copy_rows(k):
                pool.wait_ge(n2_ready, k + 1)
                pool.tensor_copy(n2_second[:, bass.ds(k, 1), 0:D].squeeze(1), n2_now).then_inc(n2b_ready, 1)

            def with_bias(g):
                pool.wait_ge(xnT2_done, g + 1)
                pool.tensor_tensor(x1_all[:, bass.ds(g, 1), :].squeeze(1), x1_all[:, bass.ds(g, 1), :].squeeze(1),
                                   bout_b[:, :], ALU.add).then_inc(x1b_ready, 1)

            def turn(i, ahead=True, back3=True, back4=True):
                if ahead:
                    with_bias(i)
                if back4:
                    copy_rows(i - 4)
                if ahead:
                    keys_by_head(i)
                if back3:
                    deviation2(i - 3)

            for k in range(TOPK):
                pool.iota(n2[k][:, :, D].bitcast(i32), pattern=[[P, NG]], base=k * TOK, channel_multiplier=1)\
                    .then_inc(dest_ready, 1)
            pool.memset(cum_a[:, 0:NE], 0.0).then_inc(dest_ready, 1)
            pool.memset(cum_b[:, 0:NE], 0.0).then_inc(dest_ready, 1)
            for i in range(4):
                turn(i, back3=i >= 3, back4=False)
            with pool.Fori(4, NG) as i:
                turn(i)
            for i in range(NG, NG + 4):
                turn(i, ahead=False, back3=i < NG + 3)
            pool.wait_ge(x2_ready, NG)
            pool.memset(count_a[:, 0:NK, :], 0.0).then_inc(dest_ready, 1)
            pool.memset(count_b[:, 0:NK, :], 0.0).then_inc(dest_ready, 1)

            pool.wait_ge(blanked, 16 * (NG - KV_RING + 1))
            pool.wait_ge(place_ready, 1)
            pool.wait_ge(n2a_ready, NG)
            pool.wait_ge(n2b_ready, NG)
            pool.wait_ge(dest_ready, TOPK)
            for g in range(NG):
                for k in range(TOPK):
                    c = g * TOPK + k
                    pool.indirect_dma_start(rows_dram, bass.IndirectOffsetOnAxis(ap=place_i[:, c:c + 1], axis=0),
                                            n2[k][:, g, :], None).then_inc(scattered, 16)

            def send(s, r):
                pool.wait_ge(y_ready, s + 1)
                pool.indirect_dma_start(y_dram, bass.IndirectOffsetOnAxis(ap=dest[:, s:s + 1], axis=0), y_sb[:, r, :], None,
                                        bounds_check=TOPK * TOK - 1, oob_is_err=False).then_inc(y_sent[r], 16)

            for n in range(SLOTS):
                send(n, n % ROWS)

        @block.scalar
        def _(act):
            act.dma_start(bq_col[:, :], t["L0_xattn_bq"].rearrange("(k p) -> p k", p=P),
                          allow_slow_non_contiguous=True).then_inc(qkb_loaded, 16)
            act.dma_start(bk_col[:, :], t["L0_xattn_bk"].rearrange("(k p) -> p k", p=P),
                          allow_slow_non_contiguous=True).then_inc(qkb_loaded, 16)
            act.wait_ge(wT_done, 1)
            act.copy(wqT[:, :, :].rearrange("p a b -> p (a b)"), bank[0][:, :]).then_inc(wT_copied, 1)
            act.wait_ge(wT_done, 2)
            act.copy(wkT[:, :, :].rearrange("p a b -> p (a b)"), bank[1][:, :]).then_inc(wT_copied, 1)
            act.dma_start(wv[:, :, :], t["L0_xattn_Wv"].rearrange("(k p) f -> p k f", p=P)).then_inc(rest_loaded, 16)
            for to, of in ((bv_b, "L0_xattn_bv"), (gamma_b, "L0_xattn_gamma"), (beta_b, "L0_xattn_beta")):
                act.dma_start(to[:, :], t[of].partition_broadcast(P)).then_inc(rest_loaded, 16)
            act.dma_start(bq2_col[:, :], t["L0_attn_b_q"].rearrange("(p a) -> p a", a=1)).then_inc(rest_loaded, 16)
            act.dma_start(bout_b[:, :], t["L0_attn_b_out"].partition_broadcast(P)).then_inc(rest_loaded, 16)
            act.dma_start(rbias_b[:, :], t["L0_ffn_router_bias"].partition_broadcast(P)).then_inc(rest_loaded, 16)
            act.wait_ge(wqk_done, 1)
            act.copy(wqk[:, :, :].rearrange("p a b -> p (a b)"), bank[2][:, :]).then_inc(wqk_copied, 1)
            act.wait_ge(wqk_done, 2)
            act.copy(bqk_col[:, :], bank[3][:, 300:300 + DH]).then_inc(wqk_copied, 1)
            act.copy(bk_row[:, :], bank[3][:, 0:D + 1]).then_inc(bk_row_copied, 1)
            act.wait_ge(wqk_copied, 2)
            for n in range(5):
                if n < 4:
                    for dh in range(DH):
                        act.wait_ge(xnT_done, n + 1)
                        act.copy(xnT[:, n % 2, dh, :], T[dh][:, :]).then_inc(xnT_copied, 1)
                if n == 4:
                    for m, to in enumerate((w_outT, sh_gateT, sh_upT, sh_downT)):
                        act.wait_ge(prep_done, m + 1)
                        act.copy(to[:, :, :].rearrange("p a b -> p (a b)"), bank[m][:, :]).then_inc(prep_copied, 1)
                if n >= 1:
                    for dc in range(DH):
                        act.wait_ge(qT_done, 2 * (n - 1) + dc + 1)
                        act.activation(qT_all[:, dc, 512 * (n - 1):512 * n], bank[6 + dc][:, :], ACT.Identity,
                                       bias=bqk_col[:, dc:dc + 1]).then_inc(qT_copied, 1)

            def copy_out(i, use):
                act.wait_ge(*done_of(use, i))
                act.copy(*copy_of(use)).then_inc(count_of(use, i)[0], 1)

            def exps(i, kb):
                if kb == 0:
                    act.wait_ge(negmax_ready, i + 1)
                act.activation(prob[:, 512 * kb:512 * kb + KW[kb]], S[kb][:, 0:KW[kb]], ACT.Exp, bias=negmax[:, 0:1],
                               accum_out=sums[:, kb:kb + 1]).then_inc(exp_done, 1)

            def UT_evac(i):
                act.wait_ge(UT_done, i + 1)
                act.copy(UT[:, :, :].rearrange("p a b -> p (a b)"), M[:, 0:D]).then_inc(UT_copied, 1)

            def turn(i, ahead=True, back1=True, back2=True):
                for use in range(0, len(USES), 2):
                    if ahead if USES[use][0] == "T" else back1:
                        copy_out(i, use)
                    if back1 and 1 <= use // 2 <= KB:
                        exps(i - 1, use // 2 - 1)
                    if back2 and use == 10:
                        UT_evac(i - 2)

            turn(0, back1=False, back2=False)
            turn(1, back2=False)
            with act.Fori(2, PAIRS) as i:
                turn(i)
            turn(PAIRS, ahead=False)
            turn(PAIRS + 1, ahead=False, back1=False)

            def turn(i, p, ahead=True, back1=True, back2=True, back3=True, back4=True):
                if ahead:
                    act.wait_ge(xnT2_done, i + 1)
                    act.copy(x_nT.rearrange("p a b -> p (a b)"), bank[0][:, 0:D]).then_inc(xnT2_copied, 1)
                if back2:
                    act.wait_ge(attnT_done, i - 1)
                    act.copy(attnT[0:HG * NP].rearrange("p a b -> p (a b)"), bank[6][0:HG * NP, 0:len(GROUPS) * P])\
                        .then_inc(attnT_copied, 1)
                if ahead:
                    act.wait_ge(q2_done, i + 1)
                    act.activation(q_T[:, p, :], bank[0][:, D:D + P], ACT.Identity, bias=bq2_col[:, 0:1]).then_inc(q2_copied, 1)
                if back3:
                    act.wait_ge(oT_done, i - 2)
                    act.copy(oT.rearrange("p a b -> p (a b)"), bank[4][:, 0:D]).then_inc(oT_copied, 1)
                if back1:
                    act.wait_ge(shifted_ready, i)
                    act.activation(attn, attn, ACT.Exp).then_inc(exp2_done, 1)
                if ahead:
                    act.wait_ge(qN_done, i + 1)
                    act.copy(q_nat.rearrange("p (h d) -> p h d", h=HEADS),
                             bank[1][:, 0:QD].rearrange("p (d h) -> p h d", h=HEADS)).then_inc(qN_copied, 1)
                if back4:
                    act.wait_ge(n2T_done, i - 3)
                    for dh in range(DH):
                        act.copy(n2T[dh][:, bass.ds((i - 4) * P, P)], bank[6][:, dh * P:dh * P + P]).then_inc(n2T_copied, 1)
                    act.copy(n2_first[:, bass.ds(i - 4, 1), 0:D].squeeze(1), n2_now).then_inc(n2a_ready, 1)

            act.wait_ge(rest_loaded, 112)
            for i in range(4):
                turn(i, i % 2, True, i >= 1, i >= 2, i >= 3, False)
            with act.Fori(2, NG // 2) as it:
                for p in range(2):
                    turn(it * 2 + p, p)
            for i in range(NG, NG + 4):
                turn(i, i % 2, False, i < NG + 1, i < NG + 2, i < NG + 3)

            act.wait_ge(logitsT_done, 1)
            act.copy(logitsT, bank[0][:, :]).then_inc(logitsT_copied, 1)
            act.wait_ge(gap_ready, 1)
            act.activation(gap_e[:, :], gap_w[:, :], ACT.Exp).then_inc(gap_exp, 1)
            for q in range(4):
                for hc in range(DH):
                    act.wait_ge(shared_up_done, 2 * DH * q + hc + 1)
                    if q >= 1:
                        act.wait_ge(shared_hid_ready, DH * (q - 1) + hc + 1)
                    act.activation(sh_silu[:, hc, :], bank[1 + hc][:, :], ACT.Silu).then_inc(shared_silu, 1)

            def turn(s, p, ahead=True, back1=True):
                if ahead:
                    act.wait_ge(rowT_done, s + 1)
                    act.copy(rowT[:, p].rearrange("p a b -> p (a b)"), bank[p][:, 0:D]).then_inc(rowT_copied, 1)
                if back1:
                    act.wait_ge(gu_done, s)
                    act.activation(silu_g[:, 1 - p, :], bank[3 - p][:, 0:HID], ACT.Silu).then_inc(silu_done, 1)

            def hidden_out(k, p):
                act.wait_ge(hidT_done, k + 1)
                act.copy(hidT[:, p, :], bank[4 + p][:, 0:P]).then_inc(hidT_copied, 1)

            turn(0, 0, back1=False)
            turn(1, 1)
            with act.Fori(1, SLOTS // 2) as it:
                for p in range(2):
                    turn(it * 2 + p, p)
                    hidden_out(it * 2 + (p - 2), p)
            for s in range(SLOTS // 2 * 2, SLOTS + 2):
                turn(s, s % 2, s < SLOTS, s < SLOTS + 1)
                hidden_out(s - 2, s % 2)

        @block.tensor
        def _(pe):
            pe.wait_ge(const_step, 5)
            pe.wait_ge(qk_loaded, 32)
            for of, to in ((wq, 0), (wk, 1)):
                for kd in range(DH):
                    for fc in range(DH):
                        last = pe.transpose(bank[to][:, fc * D + kd * P:fc * D + kd * P + P],
                                            of[:, kd, fc * P:fc * P + P], ident[:, :])
                last.then_inc(wT_done, 1)
            pe.wait_ge(wT_copied, 2)
            for kd in range(DH):
                for fc in range(DH):
                    last = pe.matmul(bank[2][:, kd * D:kd * D + D], wqT[:, fc, kd * P:kd * P + P], wkT[:, fc, :],
                                     start=fc == 0, stop=fc == DH - 1)
            last.then_inc(wqk_done, 1)
            pe.wait_ge(qkb_loaded, 32)
            for dc in range(DH):
                for fc in range(DH):
                    pe.matmul(bank[3][:, 300 + dc:301 + dc], wkT[:, fc, dc * P:dc * P + P], bq_col[:, fc:fc + 1],
                              start=fc == 0, stop=fc == DH - 1)
            pe.wait_ge(bk_rep_ready, 1)
            for fc in range(DH):
                pe.matmul(bank[3][:, 0:D], bk_rep[:, fc, :], wqT[:, fc, :], start=fc == 0, stop=fc == DH - 1)
            for fc in range(DH):
                last = pe.matmul(bank[3][:, D:D + 1], bk_rep[:, fc, :], bq_col[:, fc:fc + 1],
                                 start=fc == 0, stop=fc == DH - 1)
            last.then_inc(wqk_done, 1)
            def queries_turned(n):
                pe.wait_ge(xn_ready, 4 * n + 4)
                if n >= 1:
                    pe.wait_ge(xnT_copied, 2 * n)
                for dh in range(DH):
                    for a in range(4):
                        last = pe.transpose(T[dh][:, a * P:a * P + P], xn_all[:, 4 * n + a, dh * P:dh * P + P], ident[:, :])
                last.then_inc(xnT_done, 1)

            def queries_projected(n):
                pe.wait_ge(xnT_copied, 2 * n + 2)
                if n >= 1:
                    pe.wait_ge(qT_copied, 2 * n)
                for dc in range(DH):
                    for k in range(DH):
                        last = pe.matmul(bank[6 + dc][:, :], wqk[:, k, dc * P:dc * P + P], xnT[:, n % 2, k, :],
                                         start=k == 0, stop=k == DH - 1)
                    last.then_inc(qT_done, 1)

            pe.wait_ge(wqk_copied, 2)
            for n in range(5):
                if n < 4:
                    queries_turned(n)
                else:
                    pe.wait_ge(prep_loaded, 16 * (GB + 6))
                    pe.wait_ge(bk_row_copied, 1)
                    for m, of in enumerate((w_out, sh_gate, sh_up, sh_down)):
                        for kd in range(DH):
                            for fc in range(DH):
                                last = pe.transpose(bank[m][:, fc * D + kd * P:fc * D + kd * P + P],
                                                    of[:, kd, fc * P:fc * P + P], ident[:, :])
                        last.then_inc(prep_done, 1)
                if n >= 1:
                    queries_projected(n - 1)
            pe.wait_ge(qT_copied, 8)
            for k in range(DH):
                pe.transpose(M[:, k * QD:k * QD + QD], w_q[:, k * P:k * P + P], ident[:, :])
                pe.transpose(M[:, 256 + k * NE:256 + k * NE + NE], router_w[:, k * P:k * P + P], ident[0:NE, 0:NE])
            pe.transpose(M[:, 300:300 + NP], w_kv4, ident[0:NP, 0:NP]).then_inc(prep_done, 1)
            pe.wait_ge(prep_copied, 4)

            def fill(i, r, use):
                (kind, n), to = USES[use], T[use % 2]
                if kind == "P":
                    pe.wait_ge(exp_done, (i - 1) * KB + (n + 1))
                    for a in range(4 if n < KB - 1 else 1):
                        k = 4 * n + a
                        rows = P if k < KT else TAIL
                        last = pe.transpose(to[0:rows, a * P:a * P + P], prob[:, k * P:k * P + rows], ident[:, :])
                    last.then_inc(probT_done, 1)
                    return
                kb, b, dh = TGROUPS[n]
                if dh is None:
                    for d in range(DH):
                        last = pe.transpose(to[:, d * P:d * P + TAIL], ring[0:TAIL, r, b, KT, d * P:d * P + P],
                                            ident[0:TAIL, 0:TAIL])
                else:
                    for a in range(4):
                        last = pe.transpose(to[:, a * P:a * P + P], ring[:, r, b, 4 * kb + a, dh * P:dh * P + P], ident[:, :])
                last.then_inc(t_done, 1)

            def scores(i, kb, dh):
                if dh == 0:
                    uses = [m for m, (kind, n) in enumerate(USES) if kind == "T" and TGROUPS[n][0] == kb]
                    for m in uses[-2:]:
                        pe.wait_ge(*count_of(m, i))
                    if kb == 0:
                        pe.wait_ge(q_now_ready, i + 1)
                for b in range(2):
                    last = pe.matmul(S[kb][64 * b:64 * b + 64, 0:KW[kb]], q_now[:, dh, 64 * b:64 * b + 64],
                                     ctxT[:, b, dh, 512 * kb:512 * kb + KW[kb]], start=dh == 0, stop=dh == DH - 1)
                if dh == DH - 1:
                    last.then_inc(scores_done, 1)

            def weigh(i, r, k):
                rows = P if k < KT else TAIL
                if k % 4 == 0:
                    pe.wait_ge(*count_of(USES.index(("P", k // 4)), i + 1))
                for b in range(2):
                    last = pe.matmul(U[64 * b:64 * b + 64, 0:D], probT[0:rows, k, 64 * b:64 * b + 64],
                                     ring[0:rows, r, b, k, :], start=k == 0, stop=k == KT)
                if k == KT:
                    last.then_inc(pv_done, 1)

            def flip(i):
                pe.wait_ge(Un_ready, i + 1)
                for dh in range(DH):
                    last = pe.transpose(M[:, dh * P:dh * P + P], Un[:, dh * P:dh * P + P], ident[:, :])
                last.then_inc(UT_done, 1)

            def project(i):
                pe.wait_ge(UT_copied, i + 1)
                for k in range(DH):
                    last = pe.matmul(M[:, D:2 * D], UT[:, k, :], wv[:, k, :], start=k == 0, stop=k == DH - 1)
                last.then_inc(res_done, 1)

            AFTER = {m: [("weigh2", PV_LATE + m)] for m in range(5)}
            AFTER[5] = [("weigh2", k) for k in range(PV_LATE + 5, KT + 1)]
            AFTER[7], AFTER[8] = [("scores", 0, 0)], [("scores", 0, 1)]
            AFTER[9] = [("flip",)]
            AFTER[10], AFTER[11] = [("weigh1", 0), ("weigh1", 1)], [("scores", 1, 0)]
            AFTER[12], AFTER[13] = [("scores", 1, 1), ("project",)], [("weigh1", 2)]
            AFTER[14], AFTER[15], AFTER[16] = [("weigh1", 3)], [("scores", 2, 0)], [("scores", 2, 1)]
            AFTER[17] = [("scores", 3, 0), ("scores", 3, 1)] + [("weigh1", k) for k in range(4, PV_LATE)]

            def turn(i, r, round_, ahead=True, back1=True, back2=True, before="all"):
                def there(use, ahead, back1):
                    return ahead if USES[use][0] == "T" else back1

                was = {"all": (True, True), "first": (True, False), "last": (False, True), "none": (False, False)}[before]
                if ahead:
                    pe.wait_ge(ctx_loaded[r], round_ * 32 + 32)
                for use in range(len(USES)):
                    if there(use, ahead, back1):
                        earlier = [(m, i) for m in range(use - 2, -1, -2) if there(m, ahead, back1)] \
                            + [(m, i - 1) for m in range(len(USES) - 2 + use % 2, -1, -2) if there(m, *was)]
                        if earlier:
                            pe.wait_ge(*count_of(*earlier[0]))
                        fill(i, r, use)
                    for what, *args in AFTER.get(use, ()):
                        if what == "scores" and ahead:
                            scores(i, *args)
                        elif what == "weigh1" and back1:
                            if args[0] == 0 and back2:
                                pe.wait_ge(Un_ready, i - 1)
                            weigh(i - 1, (r - 1) % RING, *args)
                        elif what == "weigh2" and back2:
                            weigh(i - 2, (r - 2) % RING, *args)
                        elif what == "flip" and back2:
                            flip(i - 2)
                        elif what == "project" and back2:
                            project(i - 2)

            turn(0, 0, 0, back1=False, back2=False, before="none")
            pe.wait_ge(rest_loaded, 112)
            turn(1, 1, 0, back2=False, before="first")
            pe.wait_ge(smalls_ready, 2 * GB + 2)
            turn(2, 2, 0)
            with pe.Fori(0, (PAIRS - RING) // RING) as it:
                for u in range(RING):
                    turn(it * RING + (RING + u), u, it + 1)
            turn(PAIRS - 1, (PAIRS - 1) % RING, (PAIRS - 1) // RING)
            turn(PAIRS, PAIRS % RING, None, ahead=False)
            turn(PAIRS + 1, (PAIRS + 1) % RING, None, ahead=False, back1=False, before="last")

            def rows_in(i, r, round_):
                pe.wait_ge(kv_loaded[r], round_ * 32 + 32)
                for dh in range(DH):
                    last = pe.transpose(bank[0][:, dh * P:dh * P + P], kv_in[:, r, dh * P:dh * P + P], ident[:, :])
                last.then_inc(xnT2_done, 1)

            def values(i, r):
                by_head = kv_in[:, r, :].rearrange("p (v h) -> p h v", h=HEADS)
                for b in range(GB):
                    last = pe.matmul(bank[2 + b // 2][0:HG * NP, (b % 2) * D:(b % 2) * D + D],
                                     w_rep[:, b, :, :].rearrange("p h n -> p (h n)"), by_head, start=True, stop=True)
                last.then_inc(vrep_done, 1)

            def queries(i):
                pe.wait_ge(xnT2_copied, i + 1)
                for k in range(DH):
                    last = pe.matmul(bank[0][:, D:D + P], w_qT[:, k, :], x_nT[:, k, :], start=k == 0, stop=k == DH - 1)
                last.then_inc(q2_done, 1)

            def query_rows(i, p):
                pe.wait_ge(q2_copied, i + 1)
                pe.transpose(bank[1][:, 0:QD], q_T[:, p, :], ident[:, :]).then_inc(qN_done, 1)

            def keys(i):
                pe.wait_ge(qN_copied, i + 1)
                pe.matmul(bank[1][:, QD:QD + GB * NP], q_nat,
                          w_pick[:, :, :].rearrange("p b n -> p (b n)"), start=True, stop=True).then_inc(k2_done, 1)

            def group_scores(k, p):
                pe.wait_ge(k_blk_ready, k + 1)
                for b in range(GB):
                    last = pe.matmul(bank[5][NL * b:NL * b + NL, 0:HEADS * NP], q_T[:, p, NL * b:NL * b + NL],
                                     k_blk[:, b].rearrange("p h n -> p (h n)"), start=True, stop=True)
                last.then_inc(s2_done, 1)

            def attn_turned(k):
                pe.wait_ge(exp2_done, k + 1)
                flat = attn.rearrange("p h n -> p (h n)")
                for j, (h, n) in enumerate(GROUPS):
                    last = pe.transpose(bank[6][0:n * NP, j * P:j * P + P], flat[:, h * NP:(h + n) * NP], ident[:, :])
                last.then_inc(attnT_done, 1)

            def weighted(k, p):
                pe.wait_ge(attnT_copied, k + 1)
                pe.wait_ge(v_blk_ready, k * 2 + 2)
                for b in range(GB):
                    for j, (h, n) in enumerate(GROUPS):
                        last = pe.matmul(bank[7][NL * b:NL * b + NL, h * DV:(h + n) * DV], attnT[0:n * NP, j, NL * b:NL * b + NL],
                                         v_blk[p][0:n * NP, b, h:h + n, :].rearrange("p h v -> p (h v)"), start=True, stop=True)
                last.then_inc(pv2_done, 1)

            def out_turned(k):
                pe.wait_ge(o_copied, k + 1)
                for dh in range(DH):
                    last = pe.transpose(bank[4][:, dh * P:dh * P + P], o_sb[:, dh * P:dh * P + P], ident[:, :])
                last.then_inc(oT_done, 1)

            def out_product(k):
                pe.wait_ge(oT_copied, k + 1)
                for j in range(DH):
                    last = pe.matmul(bank[4][:, D:2 * D], oT[:, j, :], w_outT[:, j, :], start=j == 0, stop=j == DH - 1)
                last.then_inc(proj_done, 1)

            def normed_turned(k):
                pe.wait_ge(n2_ready, k + 1)
                for dh in range(DH):
                    last = pe.transpose(bank[6][:, dh * P:dh * P + P], n2_now[:, dh * P:dh * P + P], ident[:, :])
                last.then_inc(n2T_done, 1)

            def turn(i, r, round_, first=False, ahead=True, back1=True, back2=True, back3=True, back4=True, back5=True):
                p = r % 2
                if ahead:
                    if not first:
                        pe.wait_ge(q2_copied, i)
                    rows_in(i, r, round_)
                if back2:
                    if back5:
                        pe.wait_ge(n2T_copied, i * 2 - 8)
                    attn_turned(i - 2)
                if ahead:
                    if not first:
                        pe.wait_ge(v_blk_ready, i * 2)
                    values(i, r)
                    queries(i)
                if back1:
                    if back2:
                        pe.wait_ge(shifted_ready, i - 1)
                    group_scores(i - 1, 1 - p)
                if back3:
                    if back4:
                        pe.wait_ge(x2_ready, i - 3)
                    out_turned(i - 3)
                if back2:
                    if back3:
                        pe.wait_ge(o_copied, i - 2)
                    weighted(i - 2, p)
                if ahead:
                    if not first:
                        pe.wait_ge(k2_copied, i)
                    query_rows(i, p)
                if back4:
                    if back5:
                        pe.wait_ge(n2T_copied, i * 2 - 8)
                    normed_turned(i - 4)
                if back3:
                    out_product(i - 3)
                if ahead:
                    keys(i)

            pe.wait_ge(res_ready, PAIRS)
            for i in range(KV_RING):
                turn(i, i, 0, i == 0, True, i >= 1, i >= 2, i >= 3, False, False)
            turn(KV_RING, 0, 1, back5=False)
            for i in range(KV_RING + 1, 2 * KV_RING):
                turn(i, i % KV_RING, 1)
            with pe.Fori(2, NG // KV_RING) as it:
                for r in range(KV_RING):
                    turn(it * KV_RING + r, r, it)
            for i in range(NG, NG + 4):
                turn(i, i % KV_RING, None, False, False, i < NG + 1, i < NG + 2, i < NG + 3)

            pe.wait_ge(n2T_copied, DH * NG)
            for k in range(DH):
                for n in range(4):
                    last = pe.matmul(bank[0][NL * n:NL * n + NL, :], router_T[:, k, :], n2T[k][:, 512 * n:512 * n + 512],
                                     start=k == 0, stop=k == DH - 1)
            last.then_inc(logitsT_done, 1)

            def router_turned():
                pe.wait_ge(logitsT_copied, 1)
                for a in range(4):
                    last = pe.transpose(bank[7][:, a * P:a * P + P], logitsT[:, a * P:a * P + P], ident[:, :])
                last.then_inc(logits_done, 1)

            def shared_up(q):
                for a, w in enumerate((sh_gateT, sh_upT)):
                    for hc in range(DH):
                        if q == 0 and a == 0 and hc == 1:
                            router_turned()
                        if q >= 1:
                            pe.wait_ge(shared_hid_ready if a else shared_silu, DH * (q - 1) + hc + 1)
                        for k in range(DH):
                            last = pe.matmul(bank[1 + DH * a + hc][:, :], w[:, k, hc * P:hc * P + P],
                                             n2T[k][:, 512 * q:512 * q + 512], start=k == 0, stop=k == DH - 1)
                        last.then_inc(shared_up_done, 1)

            def shared_down(q):
                pe.wait_ge(shared_hid_ready, DH * q + DH)
                for a in range(4):
                    m = 4 * q + a
                    if m >= 2:
                        pe.wait_ge(shared_added, m - 1)
                    for hc in range(DH):
                        last = pe.matmul(bank[5 + m % 2][:, 0:D], sh_hid[:, q % 2, hc, a * P:a * P + P], sh_downT[:, hc, :],
                                         start=hc == 0, stop=hc == DH - 1)
                    last.then_inc(shared_done, 1)

            shared_up(0)
            pe.wait_ge(chosen_ready, 1)
            flat = chosen.rearrange("p c e -> p (c e)")
            pe.matmul(bank[7][:, :], below[:, :], flat, start=True, stop=True)
            pe.matmul(bank[0][:, :], ones[:, :], flat, start=True, stop=True).then_inc(before_done, 1)
            for q in range(1, 4):
                shared_up(q)
                shared_down(q - 1)
            shared_down(3)

            expert_regs = [[pe.alloc_register(f"expert_{of}{r}") for r in range(ROWS)] for of in ("up", "back")]

            def experts_of(round_):
                got = []
                for regs, of in zip(expert_regs, (expert_up, expert_back)):
                    pe.load(regs, of[0:1, bass.ds(round_ * ROWS, ROWS)])
                    got.append([pe.snap(reg, min_val=0, max_val=NE - 1) for reg in regs])
                return got

            def expert_of(of, s):
                at = s + (1 if of is expert_up else 3)
                return pe.value_load(of[0:1, at:at + 1], min_val=0, max_val=NE - 1)

            def rows_T(s, r, round_):
                pe.wait_ge(row_loaded[r], round_ * 16 + 16)
                for dh in range(DH):
                    last = pe.transpose(bank[r % 2][:, dh * P:dh * P + P], row_in[:, r, dh * P:dh * P + P], ident[:, :])
                last.then_inc(rowT_done, 1)

            def gate_up(s, p, e):
                pe.wait_ge(rowT_copied, s + 1)
                for k in range(DH):
                    last = pe.matmul(bank[2 + p][:, 0:2 * HID], rowT[:, p, k, :], w_gu[:, bass.ds(e, 1), k, :].squeeze(1),
                                     start=k == 0, stop=k == DH - 1)
                last.then_inc(gu_done, 1)

            def hidden_T(s, p):
                pe.wait_ge(hid_ready, s + 1)
                pe.transpose(bank[4 + p][:, 0:P], hid[:, p, :], ident[:, :]).then_inc(hidT_done, 1)

            def back(s, p, e, first=False):
                pe.wait_ge(hidT_copied, s + 1)
                if not first:
                    pe.wait_ge(y_ready, s - 1)
                pe.matmul(bank[6 + p][:, 0:D], hidT[:, p, :], w_down[:, bass.ds(e, 1), :].squeeze(1), start=True, stop=True)\
                    .then_inc(down_done, 1)

            def turn(s, r, round_, ahead=True, back1=True, back2=True, back3=True, back5=True, experts=None):
                p = r % 2
                if ahead:
                    rows_T(s, r, round_)
                if back1:
                    gate_up(s - 1, 1 - p, experts[0][r] if experts else expert_of(expert_up, s - 1))
                if back3:
                    back(s - 3, 1 - p, experts[1][r] if experts else expert_of(expert_back, s - 3), first=not back5)
                if back2:
                    hidden_T(s - 2, p)

            pe.wait_ge(expert_step, 5)
            pe.wait_ge(experts_loaded, 16 * 3 * NE)
            pe.wait_ge(shared_added, NG)
            pe.wait_ge(place_ready, 1)
            for s in range(ROWS):
                turn(s, s, 0, True, s >= 1, s >= 2, s >= 3, False)
            turn(ROWS, 0, 1, back5=False)
            for s in range(ROWS + 1, 2 * ROWS):
                turn(s, s % ROWS, 1)
            with pe.Fori(2, SLOTS // ROWS) as it:
                experts = experts_of(it)
                for r in range(ROWS):
                    turn(it * ROWS + r, r, it, experts=experts)
            for s in range(SLOTS // ROWS * ROWS, SLOTS + 3):
                turn(s, s % ROWS, s // ROWS, s < SLOTS, s < SLOTS + 1, s < SLOTS + 2)

        @block.vector
        def _(dve):
            def x_statistics(n):
                dve.wait_ge(x_loaded[n], 16)
                for a in range(4 * n, 4 * n + 4):
                    dve.bn_stats(x_stats[:, a, :], x_all[:, a, :]).then_inc(x_stat_ready, 1)
                for a in range(4 * n, 4 * n + 4):
                    dve.wait_ge(x_stat_ready, a + 1)
                    dve.bn_aggr(x_mv[:, a, :], x_stats[:, a, :]).then_inc(x_mv_ready, 1)

            def x_normed(n):
                dve.wait_ge(x_rstd_ready, n + 1)
                for a in range(4 * n, 4 * n + 4):
                    dve.tensor_scalar(xn_all[:, a, :], x_all[:, a, :], x_mv[:, a, 0:1], x_rstd[:, a:a + 1],
                                      ALU.subtract, ALU.mult).then_inc(xn_ready, 1)

            def small_operands():
                dve.wait_ge(prep_done, 5)
                dve.wait_ge(zeroed, 6)
                for b in range(GB):
                    mine = slice(NL * b, NL * b + NL)
                    dve.tensor_copy(w_pick[mine, b, :], M[mine, 300:300 + NP]).then_inc(smalls_ready, 1)
                    dve.tensor_copy(w_rep[mine, b, :, :], M[mine, 300:300 + NP].unsqueeze(1).broadcast_to([NL, HG, NP]))\
                        .then_inc(smalls_ready, 1)
                dve.tensor_copy(w_qT[:, :, :].rearrange("p a b -> p (a b)"), M[:, 0:DH * QD]).then_inc(smalls_ready, 1)
                dve.tensor_copy(router_T[:, :, 0:NE], M[:, 256:256 + DH * NE].rearrange("p (k e) -> p k e", k=DH))\
                    .then_inc(smalls_ready, 1)

            x_statistics(0)
            dve.wait_ge(qkb_loaded, 32)
            dve.tensor_copy(bk_rep[:, :, :], bk_col[:, :].unsqueeze(2).broadcast_to([P, DH, P])).then_inc(bk_rep_ready, 1)
            for n in range(1, 4):
                x_statistics(n)
                x_normed(n - 1)
            x_normed(3)
            dve.wait_ge(bk_row_copied, 1)

            def copy_out(i, use):
                dve.wait_ge(*done_of(use, i))
                dve.tensor_copy(*copy_of(use)).then_inc(count_of(use, i)[0], 1)

            def block_max(i, kb):
                dve.wait_ge(scores_done, i * KB + (kb + 1))
                dve.tensor_reduce(blockmax[:, kb:kb + 1], S[kb][:, 0:KW[kb]], AX.X, ALU.max).then_inc(blockmax_ready, 1)

            def row_max(i):
                dve.wait_ge(blockmax_ready, i * KB + KB)
                dve.tensor_reduce(rowmax[:, :], blockmax[:, :], AX.X, ALU.max).then_inc(rowmax_ready, 1)
                dve.wait_ge(rowmax_ready, i + 1)
                dve.tensor_tensor(topped[:, :], rowmax[:, :], shift[:, bass.ds(i, 1)], ALU.add).then_inc(topped_ready, 1)
                dve.wait_ge(topped_ready, i + 1)
                dve.tensor_tensor(negmax[:, :], shift[:, bass.ds(i, 1)], topped[:, :], ALU.subtract).then_inc(negmax_ready, 1)

            def row_sum(k):
                dve.wait_ge(exp_done, k * KB + KB)
                dve.tensor_reduce(rowsum[:, :], sums[:, :], AX.X, ALU.add).then_inc(rowsum_ready, 1)
                dve.wait_ge(rowsum_ready, k + 1)
                dve.reciprocal(rinv[:, :], rowsum[:, :]).then_inc(rinv_ready, 1)

            def normalise(k):
                dve.wait_ge(pv_done, k + 1)
                dve.wait_ge(rinv_ready, k + 1)
                dve.tensor_scalar(Un[:, :], U[:, 0:D], rinv[:, 0:1], None, ALU.mult).then_inc(Un_ready, 1)

            def residual(k):
                dve.wait_ge(res_done, k + 1)
                dve.tensor_tensor(res[:, :], M[:, D:2 * D], xn_all[:, bass.ds(k, 1), :].squeeze(1), ALU.add).then_inc(res_ready, 1)
                dve.wait_ge(res_ready, k + 1)
                dve.bn_stats(stats[:, 0, :], res[:, :]).then_inc(stat_ready, 1)
                dve.wait_ge(stat_ready, 2 * k + 1)
                dve.tensor_copy(seen[:, :], stats[:, 0, 0:1])
                dve.bn_aggr(mv[:, 0, :], stats[:, 0, :]).then_inc(mv_ready, 1)
                dve.wait_ge(mv_ready, 2 * k + 1)
                dve.scalar_tensor_tensor(scaled[:, :], res[:, :], mv[:, 0, 0:1], gamma_b[:, :],
                                         ALU.subtract, ALU.mult).then_inc(scaled_ready, 1)

            def first_norm(k):
                dve.wait_ge(scaled_ready, k + 1)
                dve.wait_ge(rstd_ready, 2 * k + 1)
                dve.wait_ge(stored, k * 32 + 32)
                dve.scalar_tensor_tensor(stage[:, 0, :], scaled[:, :], rstd[:, 0:1], x_all[:, bass.ds(k, 1), :].squeeze(1),
                                         ALU.mult, ALU.add).then_inc(x1_ready, 1)
                dve.wait_ge(x1_ready, k + 1)
                dve.bn_stats(stats[:, 1, :], stage[:, 0, :]).then_inc(stat_ready, 1)
                dve.wait_ge(stat_ready, 2 * k + 2)
                dve.tensor_copy(seen[:, :], stats[:, 1, 0:1])
                dve.bn_aggr(mv[:, 1, :], stats[:, 1, :]).then_inc(mv_ready, 1)

            def second_norm(k):
                dve.wait_ge(rstd_ready, 2 * k + 2)
                dve.tensor_scalar(stage[:, 1, :], stage[:, 0, :], mv[:, 1, 0:1], rstd[:, 1:2],
                                  ALU.subtract, ALU.mult).then_inc(n1_ready, 1)

            def turn(i, ahead=True, back1=True, back2=True, back3=True):
                for use in range(1, len(USES), 2):
                    if ahead if USES[use][0] == "T" else back1:
                        copy_out(i, use)
                    if use == 3 and back3:
                        first_norm(i - 3)
                    if use == 5 and back2:
                        normalise(i - 2)
                    if use == 9:
                        if back1:
                            row_sum(i - 1)
                        if ahead:
                            block_max(i, 0)
                        if back3:
                            second_norm(i - 3)
                    if use == 13:
                        if ahead:
                            block_max(i, 1)
                        if back2:
                            residual(i - 2)
                if ahead:
                    block_max(i, 2)
                    block_max(i, 3)
                    row_max(i)

            for a in range(PAIRS):
                if a >= 1:
                    dve.wait_ge(dot_ready, a)
                dve.tensor_tensor_reduce(out=dotted[:, :], in0=xn_all[:, a, :], in1=bk_row[:, 0:D], scale=1.0,
                                         scalar=bk_row[:, D:D + 1], op0=ALU.mult, op1=ALU.add,
                                         accum_out=shift[:, a:a + 1]).then_inc(dot_ready, 1)
            dve.wait_ge(dot_ready, PAIRS)
            dve.sem_inc(shift_ready, PAIRS)
            turn(0, back1=False, back2=False, back3=False)
            small_operands()
            turn(1, back2=False, back3=False)
            dve.wait_ge(rest_loaded, 112)
            dve.wait_ge(xnb_ready, 2)
            turn(2, back3=False)
            with dve.Fori(3, PAIRS) as i:
                turn(i)
            turn(PAIRS, ahead=False)
            turn(PAIRS + 1, ahead=False, back1=False)
            turn(PAIRS + 2, ahead=False, back1=False, back2=False)

            scores_ = bank[5][:, 0:HEADS * NP].rearrange("p (h n) -> p h n", h=HEADS)
            wide = [P, HEADS, NP]

            def shifted(k):
                dve.wait_ge(s2_done, k + 1)
                dve.tensor_reduce(head_max[:, :], scores_, AX.X, ALU.max).then_inc(head_max_ready, 1)
                dve.wait_ge(head_max_ready, k + 1)
                dve.tensor_tensor(attn, scores_, head_max[:, :].unsqueeze(2).broadcast_to(wide), ALU.subtract)\
                    .then_inc(shifted_ready, 1)

            def normed(k, first=False):
                dve.wait_ge(rstd2_ready, k + 1)
                if not first:
                    dve.wait_ge(n2T_done, k)
                    dve.wait_ge(n2a_ready, k)
                    dve.wait_ge(n2b_ready, k)
                dve.tensor_scalar(n2_now, x2_all[:, bass.ds(k, 1), :].squeeze(1),
                                  mv[:, 0, 0:1], rstd[:, 0:1], ALU.subtract, ALU.mult).then_inc(n2_ready, 1)

            def head_sums(k):
                dve.wait_ge(exp2_done, k + 1)
                dve.tensor_reduce(head_sum[:, :], attn, AX.X, ALU.add).then_inc(head_sum_ready, 1)

            def head_inverse(k):
                dve.wait_ge(head_sum_ready, k + 1)
                dve.wait_ge(o_copied, k)
                dve.reciprocal(head_inv[:, :], head_sum[:, :]).then_inc(head_inv_ready, 1)

            def divided(k):
                dve.wait_ge(pv2_done, k + 1)
                dve.wait_ge(head_inv_ready, k + 1)
                dve.tensor_tensor(o_sb.rearrange("p (v h) -> p h v", h=HEADS), bank[7][:, 0:D].rearrange("p (h v) -> p h v", v=DV),
                                  head_inv[:, :].unsqueeze(2).broadcast_to([P, HEADS, DV]), ALU.mult).then_inc(o_copied, 1)

            def values_by_head(i, p):
                rows = HG * NP
                dve.wait_ge(vrep_done, i + 1)
                for a in range(2):
                    dve.tensor_tensor(v_blk[p][0:rows, 2 * a:2 * a + 2],
                                      bank[2 + a][0:rows, :].rearrange("p (b h v) -> p b h v", b=2, h=HEADS),
                                      v_mask[0:rows, :].unsqueeze(1).unsqueeze(3).broadcast_to([rows, 2, HEADS, DV]),
                                      ALU.mult).then_inc(v_blk_ready, 1)

            def keys_out(i):
                dve.wait_ge(k2_done, i + 1)
                dve.tensor_copy(k_T, bank[1][:, QD:QD + GB * NP].rearrange("p (b n) -> p b n", b=GB)).then_inc(k2_copied, 1)

            def summed(k):
                dve.wait_ge(proj_done, k + 1)
                dve.wait_ge(x1b_ready, k + 1)
                dve.tensor_tensor(x2_all[:, bass.ds(k, 1), :].squeeze(1), bank[4][:, D:2 * D],
                                  x1_all[:, bass.ds(k, 1), :].squeeze(1), ALU.add).then_inc(x2_ready, 1)
                dve.wait_ge(x2_ready, k + 1)
                dve.tensor_copy(seen[:, :], mv[:, 0, 0:1])
                dve.bn_stats(stats[:, 0, :], x2_all[:, bass.ds(k, 1), :].squeeze(1)).then_inc(stat2_ready, 1)
                dve.wait_ge(stat2_ready, k + 1)
                dve.tensor_copy(seen[:, :], stats[:, 0, 0:1])
                dve.bn_aggr(mv[:, 0, :], stats[:, 0, :]).then_inc(mv2_ready, 1)

            def turn(i, p, ahead=True, back1=True, back2=True, back3=True, back4=True):
                if back4:
                    normed(i - 4, first=back4 == "first")
                if back1:
                    shifted(i - 1)
                if ahead:
                    if back2:
                        dve.wait_ge(pv2_done, i - 1)
                    values_by_head(i, p)
                    if back1:
                        dve.wait_ge(k_blk_ready, i)
                    keys_out(i)
                if back1:
                    head_sums(i - 1)
                if back2:
                    divided(i - 2)
                if back1:
                    if back2:
                        head_inverse(i - 1)
                    else:
                        dve.wait_ge(head_sum_ready, i)
                        dve.reciprocal(head_inv[:, :], head_sum[:, :]).then_inc(head_inv_ready, 1)
                if back3:
                    summed(i - 3)

            dve.wait_ge(masks_ready, 11)
            for i in range(4):
                turn(i, i % 2, True, i >= 1, i >= 2, i >= 3, False)
            turn(4, 0, back4="first")
            turn(5, 1)
            with dve.Fori(3, NG // 2) as it:
                for p in range(2):
                    turn(it * 2 + p, p)
            for i in range(NG, NG + 4):
                turn(i, i % 2, False, i < NG + 1, i < NG + 2, i < NG + 3)

            def shared_hidden(q):
                for hc in range(DH):
                    dve.wait_ge(shared_silu, DH * q + hc + 1)
                    dve.wait_ge(shared_up_done, 2 * DH * q + DH + hc + 1)
                    if q >= 2:
                        dve.wait_ge(shared_done, 4 * (q - 1))
                    dve.tensor_tensor(sh_hid[:, q % 2, hc, :], bank[1 + DH + hc][:, :], sh_silu[:, hc, :], ALU.mult)\
                        .then_inc(shared_hid_ready, 1)

            def shared_add(q):
                for m in range(4 * q, 4 * q + 4):
                    dve.wait_ge(shared_done, m + 1)
                    dve.tensor_tensor(x2_all[:, m, :], x2_all[:, m, :], bank[5 + m % 2][:, 0:D], ALU.add).then_inc(shared_added, 1)

            dve.wait_ge(logits_done, 1)
            by_block = [P, 4, GB, NE]
            dve.tensor_tensor(logits.rearrange("p (n a) e -> p n a e", n=4),
                              bank[7][:, :].rearrange("p (a n e) -> p n a e", a=4, e=NL)[:, :, :, 0:NE],
                              rbias_b[:, :].unsqueeze(1).unsqueeze(1).broadcast_to(by_block), ALU.add).then_inc(logits_ready, 1)
            dve.wait_ge(logits_ready, 1)
            for g in range(NG):
                dve.max(best[:, g, :], logits[:, g, :]).then_inc(best_ready, 1)
            for g in range(NG):
                dve.wait_ge(best_ready, g + 1)
                dve.max_index(best_at[:, g, :], best[:, g, :], logits[:, g, :]).then_inc(best_at_ready, 1)
            dve.wait_ge(best_at_ready, NG)
            dve.tensor_copy(best_f[:, :, :], best_at[:, :, 0:TOPK]).then_inc(best_f_ready, 1)
            dve.wait_ge(best_f_ready, 1)
            wide = [P, NK, NE]
            dve.tensor_tensor(chosen, best_f[:, :, :].rearrange("p g k -> p (g k)").unsqueeze(2).broadcast_to(wide),
                              lane[:, :].unsqueeze(1).broadcast_to(wide), ALU.is_equal).then_inc(chosen_ready, 1)
            dve.tensor_tensor(gap_w[:, :], best[:, :, 1], best[:, :, 0], ALU.subtract).then_inc(gap_ready, 1)
            shared_hidden(0)
            dve.wait_ge(before_done, 1)
            dve.wait_ge(dest_ready, TOPK + 4)
            in_tile = bank[0][:, :].rearrange("p (c e) -> p c e", e=NE)
            earlier = bank[7][:, :].rearrange("p (c e) -> p c e", e=NE)
            dve.tensor_copy(count_a[:, NK:, :], in_tile).then_inc(count_step, 1)
            of, to, step, n = count_a, count_b, 1, 1
            while step < NK:
                dve.wait_ge(count_step, n)
                dve.tensor_tensor(to[:, NK:, :], of[:, NK:, :], of[:, NK - step:2 * NK - step, :], ALU.add).then_inc(count_step, 1)
                of, to, step, n = to, of, 2 * step, n + 1
            dve.wait_ge(count_step, n)
            counted, spare = of, to
            dve.tensor_scalar(tiles_f[:, :], counted[:, 2 * NK - 1, :], float(P - 1), None, ALU.add).then_inc(tiles_step, 1)
            dve.wait_ge(tiles_step, 1)
            dve.tensor_copy(tiles_i[:, :], tiles_f[:, :]).then_inc(tiles_step, 1)
            dve.wait_ge(tiles_step, 2)
            dve.tensor_single_scalar(tiles_h[:, :], tiles_i[:, :], P.bit_length() - 1, ALU.logical_shift_right).then_inc(tiles_step, 1)
            dve.wait_ge(tiles_step, 3)
            dve.tensor_copy(tiles_n[:, :], tiles_h[:, :]).then_inc(tiles_step, 1)
            dve.tensor_copy(cum_a[:, NE:], tiles_h[:, :]).then_inc(tiles_step, 1)
            cum, nxt, step, n = cum_a, cum_b, 1, 5
            while step < NE:
                dve.wait_ge(tiles_step, n)
                dve.tensor_tensor(nxt[:, NE:], cum[:, NE:], cum[:, NE - step:2 * NE - step], ALU.add).then_inc(tiles_step, 1)
                cum, nxt, step, n = nxt, cum, 2 * step, n + 1
            dve.wait_ge(tiles_step, n)
            dve.tensor_tensor(first_row[:, :], cum[:, NE:], tiles_n[:, :], ALU.subtract).then_inc(first_ready, 1)
            dve.tensor_tensor(place, counted[:, NK:, :], in_tile, ALU.subtract).then_inc(place_step, 1)
            dve.wait_ge(place_step, 1)
            dve.tensor_tensor(place, place, earlier, ALU.add).then_inc(place_step, 1)
            dve.wait_ge(place_step, 2)
            dve.wait_ge(first_ready, 1)
            dve.scalar_tensor_tensor(place, first_row[:, :].unsqueeze(1).broadcast_to(wide), float(P), place,
                                     ALU.mult, ALU.add).then_inc(place_step, 1)
            dve.wait_ge(place_step, 3)
            dve.tensor_tensor(place, place, chosen, ALU.mult).then_inc(place_step, 1)
            dve.wait_ge(place_step, 4)
            dve.tensor_reduce(place_f[:, :], place, AX.X, ALU.add).then_inc(place_step, 1)
            dve.wait_ge(place_step, 5)
            dve.tensor_copy(place_i[:, :], place_f[:, :]).then_inc(place_ready, 1)
            shared_hidden(1)
            shared_add(0)
            most = [1, SLOTS + 1, NE]
            dve.tensor_tensor(passed, tile_no[:, :].unsqueeze(2).broadcast_to(most),
                              cum[0:1, NE:].unsqueeze(1).broadcast_to(most), ALU.is_ge).then_inc(expert_step, 1)
            dve.wait_ge(expert_step, 1)
            dve.tensor_reduce(expert_f[:, :], passed, AX.X, ALU.add).then_inc(expert_step, 1)
            dve.wait_ge(expert_step, 2)
            dve.tensor_scalar(expert_m[:, :], expert_f[:, :], float(NE - 1), None, ALU.min).then_inc(expert_step, 1)
            dve.wait_ge(expert_step, 3)
            dve.tensor_copy(expert_up[:, 1:SLOTS + 2], expert_m[:, :]).then_inc(expert_step, 1)
            dve.tensor_copy(expert_back[:, 3:SLOTS + 4], expert_m[:, :]).then_inc(expert_step, 1)
            dve.wait_ge(gap_exp, 1)
            dve.tensor_scalar(gap_s[:, :], gap_e[:, :], 1.0, None, ALU.add).then_inc(gap_sum_ready, 1)
            dve.wait_ge(gap_sum_ready, 1)
            dve.reciprocal(mix[:, 0, :], gap_s[:, :]).then_inc(mix_ready, 1)
            dve.wait_ge(mix_ready, 1)
            dve.tensor_tensor(mix[:, 1, :], gap_e[:, :], mix[:, 0, :], ALU.mult).then_inc(mix_ready, 1)

            for q in range(2, 4):
                shared_hidden(q)
                shared_add(q - 1)
            shared_add(3)

            def dest_of(s, r, round_):
                dve.wait_ge(row_loaded[r], round_ * 16 + 16)
                dve.tensor_copy(dest[:, bass.ds(s, 1)], row_in[:, r, D:ROW].bitcast(u32)).then_inc(dest_copied, 1)

            def hidden(s, p):
                dve.wait_ge(silu_done, s + 1)
                dve.tensor_tensor(hid[:, p, :], bank[2 + p][:, HID:2 * HID], silu_g[:, p, :], ALU.mult).then_inc(hid_ready, 1)

            def result(s, r, round_, first=False):
                if not first:
                    dve.wait_ge(y_sent[r], round_ * 16)
                dve.wait_ge(down_done, s + 1)
                dve.tensor_copy(y_sb[:, r, :], bank[6 + r % 2][:, 0:D]).then_inc(y_ready, 1)

            def turn(s, r, round_, first=False):
                dest_of(s, r, round_)
                hidden(s - 1, (r - 1) % 2)
                result(s - 3, (r - 3) % ROWS, round_ - (1 if r < 3 else 0), first)

            for s in range(ROWS):
                dest_of(s, s, 0)
                if s >= 1:
                    hidden(s - 1, (s - 1) % 2)
                if s >= 3:
                    result(s - 3, s - 3, 0, first=True)
            for s in range(ROWS, 2 * ROWS):
                turn(s, s % ROWS, 1, first=s < ROWS + 3)
            with dve.Fori(2, SLOTS // ROWS) as it:
                for r in range(ROWS):
                    turn(it * ROWS + r, r, it)
            for s in range(SLOTS // ROWS * ROWS, SLOTS):
                turn(s, s % ROWS, s // ROWS)
            for s in range(SLOTS, SLOTS + 3):
                if s == SLOTS:
                    hidden(s - 1, (s - 1) % 2)
                result(s - 3, (s - 3) % ROWS, (s - 3) // ROWS)

            for n, size in enumerate(CHUNKS):
                first = sum(CHUNKS[:n])
                dve.wait_ge(y_loaded[n], 16 * TOPK)
                dve.wait_ge(mix_ready, 2)
                for g in range(first, first + size):
                    dve.scalar_tensor_tensor(x2_all[:, g, :], y_all[0][:, g, :], mix[:, 0, g:g + 1], x2_all[:, g, :],
                                             ALU.mult, ALU.add).then_inc(mixed_ready, 1)
                for g in range(first, first + size):
                    dve.wait_ge(mixed_ready, g + 1)
                    dve.scalar_tensor_tensor(x2_all[:, g, :], y_all[1][:, g, :], mix[:, 1, g:g + 1], x2_all[:, g, :],
                                             ALU.mult, ALU.add).then_inc(out_ready, 1)


_INS = ["x", "ctx_1024", "L0_xattn_Wq", "L0_xattn_bq", "L0_xattn_Wk", "L0_xattn_bk", "L0_xattn_Wv", "L0_xattn_bv",
        "L0_xattn_gamma", "L0_xattn_beta", "L0_attn_w_kv", "L0_attn_w_q", "L0_attn_b_q", "L0_attn_w_out", "L0_attn_b_out",
        "L0_ffn_router_w", "L0_ffn_router_bias", "L0_ffn_up_proj", "L0_ffn_gate_proj", "L0_ffn_down_proj",
        "L0_ffn_sh_gate", "L0_ffn_sh_up", "L0_ffn_sh_down"]


def kernel(**inputs):
    import numpy as _np
    import concourse.bacc as _bacc
    from concourse import mybir as _mybir
    from concourse.bass_utils import run_bass_kernel_spmd as _run

    nc = _bacc.Bacc("TRN2", target_bir_lowering=False, num_devices=1)
    arrays, tensors = {}, {}
    for name in _INS:
        a = _np.ascontiguousarray(inputs[name])
        arrays[f"in_{name}_dram"] = a
        tensors[name] = nc.dram_tensor(f"in_{name}_dram", a.shape, _mybir.dt.from_np(a.dtype), kind="ExternalInput").ap()
    shape = inputs["x"].shape
    out = nc.dram_tensor("out_dram", shape, _mybir.dt.from_np(_np.dtype("float32")), kind="ExternalOutput").ap()
    perceiver_layer(nc, tensors, out)
    r = _run(nc, [arrays], core_ids=[0])
    return r.results[0]["out_dram"]
```

```python
from contextlib import ExitStack

import concourse.bass as bass
from concourse import mybir


def perceiver_layer(nc, t, out):
    fp32 = mybir.dt.float32
    i32 = mybir.dt.int32
    u32 = mybir.dt.uint32
    ALU = mybir.AluOpType
    ACT = mybir.ActivationFunctionType
    AX = mybir.AxisListType

    x_in, ctx_in = t["x"], t["ctx_1024"]
    NL, NB, D = x_in.shape
    KEYS = ctx_in.shape[1]
    P = 128
    DH = D // P
    TOK = NL * NB
    PAIRS = TOK // P
    KT = KEYS // P
    TAIL = KEYS - KT * P
    KB = -(-KEYS // 512)
    KW = [min(512, KEYS - 512 * kb) for kb in range(KB)]
    LN_EPS = 1e-5
    TG = 2 * (2 * (KB - 1) + 1)
    TGH = TG // 2
    PH = KB // 2
    PV_LATE = 6
    RING = 3

    QD = t["L0_attn_w_q"].shape[0]
    HEADS = 16
    HD = QD // HEADS
    DV = D // HEADS
    NP = NL // 2 + 1
    Q_SCALE = float(DV) ** -0.5
    NG = TOK // P
    GB = P // NL
    CHUNKS = (4, 5, 5, 2)
    ROWS = 4
    KV_RING = 4
    HG = 6
    GROUPS = [(h, min(HG, HEADS - h)) for h in range(0, HEADS, HG)]

    NE, _, HID = t["L0_ffn_up_proj"].shape
    TOPK = 2
    NK = NG * TOPK
    SLOTS = (TOPK * TOK + NE * (P - 1)) // P
    NOWHERE = TOPK * TOK
    ROW = D + 1

    cross = ExitStack()
    with cross:
        def sb(name, shape, dt=fp32):
            return cross.enter_context(nc.sbuf_tensor(name, shape, dt))

        def sem(name):
            return cross.enter_context(nc.semaphore(name))

        bank = [cross.enter_context(nc.psum_tensor(f"bank{n}", [P, 512], fp32)) for n in range(8)]
        mid = nc.dram_tensor("mid", [TOK, 2 * D], fp32).ap()
        rows_dram = nc.dram_tensor("rows_by_expert", [SLOTS * P, ROW], fp32).ap()
        y_dram = nc.dram_tensor("expert_out", [TOPK * TOK, D], fp32).ap()

        ident = sb("ident", [P, P])
        ones = sb("ones", [P, P])
        ring_mem = sb("ring", [P, RING * 2 * (KT + 1) * D])
        ring = ring_mem[:, :].rearrange("p (r b k c) -> p r b k c", r=RING, b=2, c=D)
        ctxT_mem = sb("ctxT", [P, 2 * DH * KEYS])
        ctxT = ctxT_mem[:, :].rearrange("p (b d k) -> p b d k", b=2, d=DH)
        prob_mem = sb("prob", [P, KEYS + (KT + 1) * P])
        prob = prob_mem[:, 0:KEYS]
        probT = prob_mem[:, KEYS:].rearrange("p (k q) -> p k q", q=P)
        x_all = sb("x_all", [P, PAIRS, D])
        xn_mem = sb("xn_all", [P, PAIRS * ROW])
        xn_all = xn_mem[:, 0:PAIRS * D].rearrange("p (i c) -> p i c", c=D)
        qT_mem = sb("qT_all", [P, DH * TOK])
        qT_all = qT_mem[:, :].rearrange("p (d s) -> p d s", d=DH)
        q_now = sb("q_now", [P, DH, P])

        def views(mem, *shapes):
            at, got = 0, []
            for shape in shapes:
                size = 1
                for n in shape[1:]:
                    size *= n
                piece = mem[0:shape[0], at:at + size]
                if len(shape) > 2:
                    names = "abcd"[:len(shape) - 1]
                    piece = piece.rearrange(f"p ({' '.join(names)}) -> p {' '.join(names)}",
                                            **dict(zip(names[1:], shape[2:])))
                got.append(piece)
                at += size
            return got

        third = ring_mem[:, 2 * 2 * (KT + 1) * D:]
        wq, wk = views(third, [P, DH, D], [P, DH, D])
        wv = sb("wv", [P, DH, D])
        turned_mem = sb("turned", [P, 4 * DH * D])
        xnT, = views(turned_mem, [P, 2, DH, 512])
        w_outT, sh_gateT, sh_upT, sh_downT = views(turned_mem, [P, DH, D], [P, DH, D], [P, DH, D], [P, DH, D])
        wqT = sb("wqT", [P, DH, D])
        wkT = sb("wkT", [P, DH, D])
        wqk = sb("wqk", [P, DH, D])
        bq_col = sb("bq_col", [P, DH])
        bk_col = sb("bk_col", [P, DH])
        bk_rep = sb("bk_rep", [P, DH, P])
        bqk_col = sb("bqk_col", [P, DH])
        bk_row = sb("bk_row", [P, D + 1])
        gamma_b = sb("gamma_b", [P, D])
        beta_b = sb("beta_b", [P, D])
        bv_b = sb("bv_b", [P, D])
        x_stats = sb("x_stats", [P, PAIRS, 6])
        x_mv = sb("x_mv", [P, PAIRS, 2])
        x_rstd = sb("x_rstd", [P, PAIRS])
        x_var = sb("x_var", [P, PAIRS])
        shift = sb("shift", [P, PAIRS])
        dotted = sb("dotted", [P, D])
        eps = sb("eps", [P, 1])
        seen = sb("seen", [P, 1])
        m_half = sb("m_half", [P, PAIRS])
        blockmax = sb("blockmax", [P, KB])
        rowmax = sb("rowmax", [P, 1])
        topped = sb("topped", [P, 1])
        negmax = sb("negmax", [P, 1])
        sums = sb("sums", [P, KB])
        rowsum = sb("rowsum", [P, 1])
        rinv = sb("rinv", [P, 1])
        Un = sb("Un", [P, D])
        UT = sb("UT", [P, DH, P])
        res = sb("res", [P, D])
        scaled = sb("scaled", [P, D])
        stats = sb("stats", [P, 2, 6])
        mv = sb("mv", [P, 2, 2])
        var = sb("var", [P, 2])
        rstd = sb("rstd", [P, 2])
        stage = sb("stage", [P, 2, D])

        w_qT = sb("w_qT", [P, DH, QD])
        bout_b = sb("bout_b", [P, D])
        bq2_col = sb("bq2_col", [P, 1])
        w_pick = sb("w_pick", [P, GB, NP])
        w_rep = sb("w_rep", [P, GB, HG, NP])
        k_mask = sb("k_mask", [P, HEADS])
        v_mask = sb("v_mask", [P, HEADS])
        (kv_in, x_nT, q_T, q_nat, k_T, k_blk, v_blk_even, attn, attnT, o_sb, oT, n2_now) = views(
            ctxT_mem, [P, KV_RING, D], [P, DH, P], [P, 2, P], [P, P], [P, GB, NP], [P, GB, HEADS, NP],
            [P, GB, HEADS, DV], [P, HEADS, NP], [P, len(GROUPS), P], [P, D], [P, DH, P], [P, D])
        head_max = sb("head_max", [P, HEADS])
        head_sum = sb("head_sum", [P, HEADS])
        head_inv = sb("head_inv", [P, HEADS])
        x1_all = qT_mem[:, :].rearrange("p (g c) -> p g c", c=D)
        x2_all = x_all
        router_T = sb("router_T", [P, DH, NL])
        rbias_b = sb("rbias_b", [P, NE])
        not_below = sb("not_below", [P, P])
        lane = sb("lane", [P, NE])
        tile_no = sb("tile_no", [1, SLOTS + 1])
        blank = sb("blank", [P, ROW])
        w_gu, w_down, n2_first, n2T_low, passed = views(
            ring_mem, [P, NE, DH, 2 * HID], [P, NE, D], [P, NG, ROW], [P, TOK], [1, SLOTS + 1, NE])
        *raw_weights, w_q, router_w, w_kv4 = views(
            ring_mem[:, NE * DH * 2 * HID:], [P, DH, D], [P, DH, D], [P, DH, D], [P, DH, D], [P, D], [NE, D], [NP, P])
        n2T_high, v_blk_odd = views(prob_mem, [P, TOK], [P, GB, HEADS, DV])
        y_sb = views(prob_mem, [P, TOK], [P, ROWS, D])[1]
        n2T = [n2T_low, n2T_high]
        v_blk = [v_blk_even, v_blk_odd]
        n2_second = xn_mem[:, :].rearrange("p (g c) -> p g c", c=ROW)
        n2 = [n2_first, n2_second]
        y_all = [qT_mem[:, :].rearrange("p (g c) -> p g c", c=D), xn_all]
        logits, chosen, counted, place, keep, logitsT, best, best_at = views(
            qT_mem, [P, NG, NE], [P, NE, NK], [P, NE, NK], [P, NE, NK], [P, NE, NK], [P, 512], [P, NG, 8], [P, NG, 8])
        (sh_silu, sh_hid, row_in, rowT, silu_g, hid, hidT) = views(
            ctxT_mem, [P, DH, 512], [P, 2, DH, 512], [P, ROWS, ROW], [P, 2, DH, P], [P, 2, HID], [P, 2, HID], [P, 2, P])
        best_at = best_at.bitcast(u32)
        best_f = sb("best_f", [P, NG, TOPK])
        gap_w = sb("gap_w", [P, NG])
        gap_e = sb("gap_e", [P, NG])
        gap_s = sb("gap_s", [P, NG])
        mix = sb("mix", [P, TOPK, NG])
        tiles_i = sb("tiles_i", [P, NE], i32)
        tiles_h = sb("tiles_h", [P, NE], i32)
        tiles_n = sb("tiles_n", [P, NE])
        tiles_to = sb("tiles_to", [P, NE])
        first_row = sb("first_row", [P, NE])
        place_f = sb("place_f", [P, NK])
        place_i = sb("place_i", [P, NK], u32)
        expert_f = sb("expert_f", [1, SLOTS + 1])
        expert_m = sb("expert_m", [1, SLOTS + 1])
        experts_i = sb("experts_i", [1, SLOTS + 1 + ROWS], i32)
        dest = sb("dest", [P, SLOTS], u32)

        S = bank[0:KB]
        T = bank[4:6]
        U = bank[6]
        M = bank[7]

        x_loaded = [sem(f"x_loaded{n}") for n in range(4)]
        qk_loaded = sem("qk_loaded")
        rest_loaded = sem("rest_loaded")
        ctx_loaded = [sem(f"ctx_loaded{r}") for r in range(RING)]
        stored = sem("stored")
        const_step = sem("const_step")
        wT_done = sem("wT_done")
        wT_copied = sem("wT_copied")
        bk_rep_ready = sem("bk_rep_ready")
        wqk_done = sem("wqk_done")
        wqk_copied = sem("wqk_copied")
        bk_row_copied = sem("bk_row_copied")
        x_stat_ready = sem("x_stat_ready")
        x_mv_ready = sem("x_mv_ready")
        x_var_ready = sem("x_var_ready")
        x_rstd_ready = sem("x_rstd_ready")
        xn_ready = sem("xn_ready")
        dot_ready = sem("dot_ready")
        shift_ready = sem("shift_ready")
        xnT_done = sem("xnT_done")
        xnT_copied = sem("xnT_copied")
        qT_done = sem("qT_done")
        qT_copied = sem("qT_copied")
        xnb_ready = sem("xnb_ready")
        q_now_ready = sem("q_now_ready")
        t_done = sem("t_done")
        t_act = sem("t_act")
        t_dve = sem("t_dve")
        scores_done = sem("scores_done")
        blockmax_ready = sem("blockmax_ready")
        rowmax_ready = sem("rowmax_ready")
        topped_ready = sem("topped_ready")
        negmax_ready = sem("negmax_ready")
        exp_done = sem("exp_done")
        probT_done = sem("probT_done")
        probT_act = sem("probT_act")
        probT_dve = sem("probT_dve")
        pv_done = sem("pv_done")
        rowsum_ready = sem("rowsum_ready")
        rinv_ready = sem("rinv_ready")
        Un_ready = sem("Un_ready")
        UT_done = sem("UT_done")
        UT_copied = sem("UT_copied")
        res_done = sem("res_done")
        res_ready = sem("res_ready")
        stat_ready = sem("stat_ready")
        mv_ready = sem("mv_ready")
        var_ready = sem("var_ready")
        rstd_ready = sem("rstd_ready")
        scaled_ready = sem("scaled_ready")
        x1_ready = sem("x1_ready")
        n1_ready = sem("n1_ready")
        prep_loaded = sem("prep_loaded")
        qkb_loaded = sem("qkb_loaded")
        masks_ready = sem("masks_ready")
        prep_done = sem("prep_done")
        prep_copied = sem("prep_copied")
        smalls_ready = sem("smalls_ready")
        zeroed = sem("zeroed")
        x1b_ready = sem("x1b_ready")
        xnT2_done = sem("xnT2_done")
        xnT2_copied = sem("xnT2_copied")
        vrep_done = sem("vrep_done")
        v_blk_ready = sem("v_blk_ready")
        qN_done = sem("qN_done")
        qN_copied = sem("qN_copied")
        n2T_copied = sem("n2T_copied")
        q2_done = sem("q2_done")
        q2_copied = sem("q2_copied")
        k2_done = sem("k2_done")
        k2_copied = sem("k2_copied")
        k_blk_ready = sem("k_blk_ready")
        s2_done = sem("s2_done")
        head_max_ready = sem("head_max_ready")
        shifted_ready = sem("shifted_ready")
        exp2_done = sem("exp2_done")
        head_sum_ready = sem("head_sum_ready")
        head_inv_ready = sem("head_inv_ready")
        attnT_done = sem("attnT_done")
        attnT_copied = sem("attnT_copied")
        pv2_done = sem("pv2_done")
        o_copied = sem("o_copied")
        oT_done = sem("oT_done")
        oT_copied = sem("oT_copied")
        proj_done = sem("proj_done")
        x2_ready = sem("x2_ready")
        stat2_ready = sem("stat2_ready")
        mv2_ready = sem("mv2_ready")
        var2_ready = sem("var2_ready")
        rstd2_ready = sem("rstd2_ready")
        n2_ready = sem("n2_ready")
        n2a_ready = sem("n2a_ready")
        n2b_ready = sem("n2b_ready")
        experts_loaded = sem("experts_loaded")
        blank_ready = sem("blank_ready")
        blanked = sem("blanked")
        n2T_done = sem("n2T_done")
        logitsT_done = sem("logitsT_done")
        logitsT_copied = sem("logitsT_copied")
        logits_done = sem("logits_done")
        logits_ready = sem("logits_ready")
        best_ready = sem("best_ready")
        best_at_ready = sem("best_at_ready")
        best_f_ready = sem("best_f_ready")
        chosen_ready = sem("chosen_ready")
        before_done = sem("before_done")
        gap_ready = sem("gap_ready")
        gap_exp = sem("gap_exp")
        gap_sum_ready = sem("gap_sum_ready")
        mix_ready = sem("mix_ready")
        tiles_step = sem("tiles_step")
        first_ready = sem("first_ready")
        place_step = sem("place_step")
        place_ready = sem("place_ready")
        expert_step = sem("expert_step")
        dest_ready = sem("dest_ready")
        scattered = sem("scattered")
        shared_up_done = sem("shared_up_done")
        shared_silu = sem("shared_silu")
        shared_hid_ready = sem("shared_hid_ready")
        shared_done = sem("shared_done")
        shared_added = sem("shared_added")
        rowT_done = sem("rowT_done")
        rowT_copied = sem("rowT_copied")
        dest_copied = sem("dest_copied")
        gu_done = sem("gu_done")
        silu_done = sem("silu_done")
        hid_ready = sem("hid_ready")
        hidT_done = sem("hidT_done")
        hidT_copied = sem("hidT_copied")
        down_done = sem("down_done")
        y_ready = sem("y_ready")
        mixed_ready = sem("mixed_ready")
        written = sem("written")
        kv_loaded = [sem(f"kv_loaded{r}") for r in range(KV_RING)]
        row_loaded = [sem(f"row_loaded{r}") for r in range(ROWS)]
        y_sent = [sem(f"y_sent{r}") for r in range(ROWS)]
        y_loaded = [sem(f"y_loaded{n}") for n in range(len(CHUNKS))]

        block = cross.enter_context(nc.Block())

        TGROUPS = [(kb, b, dh) for kb in range(KB - 1) for b in range(2) for dh in range(DH)] \
            + [(KB - 1, b, None) for b in range(2)]
        USES = [("T", n) for n in range(6)] + [("P", 0), ("T", 6), ("T", 7), ("P", 1)] \
            + [("T", n) for n in range(8, 12)] + [("P", 2), ("T", 12), ("T", 13), ("P", 3)]

        LATE_QUERIES = ({1: (2, 0), 3: (2, 1), 5: (3, 0)}, {1: (3, 1)})

        def count_of(use, i):
            kind, n = USES[use]
            mine = sum(1 for m in range(use % 2, use + 1, 2) if USES[m][0] == kind)
            if kind == "T":
                return (t_dve if use % 2 else t_act), i * TGH + mine
            return (probT_dve if use % 2 else probT_act), (i - 1) * PH + mine

        def done_of(use, i):
            kind, n = USES[use]
            return (t_done, i * TG + (n + 1)) if kind == "T" else (probT_done, (i - 1) * KB + (n + 1))

        def copy_of(use):
            (kind, n), of = USES[use], T[use % 2]
            if kind == "P":
                rows, tiles = (P, 4) if n < KB - 1 else (TAIL, 1)
                return probT[0:rows, 4 * n:4 * n + tiles, :].rearrange("p a b -> p (a b)"), of[0:rows, 0:tiles * P]
            kb, b, dh = TGROUPS[n]
            if dh is None:
                return (ctxT[:, b, :, KT * P:KEYS],
                        of[:, 0:DH * P].rearrange("p (d k) -> p d k", d=DH)[:, :, 0:TAIL])
            return ctxT[:, b, dh, kb * 512:(kb + 1) * 512], of[:, :]

        @block.sync
        def _(sp):
            rows = x_in.rearrange("l b c -> (l b) c").rearrange("(i p) c -> p i c", p=P)
            for to, of in ((wq, "L0_xattn_Wq"), (wk, "L0_xattn_Wk")):
                sp.dma_start(to[:, :, :], t[of].rearrange("(k p) f -> p k f", p=P)).then_inc(qk_loaded, 16)
            for n in range(4):
                sp.dma_start(x_all[:, 4 * n:4 * n + 4, :], rows[:, 4 * n:4 * n + 4, :]).then_inc(x_loaded[n], 16)

            def load(i, r):
                pair = ctx_in[bass.ds(2 * i, 2)]
                sp.dma_start(ring[:, r, :, 0:KT, :].rearrange("p b k c -> p b (k c)"),
                             pair[:, 0:KT * P, :].rearrange("b (p k) c -> p b (k c)", k=KT)).then_inc(ctx_loaded[r], 16)
                sp.dma_start(ring[0:TAIL, r, :, KT, :],
                             pair[:, KT * P:KEYS, :].rearrange("b p c -> p b c")).then_inc(ctx_loaded[r], 16)

            def store(k):
                sp.wait_ge(n1_ready, k + 1)
                cols = mid.rearrange("(g q l) c -> l q g c", g=16, q=4)
                for b in range(2):
                    sp.dma_start(cols[bass.ds(2 * k + b, 1)].squeeze(0),
                                 stage[64 * b:64 * b + 64, :, :].rearrange("p a c -> p (a c)")).then_inc(stored, 16)

            sp.sem_inc(stored, 32)
            for i in range(RING):
                if i == 2:
                    sp.wait_ge(wT_done, 2)
                load(i, i)
            sp.wait_ge(pv_done, 1)
            load(RING, 0)
            with sp.Fori(0, (PAIRS - RING - 1) // RING) as it:
                for u in range(RING):
                    i = it * RING + (RING + 1 + u)
                    sp.wait_ge(pv_done, i - (RING - 1))
                    load(i, (RING + 1 + u) % RING)
                    store(i - RING - 1)
            store(PAIRS - RING - 1)
            sp.wait_ge(pv_done, PAIRS - 2)
            for to, of in zip(raw_weights, ("attn_w_out", "ffn_sh_gate", "ffn_sh_up", "ffn_sh_down")):
                sp.dma_start(to, t["L0_" + of].rearrange("(k p) c -> p k c", p=P)).then_inc(prep_loaded, 16)
            sp.dma_start(w_q, t["L0_attn_w_q"]).then_inc(prep_loaded, 16)
            for q in range(GB):
                sp.dma_start(w_kv4[:, NL * q:NL * q + NL], t["L0_attn_w_kv"][0:NP, 0:NL]).then_inc(prep_loaded, 16)
            sp.dma_start(router_w, t["L0_ffn_router_w"]).then_inc(prep_loaded, 16)
            for k in range(PAIRS - RING, PAIRS):
                store(k)
            sp.wait_ge(stored, 32 * (PAIRS + 1))

            def load_group(g, r):
                rows = mid[bass.ds(g * P, P)]
                sp.dma_start(kv_in[:, r, :], rows[:, D:2 * D]).then_inc(kv_loaded[r], 16)
                sp.dma_start(x1_all[:, bass.ds(g, 1), :].squeeze(1), rows[:, 0:D]).then_inc(kv_loaded[r], 16)

            def load_expert(e):
                for a, of in enumerate(("gate", "up")):
                    sp.dma_start(w_gu[:, bass.ds(e, 1), :, a * HID:(a + 1) * HID].squeeze(1),
                                 t[f"L0_ffn_{of}_proj"][bass.ds(e, 1)].squeeze(0).rearrange("(k p) h -> p k h", p=P))\
                        .then_inc(experts_loaded, 16)
                sp.dma_start(w_down[:, bass.ds(e, 1), :].squeeze(1), t["L0_ffn_down_proj"][bass.ds(e, 1)].squeeze(0))\
                    .then_inc(experts_loaded, 16)

            BLANKED = SLOTS // (NG - KV_RING)

            def blank_tiles(s, n):
                sp.dma_start(rows_dram[bass.ds(s * P, n * P)].rearrange("(s p) c -> p s c", p=P),
                             blank[:, :].unsqueeze(1).broadcast_to([P, n, ROW])).then_inc(blanked, 16)

            for g in range(KV_RING):
                load_group(g, g)
            sp.wait_ge(prep_done, 5)
            for e in range(NE - (NG - KV_RING)):
                load_expert(e)
            sp.wait_ge(blank_ready, 2)
            with sp.Fori(1, NG // KV_RING) as it:
                for u in range(KV_RING):
                    g = it * KV_RING + u
                    sp.wait_ge(vrep_done, g - (KV_RING - 1))
                    load_group(g, u)
                    load_expert(g + (NE - NG))
                    blank_tiles((g - KV_RING) * BLANKED, BLANKED)
            blank_tiles((NG - KV_RING) * BLANKED, SLOTS - (NG - KV_RING) * BLANKED)

            def load_rows(s, r):
                sp.dma_start(row_in[:, r, :], rows_dram[bass.ds(s * P, P), :]).then_inc(row_loaded[r], 16)

            sp.wait_ge(scattered, 16 * NK)
            for s in range(ROWS):
                load_rows(s, s)
            with sp.Fori(1, SLOTS // ROWS) as it:
                for r in range(ROWS):
                    s = it * ROWS + r
                    sp.wait_ge(rowT_done, s - (ROWS - 1))
                    sp.wait_ge(dest_copied, s - (ROWS - 1))
                    load_rows(s, r)
            for s in range(SLOTS // ROWS * ROWS, SLOTS):
                sp.wait_ge(rowT_done, s - (ROWS - 1))
                sp.wait_ge(dest_copied, s - (ROWS - 1))
                load_rows(s, s % ROWS)
            for r in range(ROWS):
                sp.wait_ge(y_sent[r], 16 * ((SLOTS - r + ROWS - 1) // ROWS))
            for n, size in enumerate(CHUNKS):
                first = sum(CHUNKS[:n])
                for k in range(TOPK):
                    sp.dma_start(y_all[k][:, first:first + size, :],
                                 y_dram[k * TOK:(k + 1) * TOK, :].rearrange("(g p) c -> p g c", p=P)[:, first:first + size, :])\
                        .then_inc(y_loaded[n], 16)
            for n, size in enumerate(CHUNKS):
                first = sum(CHUNKS[:n])
                sp.wait_ge(mixed_ready, TOPK * (first + size))
                for q in range(GB):
                    sp.dma_start(out.rearrange("l (q g) c -> q l g c", q=GB)[q][:, first:first + size, :],
                                 x2_all[NL * q:NL * q + NL, first:first + size, :]).then_inc(written, 16)
            sp.wait_ge(written, 16 * len(CHUNKS) * GB)

        @block.gpsimd
        def _(pool):
            pool.memset(ident[:, :], 0.0).then_inc(const_step, 1)
            pool.memset(m_half[:, :], -0.5).then_inc(const_step, 1)
            pool.memset(ones[:, :], 1.0).then_inc(const_step, 1)
            pool.memset(eps[:, :], LN_EPS).then_inc(const_step, 1)
            pool.wait_ge(const_step, 4)
            pool.affine_select(out=ident[:, :], in_=ident[:, :], compare_op=ALU.not_equal, fill=1.0, base=0,
                               pattern=[[-1, P]], channel_multiplier=1).then_inc(const_step, 1)
            pool.memset(blank[:, 0:D], 0.0).then_inc(blank_ready, 1)
            pool.iota(blank[:, D:ROW].bitcast(i32), pattern=[[0, 1]], base=NOWHERE, channel_multiplier=0)\
                .then_inc(blank_ready, 1)
            pool.memset(w_pick[:, :, :], 0.0).then_inc(zeroed, 1)
            pool.memset(w_rep[:, :, :, :], 0.0).then_inc(zeroed, 1)
            pool.memset(k_mask[:, :], Q_SCALE).then_inc(zeroed, 1)
            pool.memset(v_mask[:, :], 1.0).then_inc(zeroed, 1)
            pool.memset(not_below[:, :], 0.0).then_inc(zeroed, 1)
            pool.memset(router_T[:, :, :], 0.0).then_inc(zeroed, 1)
            pool.wait_ge(zeroed, 6)
            pool.affine_select(out=k_mask[:, :], in_=k_mask[:, :], compare_op=ALU.is_ge, fill=0.0, base=0,
                               pattern=[[-HD, HEADS]], channel_multiplier=1).then_inc(masks_ready, 1)
            pool.affine_select(out=not_below[:, :], in_=not_below[:, :], compare_op=ALU.is_ge, fill=-1.0, base=-1,
                               pattern=[[1, P]], channel_multiplier=-1).then_inc(masks_ready, 1)
            for h, n in GROUPS:
                pool.affine_select(out=v_mask[:, h:h + n], in_=v_mask[:, h:h + n], compare_op=ALU.is_ge, fill=0.0, base=0,
                                   pattern=[[-NP, n]], channel_multiplier=1).then_inc(masks_ready, 1)
            pool.wait_ge(masks_ready, 5)
            pool.affine_select(out=k_mask[:, :], in_=k_mask[:, :], compare_op=ALU.is_ge, fill=0.0, base=HD - 1,
                               pattern=[[HD, HEADS]], channel_multiplier=-1).then_inc(masks_ready, 1)
            for h, n in GROUPS:
                pool.affine_select(out=v_mask[:, h:h + n], in_=v_mask[:, h:h + n], compare_op=ALU.is_ge, fill=0.0,
                                   base=NP - 1, pattern=[[NP, n]], channel_multiplier=-1).then_inc(masks_ready, 1)
            pool.iota(lane[:, :], pattern=[[1, NE]], base=0, channel_multiplier=0,
                      allow_small_or_imprecise_dtypes=True).then_inc(masks_ready, 1)
            pool.iota(tile_no[:, :], pattern=[[1, SLOTS + 1]], base=0, channel_multiplier=0,
                      allow_small_or_imprecise_dtypes=True).then_inc(masks_ready, 1)
            for n in range(4):
                part = slice(4 * n, 4 * n + 4)
                pool.wait_ge(x_mv_ready, 4 * n + 4)
                pool.tensor_scalar(x_var[:, part], x_mv[:, part, 1], LN_EPS, None, ALU.add).then_inc(x_var_ready, 1)
                pool.wait_ge(x_var_ready, n + 1)
                pool.tensor_tensor(x_rstd[:, part], x_var[:, part], m_half[:, part], ALU.pow).then_inc(x_rstd_ready, 1)

            def take_q(i, first=False):
                pool.wait_ge(qT_copied, 2 if first else 8)
                pool.tensor_copy(q_now[:, :, :], qT_all[:, :, bass.ds(i * P, P)]).then_inc(q_now_ready, 1)

            def deviation(k, n):
                pool.wait_ge(mv_ready, 2 * k + (n + 1))
                pool.tensor_tensor(var[:, n:n + 1], mv[:, n, 1:2], eps[:, :], ALU.add).then_inc(var_ready, 1)
                pool.wait_ge(var_ready, 2 * k + (n + 1))
                pool.tensor_tensor(rstd[:, n:n + 1], var[:, n:n + 1], m_half[:, 0:1], ALU.pow).then_inc(rstd_ready, 1)

            take_q(0, first=True)
            def add_vectors(i):
                for to, vector in ((xn_all, bv_b), (x_all, beta_b)):
                    rows = to[:, bass.ds(i, 1), :].squeeze(1)
                    pool.tensor_tensor(rows, rows, vector[:, :], ALU.add).then_inc(xnb_ready, 1)

            pool.wait_ge(rest_loaded, 112)
            pool.wait_ge(xnT_done, 4)
            pool.wait_ge(shift_ready, PAIRS)
            add_vectors(0)
            for i in (1, 2):
                pool.wait_ge(scores_done, i * KB)
                take_q(i)
                add_vectors(i)
            deviation(0, 0)
            with pool.Fori(3, PAIRS) as i:
                pool.wait_ge(scores_done, i * KB)
                take_q(i)
                add_vectors(i)
                deviation(i - 3, 1)
                deviation(i - 2, 0)
            deviation(PAIRS - 3, 1)
            deviation(PAIRS - 2, 0)
            deviation(PAIRS - 2, 1)
            deviation(PAIRS - 1, 0)
            deviation(PAIRS - 1, 1)

            def keys_by_head(g):
                pool.wait_ge(k2_copied, g + 1)
                pool.tensor_tensor(k_blk, k_T.unsqueeze(2).broadcast_to([P, GB, HEADS, NP]),
                                   k_mask[:, :].unsqueeze(1).unsqueeze(3).broadcast_to([P, GB, HEADS, NP]),
                                   ALU.mult).then_inc(k_blk_ready, 1)

            def deviation2(k):
                pool.wait_ge(mv2_ready, k + 1)
                pool.tensor_tensor(var[:, 0:1], mv[:, 0, 1:2], eps[:, :], ALU.add).then_inc(var2_ready, 1)
                pool.wait_ge(var2_ready, k + 1)
                pool.tensor_tensor(rstd[:, 0:1], var[:, 0:1], m_half[:, 0:1], ALU.pow).then_inc(rstd2_ready, 1)

            def copy_rows(k):
                pool.wait_ge(n2_ready, k + 1)
                pool.tensor_copy(n2_second[:, bass.ds(k, 1), 0:D].squeeze(1), n2_now).then_inc(n2b_ready, 1)

            def with_bias(g):
                pool.wait_ge(xnT2_done, g + 1)
                pool.tensor_tensor(x1_all[:, bass.ds(g, 1), :].squeeze(1), x1_all[:, bass.ds(g, 1), :].squeeze(1),
                                   bout_b[:, :], ALU.add).then_inc(x1b_ready, 1)

            def turn(i, ahead=True, back3=True, back4=True):
                if ahead:
                    with_bias(i)
                if back4:
                    copy_rows(i - 4)
                if ahead:
                    keys_by_head(i)
                if back3:
                    deviation2(i - 3)

            for k in range(TOPK):
                pool.iota(n2[k][:, :, D].bitcast(i32), pattern=[[P, NG]], base=k * TOK, channel_multiplier=1)\
                    .then_inc(dest_ready, 1)
            for i in range(4):
                turn(i, back3=i >= 3, back4=False)
            with pool.Fori(4, NG) as i:
                turn(i)
            for i in range(NG, NG + 4):
                turn(i, ahead=False, back3=i < NG + 3)
                if i == NG:
                    pool.wait_ge(x2_ready, NG - 3)
                    pool.memset(keep, 1.0).then_inc(dest_ready, 1)
                if i == NG + 1:
                    pool.wait_ge(dest_ready, TOPK + 1)
                    pool.memset(keep[:, :, 0:1], 0.0).then_inc(dest_ready, 1)

            pool.wait_ge(blanked, 16 * (NG - KV_RING + 1))
            pool.wait_ge(place_ready, 1)
            pool.wait_ge(n2a_ready, NG)
            pool.wait_ge(n2b_ready, NG)
            pool.wait_ge(dest_ready, TOPK)
            for g in range(NG):
                for k in range(TOPK):
                    c = g * TOPK + k
                    pool.indirect_dma_start(rows_dram, bass.IndirectOffsetOnAxis(ap=place_i[:, c:c + 1], axis=0),
                                            n2[k][:, g, :], None).then_inc(scattered, 16)

            def send(s, r):
                pool.wait_ge(y_ready, s + 1)
                pool.indirect_dma_start(y_dram, bass.IndirectOffsetOnAxis(ap=dest[:, s:s + 1], axis=0), y_sb[:, r, :], None,
                                        bounds_check=TOPK * TOK - 1, oob_is_err=False).then_inc(y_sent[r], 16)

            for n in range(SLOTS):
                send(n, n % ROWS)

        @block.scalar
        def _(act):
            act.dma_start(bq_col[:, :], t["L0_xattn_bq"].rearrange("(k p) -> p k", p=P),
                          allow_slow_non_contiguous=True).then_inc(qkb_loaded, 16)
            act.dma_start(bk_col[:, :], t["L0_xattn_bk"].rearrange("(k p) -> p k", p=P),
                          allow_slow_non_contiguous=True).then_inc(qkb_loaded, 16)
            act.wait_ge(wT_done, 1)
            act.copy(wqT[:, :, :].rearrange("p a b -> p (a b)"), bank[0][:, :]).then_inc(wT_copied, 1)
            act.wait_ge(wT_done, 2)
            act.copy(wkT[:, :, :].rearrange("p a b -> p (a b)"), bank[1][:, :]).then_inc(wT_copied, 1)
            act.dma_start(wv[:, :, :], t["L0_xattn_Wv"].rearrange("(k p) f -> p k f", p=P)).then_inc(rest_loaded, 16)
            for to, of in ((bv_b, "L0_xattn_bv"), (gamma_b, "L0_xattn_gamma"), (beta_b, "L0_xattn_beta")):
                act.dma_start(to[:, :], t[of].partition_broadcast(P)).then_inc(rest_loaded, 16)
            act.dma_start(bq2_col[:, :], t["L0_attn_b_q"].rearrange("(p a) -> p a", a=1)).then_inc(rest_loaded, 16)
            act.dma_start(bout_b[:, :], t["L0_attn_b_out"].partition_broadcast(P)).then_inc(rest_loaded, 16)
            act.dma_start(rbias_b[:, :], t["L0_ffn_router_bias"].partition_broadcast(P)).then_inc(rest_loaded, 16)
            act.wait_ge(wqk_done, 1)
            act.copy(wqk[:, :, :].rearrange("p a b -> p (a b)"), bank[2][:, :]).then_inc(wqk_copied, 1)
            act.wait_ge(wqk_done, 2)
            act.copy(bqk_col[:, :], bank[3][:, 300:300 + DH]).then_inc(wqk_copied, 1)
            act.copy(bk_row[:, :], bank[3][:, 0:D + 1]).then_inc(bk_row_copied, 1)
            act.wait_ge(wqk_copied, 2)

            def query_block(n, dc):
                act.wait_ge(qT_done, 2 * n + dc + 1)
                act.activation(qT_all[:, dc, 512 * n:512 * n + 512], bank[6 + dc][:, :], ACT.Identity,
                               bias=bqk_col[:, dc:dc + 1]).then_inc(qT_copied, 1)

            for n in range(4):
                for dh in range(DH):
                    act.wait_ge(xnT_done, n + 1)
                    act.copy(xnT[:, n % 2, dh, :], T[dh][:, :]).then_inc(xnT_copied, 1)
                if 1 <= n <= 2:
                    for dc in range(DH):
                        query_block(n - 1, dc)
            def copy_out(i, use):
                act.wait_ge(*done_of(use, i))
                act.copy(*copy_of(use)).then_inc(count_of(use, i)[0], 1)

            def exps(i, kb):
                if kb == 0:
                    act.wait_ge(negmax_ready, i + 1)
                act.activation(prob[:, 512 * kb:512 * kb + KW[kb]], S[kb][:, 0:KW[kb]], ACT.Exp, bias=negmax[:, 0:1],
                               accum_out=sums[:, kb:kb + 1]).then_inc(exp_done, 1)

            def UT_evac(i):
                act.wait_ge(UT_done, i + 1)
                act.copy(UT[:, :, :].rearrange("p a b -> p (a b)"), M[:, 0:D]).then_inc(UT_copied, 1)

            def turn(i, ahead=True, back1=True, back2=True, also=None):
                for use in range(0, len(USES), 2):
                    if ahead if USES[use][0] == "T" else back1:
                        copy_out(i, use)
                    for after in (use, use + 1):
                        if also and after in also:
                            query_block(*also[after])
                    if back1 and 1 <= use // 2 <= KB:
                        exps(i - 1, use // 2 - 1)
                    if back2 and use == 10:
                        UT_evac(i - 2)

            turn(0, back1=False, back2=False, also=LATE_QUERIES[0])
            turn(1, back2=False, also=LATE_QUERIES[1])
            with act.Fori(2, PAIRS) as i:
                turn(i)
            turn(PAIRS, ahead=False)
            turn(PAIRS + 1, ahead=False, back1=False)
            for m, to in enumerate((w_outT, sh_gateT, sh_upT, sh_downT)):
                act.wait_ge(prep_done, m + 2)
                act.copy(to.rearrange("p a b -> p (a b)"), bank[m][:, :]).then_inc(prep_copied, 1)

            def turn(i, p, ahead=True, back1=True, back2=True, back3=True, back4=True):
                if ahead:
                    act.wait_ge(xnT2_done, i + 1)
                    act.copy(x_nT.rearrange("p a b -> p (a b)"), bank[0][:, 0:D]).then_inc(xnT2_copied, 1)
                if back2:
                    act.wait_ge(attnT_done, i - 1)
                    act.copy(attnT[0:HG * NP].rearrange("p a b -> p (a b)"), bank[6][0:HG * NP, 0:len(GROUPS) * P])\
                        .then_inc(attnT_copied, 1)
                if ahead:
                    act.wait_ge(q2_done, i + 1)
                    act.activation(q_T[:, p, :], bank[0][:, D:D + P], ACT.Identity, bias=bq2_col[:, 0:1]).then_inc(q2_copied, 1)
                if back3:
                    act.wait_ge(oT_done, i - 2)
                    act.copy(oT.rearrange("p a b -> p (a b)"), bank[4][:, 0:D]).then_inc(oT_copied, 1)
                if back1:
                    act.wait_ge(shifted_ready, i)
                    act.activation(attn, attn, ACT.Exp).then_inc(exp2_done, 1)
                if ahead:
                    act.wait_ge(qN_done, i + 1)
                    act.copy(q_nat.rearrange("p (h d) -> p h d", h=HEADS),
                             bank[1][:, 0:QD].rearrange("p (d h) -> p h d", h=HEADS)).then_inc(qN_copied, 1)
                if back4:
                    act.wait_ge(n2T_done, i - 3)
                    for dh in range(DH):
                        act.copy(n2T[dh][:, bass.ds((i - 4) * P, P)], bank[6][:, dh * P:dh * P + P]).then_inc(n2T_copied, 1)
                    act.copy(n2_first[:, bass.ds(i - 4, 1), 0:D].squeeze(1), n2_now).then_inc(n2a_ready, 1)

            act.wait_ge(rest_loaded, 112)
            for i in range(4):
                turn(i, i % 2, True, i >= 1, i >= 2, i >= 3, False)
            with act.Fori(2, NG // 2) as it:
                for p in range(2):
                    turn(it * 2 + p, p)
            for i in range(NG, NG + 4):
                turn(i, i % 2, False, i < NG + 1, i < NG + 2, i < NG + 3)
                if i >= NG + 2:
                    cols = slice(0, 3 * NL) if i == NG + 2 else slice(3 * NL, 4 * NL)
                    act.wait_ge(logitsT_done, i - NG - 1)
                    act.copy(logitsT[cols, :], bank[0][cols, :]).then_inc(logitsT_copied, 1)

            for q in range(4):
                for hc in range(DH):
                    act.wait_ge(shared_up_done, 2 * DH * q + hc + 1)
                    if q >= 1:
                        act.wait_ge(shared_hid_ready, DH * (q - 1) + hc + 1)
                    act.activation(sh_silu[:, hc, :], bank[1 + hc][:, :], ACT.Silu).then_inc(shared_silu, 1)
            act.wait_ge(gap_ready, 1)
            act.activation(gap_e[:, :], gap_w[:, :], ACT.Exp).then_inc(gap_exp, 1)

            def turn(s, p, ahead=True, back1=True):
                if ahead:
                    act.wait_ge(rowT_done, s + 1)
                    act.copy(rowT[:, p].rearrange("p a b -> p (a b)"), bank[p][:, 0:D]).then_inc(rowT_copied, 1)
                if back1:
                    act.wait_ge(gu_done, s)
                    act.activation(silu_g[:, 1 - p, :], bank[3 - p][:, 0:HID], ACT.Silu).then_inc(silu_done, 1)

            def hidden_out(k, p):
                act.wait_ge(hidT_done, k + 1)
                act.copy(hidT[:, p, :], bank[4 + p][:, 0:P]).then_inc(hidT_copied, 1)

            turn(0, 0, back1=False)
            turn(1, 1)
            with act.Fori(1, SLOTS // 2) as it:
                for p in range(2):
                    turn(it * 2 + p, p)
                    hidden_out(it * 2 + (p - 2), p)
            for s in range(SLOTS // 2 * 2, SLOTS + 2):
                turn(s, s % 2, s < SLOTS, s < SLOTS + 1)
                hidden_out(s - 2, s % 2)

        @block.tensor
        def _(pe):
            pe.wait_ge(const_step, 5)
            pe.wait_ge(qk_loaded, 32)
            for of, to in ((wq, 0), (wk, 1)):
                for kd in range(DH):
                    for fc in range(DH):
                        last = pe.transpose(bank[to][:, fc * D + kd * P:fc * D + kd * P + P],
                                            of[:, kd, fc * P:fc * P + P], ident[:, :])
                last.then_inc(wT_done, 1)
            pe.wait_ge(wT_copied, 2)
            for kd in range(DH):
                for fc in range(DH):
                    last = pe.matmul(bank[2][:, kd * D:kd * D + D], wqT[:, fc, kd * P:kd * P + P], wkT[:, fc, :],
                                     start=fc == 0, stop=fc == DH - 1)
            last.then_inc(wqk_done, 1)
            pe.wait_ge(qkb_loaded, 32)
            for dc in range(DH):
                for fc in range(DH):
                    pe.matmul(bank[3][:, 300 + dc:301 + dc], wkT[:, fc, dc * P:dc * P + P], bq_col[:, fc:fc + 1],
                              start=fc == 0, stop=fc == DH - 1)
            pe.wait_ge(bk_rep_ready, 1)
            for fc in range(DH):
                pe.matmul(bank[3][:, 0:D], bk_rep[:, fc, :], wqT[:, fc, :], start=fc == 0, stop=fc == DH - 1)
            for fc in range(DH):
                last = pe.matmul(bank[3][:, D:D + 1], bk_rep[:, fc, :], bq_col[:, fc:fc + 1],
                                 start=fc == 0, stop=fc == DH - 1)
            last.then_inc(wqk_done, 1)
            def queries_turned(n):
                pe.wait_ge(xn_ready, 4 * n + 4)
                if n >= 1:
                    pe.wait_ge(xnT_copied, 2 * n)
                for dh in range(DH):
                    for a in range(4):
                        last = pe.transpose(T[dh][:, a * P:a * P + P], xn_all[:, 4 * n + a, dh * P:dh * P + P], ident[:, :])
                last.then_inc(xnT_done, 1)

            def queries_projected(n, dc):
                pe.wait_ge(xnT_copied, 2 * n + 2)
                if n >= 1:
                    pe.wait_ge(qT_copied, 2 * n - 1 + dc)
                for k in range(DH):
                    last = pe.matmul(bank[6 + dc][:, :], wqk[:, k, dc * P:dc * P + P], xnT[:, n % 2, k, :],
                                     start=k == 0, stop=k == DH - 1)
                last.then_inc(qT_done, 1)

            pe.wait_ge(wqk_copied, 2)
            for n in range(4):
                queries_turned(n)
                if 1 <= n <= 2:
                    for dc in range(DH):
                        queries_projected(n - 1, dc)
            def fill(i, r, use):
                (kind, n), to = USES[use], T[use % 2]
                if kind == "P":
                    pe.wait_ge(exp_done, (i - 1) * KB + (n + 1))
                    for a in range(4 if n < KB - 1 else 1):
                        k = 4 * n + a
                        rows = P if k < KT else TAIL
                        last = pe.transpose(to[0:rows, a * P:a * P + P], prob[:, k * P:k * P + rows], ident[:, :])
                    last.then_inc(probT_done, 1)
                    return
                kb, b, dh = TGROUPS[n]
                if dh is None:
                    for d in range(DH):
                        last = pe.transpose(to[:, d * P:d * P + TAIL], ring[0:TAIL, r, b, KT, d * P:d * P + P],
                                            ident[0:TAIL, 0:TAIL])
                else:
                    for a in range(4):
                        last = pe.transpose(to[:, a * P:a * P + P], ring[:, r, b, 4 * kb + a, dh * P:dh * P + P], ident[:, :])
                last.then_inc(t_done, 1)

            def scores(i, kb, dh):
                if dh == 0:
                    uses = [m for m, (kind, n) in enumerate(USES) if kind == "T" and TGROUPS[n][0] == kb]
                    for m in uses[-2:]:
                        pe.wait_ge(*count_of(m, i))
                    if kb == 0:
                        pe.wait_ge(q_now_ready, i + 1)
                for b in range(2):
                    last = pe.matmul(S[kb][64 * b:64 * b + 64, 0:KW[kb]], q_now[:, dh, 64 * b:64 * b + 64],
                                     ctxT[:, b, dh, 512 * kb:512 * kb + KW[kb]], start=dh == 0, stop=dh == DH - 1)
                if dh == DH - 1:
                    last.then_inc(scores_done, 1)

            def weigh(i, r, k):
                rows = P if k < KT else TAIL
                if k % 4 == 0:
                    pe.wait_ge(*count_of(USES.index(("P", k // 4)), i + 1))
                for b in range(2):
                    last = pe.matmul(U[64 * b:64 * b + 64, 0:D], probT[0:rows, k, 64 * b:64 * b + 64],
                                     ring[0:rows, r, b, k, :], start=k == 0, stop=k == KT)
                if k == KT:
                    last.then_inc(pv_done, 1)

            def flip(i):
                pe.wait_ge(Un_ready, i + 1)
                for dh in range(DH):
                    last = pe.transpose(M[:, dh * P:dh * P + P], Un[:, dh * P:dh * P + P], ident[:, :])
                last.then_inc(UT_done, 1)

            def project(i):
                pe.wait_ge(UT_copied, i + 1)
                for k in range(DH):
                    last = pe.matmul(M[:, D:2 * D], UT[:, k, :], wv[:, k, :], start=k == 0, stop=k == DH - 1)
                last.then_inc(res_done, 1)

            AFTER = {m: [("weigh2", PV_LATE + m)] for m in range(KT + 1 - PV_LATE)}
            AFTER[6] = AFTER[6] + [("scores", 0, 0)]
            AFTER[8], AFTER[9], AFTER[10] = [("scores", 0, 1)], [("flip",)], [("weigh1", 0), ("weigh1", 1)]
            AFTER[12], AFTER[13] = [("scores", 1, 0)], [("project",), ("scores", 1, 1)]
            AFTER[14], AFTER[15] = [("scores", 2, 0), ("weigh1", 2)], [("weigh1", 3), ("weigh1", 4)]
            AFTER[16], AFTER[17] = [("scores", 2, 1)], [("scores", 3, 0), ("scores", 3, 1), ("weigh1", PV_LATE - 1)]

            def turn(i, r, round_, ahead=True, back1=True, back2=True, before="all", also=None):
                def there(use, ahead, back1):
                    return ahead if USES[use][0] == "T" else back1

                was = {"all": (True, True), "first": (True, False), "last": (False, True), "none": (False, False)}[before]
                if ahead:
                    pe.wait_ge(ctx_loaded[r], round_ * 32 + 32)
                for use in range(len(USES)):
                    if there(use, ahead, back1):
                        earlier = [(m, i) for m in range(use - 2, -1, -2) if there(m, ahead, back1)] \
                            + [(m, i - 1) for m in range(len(USES) - 2 + use % 2, -1, -2) if there(m, *was)]
                        if earlier:
                            pe.wait_ge(*count_of(*earlier[0]))
                        fill(i, r, use)
                    if also and use in also:
                        queries_projected(*also[use])
                    for what, *args in AFTER.get(use, ()):
                        if what == "scores" and ahead:
                            scores(i, *args)
                        elif what == "weigh1" and back1:
                            if args[0] == 0:
                                if back2:
                                    pe.wait_ge(Un_ready, i - 1)
                                else:
                                    pe.wait_ge(qT_copied, 8)
                            weigh(i - 1, (r - 1) % RING, *args)
                        elif what == "weigh2" and back2:
                            weigh(i - 2, (r - 2) % RING, *args)
                        elif what == "flip" and back2:
                            flip(i - 2)
                        elif what == "project" and back2:
                            project(i - 2)

            pe.wait_ge(xnT_copied, 8)
            turn(0, 0, 0, back1=False, back2=False, before="none", also=LATE_QUERIES[0])
            pe.wait_ge(rest_loaded, 112)
            turn(1, 1, 0, back2=False, before="first", also=LATE_QUERIES[1])
            turn(2, 2, 0)
            with pe.Fori(0, (PAIRS - RING) // RING) as it:
                for u in range(RING):
                    turn(it * RING + (RING + u), u, it + 1)
            turn(PAIRS - 1, (PAIRS - 1) % RING, (PAIRS - 1) // RING)
            turn(PAIRS, PAIRS % RING, None, ahead=False)
            turn(PAIRS + 1, (PAIRS + 1) % RING, None, ahead=False, back1=False, before="last")
            pe.wait_ge(prep_loaded, 16 * (GB + 6))
            for k in range(DH):
                pe.transpose(T[0][:, k * QD:k * QD + QD], w_q[:, k * P:k * P + P], ident[:, :])
                pe.transpose(T[0][:, 256 + k * NE:256 + k * NE + NE], router_w[:, k * P:k * P + P], ident[0:NE, 0:NE])
            pe.transpose(T[0][:, 300:300 + NP], w_kv4, ident[0:NP, 0:NP]).then_inc(prep_done, 1)
            for m, of in enumerate(raw_weights):
                for kd in range(DH):
                    for fc in range(DH):
                        last = pe.transpose(bank[m][:, fc * D + kd * P:fc * D + kd * P + P],
                                            of[:, kd, fc * P:fc * P + P], ident[:, :])
                last.then_inc(prep_done, 1)

            def rows_in(i, r, round_):
                pe.wait_ge(kv_loaded[r], round_ * 32 + 32)
                for dh in range(DH):
                    last = pe.transpose(bank[0][:, dh * P:dh * P + P], kv_in[:, r, dh * P:dh * P + P], ident[:, :])
                last.then_inc(xnT2_done, 1)

            def values(i, r):
                by_head = kv_in[:, r, :].rearrange("p (v h) -> p h v", h=HEADS)
                for b in range(GB):
                    last = pe.matmul(bank[2 + b // 2][0:HG * NP, (b % 2) * D:(b % 2) * D + D],
                                     w_rep[:, b, :, :].rearrange("p h n -> p (h n)"), by_head, start=True, stop=True)
                last.then_inc(vrep_done, 1)

            def queries(i):
                pe.wait_ge(xnT2_copied, i + 1)
                for k in range(DH):
                    last = pe.matmul(bank[0][:, D:D + P], w_qT[:, k, :], x_nT[:, k, :], start=k == 0, stop=k == DH - 1)
                last.then_inc(q2_done, 1)

            def query_rows(i, p):
                pe.wait_ge(q2_copied, i + 1)
                pe.transpose(bank[1][:, 0:QD], q_T[:, p, :], ident[:, :]).then_inc(qN_done, 1)

            def keys(i):
                pe.wait_ge(qN_copied, i + 1)
                pe.matmul(bank[1][:, QD:QD + GB * NP], q_nat,
                          w_pick[:, :, :].rearrange("p b n -> p (b n)"), start=True, stop=True).then_inc(k2_done, 1)

            def group_scores(k, p):
                pe.wait_ge(k_blk_ready, k + 1)
                for b in range(GB):
                    last = pe.matmul(bank[5][NL * b:NL * b + NL, 0:HEADS * NP], q_T[:, p, NL * b:NL * b + NL],
                                     k_blk[:, b].rearrange("p h n -> p (h n)"), start=True, stop=True)
                last.then_inc(s2_done, 1)

            def attn_turned(k):
                pe.wait_ge(exp2_done, k + 1)
                flat = attn.rearrange("p h n -> p (h n)")
                for j, (h, n) in enumerate(GROUPS):
                    last = pe.transpose(bank[6][0:n * NP, j * P:j * P + P], flat[:, h * NP:(h + n) * NP], ident[:, :])
                last.then_inc(attnT_done, 1)

            def weighted(k, p):
                pe.wait_ge(attnT_copied, k + 1)
                pe.wait_ge(v_blk_ready, k * 2 + 2)
                for b in range(GB):
                    for j, (h, n) in enumerate(GROUPS):
                        last = pe.matmul(bank[7][NL * b:NL * b + NL, h * DV:(h + n) * DV], attnT[0:n * NP, j, NL * b:NL * b + NL],
                                         v_blk[p][0:n * NP, b, h:h + n, :].rearrange("p h v -> p (h v)"), start=True, stop=True)
                last.then_inc(pv2_done, 1)

            def out_turned(k):
                pe.wait_ge(o_copied, k + 1)
                for dh in range(DH):
                    last = pe.transpose(bank[4][:, dh * P:dh * P + P], o_sb[:, dh * P:dh * P + P], ident[:, :])
                last.then_inc(oT_done, 1)

            def out_product(k):
                pe.wait_ge(oT_copied, k + 1)
                for j in range(DH):
                    last = pe.matmul(bank[4][:, D:2 * D], oT[:, j, :], w_outT[:, j, :], start=j == 0, stop=j == DH - 1)
                last.then_inc(proj_done, 1)

            def normed_turned(k):
                pe.wait_ge(n2_ready, k + 1)
                for dh in range(DH):
                    last = pe.transpose(bank[6][:, dh * P:dh * P + P], n2_now[:, dh * P:dh * P + P], ident[:, :])
                last.then_inc(n2T_done, 1)

            def turn(i, r, round_, first=False, ahead=True, back1=True, back2=True, back3=True, back4=True, back5=True):
                p = r % 2
                if ahead:
                    if not first:
                        pe.wait_ge(q2_copied, i)
                    rows_in(i, r, round_)
                if back2:
                    if back5:
                        pe.wait_ge(n2T_copied, i * 2 - 8)
                    attn_turned(i - 2)
                if ahead:
                    if not first:
                        pe.wait_ge(v_blk_ready, i * 2)
                    values(i, r)
                    queries(i)
                if back1:
                    if back2:
                        pe.wait_ge(shifted_ready, i - 1)
                    group_scores(i - 1, 1 - p)
                if back3:
                    if back4:
                        pe.wait_ge(x2_ready, i - 3)
                    out_turned(i - 3)
                if back2:
                    if back3:
                        pe.wait_ge(o_copied, i - 2)
                    weighted(i - 2, p)
                if ahead:
                    if not first:
                        pe.wait_ge(k2_copied, i)
                    query_rows(i, p)
                if back4:
                    if back5:
                        pe.wait_ge(n2T_copied, i * 2 - 8)
                    normed_turned(i - 4)
                if back3:
                    out_product(i - 3)
                if ahead:
                    keys(i)

            pe.wait_ge(res_ready, PAIRS)
            pe.wait_ge(prep_copied, 4)
            pe.wait_ge(smalls_ready, 2 * GB + 2)
            for i in range(KV_RING):
                turn(i, i, 0, i == 0, True, i >= 1, i >= 2, i >= 3, False, False)
            turn(KV_RING, 0, 1, back5=False)
            for i in range(KV_RING + 1, 2 * KV_RING):
                turn(i, i % KV_RING, 1)
            with pe.Fori(2, NG // KV_RING) as it:
                for r in range(KV_RING):
                    turn(it * KV_RING + r, r, it)
            def router(blocks):
                for k in range(DH):
                    for n in blocks:
                        last = pe.matmul(bank[0][NL * n:NL * n + NL, :], router_T[:, k, :], n2T[k][:, 512 * n:512 * n + 512],
                                         start=k == 0, stop=k == DH - 1)
                last.then_inc(logitsT_done, 1)

            def router_turned(blocks, n):
                pe.wait_ge(logitsT_copied, n)
                lo, hi = NL * blocks[0], NL * blocks[-1] + NL
                for a in range(4):
                    last = pe.transpose(bank[7][:, a * P + lo:a * P + hi], logitsT[lo:hi, a * P:a * P + P], ident[lo:hi, lo:hi])
                last.then_inc(logits_done, 1)

            def shared_half(q, a, hc):
                if q >= 1:
                    pe.wait_ge(shared_hid_ready if a else shared_silu, DH * (q - 1) + hc + 1)
                w = sh_upT if a else sh_gateT
                for k in range(DH):
                    last = pe.matmul(bank[1 + DH * a + hc][:, :], w[:, k, hc * P:hc * P + P],
                                     n2T[k][:, 512 * q:512 * q + 512], start=k == 0, stop=k == DH - 1)
                last.then_inc(shared_up_done, 1)

            for i in range(NG, NG + 4):
                turn(i, i % KV_RING, None, False, False, i < NG + 1, i < NG + 2, i < NG + 3)
                if i == NG + 1:
                    router((0, 1, 2))
                if i == NG + 2:
                    pe.wait_ge(o_copied, NG)
                    router_turned((0, 1, 2), 1)
                    shared_half(0, 0, 0)

            pe.wait_ge(n2T_copied, DH * NG)
            router((3,))
            shared_half(0, 0, 1)
            pe.wait_ge(logits_ready, 1)
            router_turned((3,), 2)
            shared_half(0, 1, 0)
            shared_half(0, 1, 1)

            def shared_up(q):
                for a in range(2):
                    for hc in range(DH):
                        shared_half(q, a, hc)

            def shared_down(q):
                pe.wait_ge(shared_hid_ready, DH * q + DH)
                for a in range(4):
                    m = 4 * q + a
                    if m >= 2:
                        pe.wait_ge(shared_added, m - 1)
                    for hc in range(DH):
                        last = pe.matmul(bank[5 + m % 2][:, 0:D], sh_hid[:, q % 2, hc, a * P:a * P + P], sh_downT[:, hc, :],
                                         start=hc == 0, stop=hc == DH - 1)
                    last.then_inc(shared_done, 1)

            pe.wait_ge(chosen_ready, 2)
            pe.wait_ge(logits_ready, 2)
            pe.matmul(bank[0][:, 0:NE], ones[:, :], counted[:, :, NK - 1], start=True, stop=True).then_inc(before_done, 1)
            pe.matmul(bank[7][:, :], not_below[:, :], chosen.rearrange("p e c -> p (e c)"), start=True, stop=False)
            pe.matmul(bank[7][:, :], ones[:, :], counted.rearrange("p e c -> p (e c)"), start=False, stop=True)\
                .then_inc(before_done, 1)
            for q in range(1, 4):
                shared_up(q)
                shared_down(q - 1)
            shared_down(3)

            expert_now = [pe.alloc_register(f"expert_now{r}") for r in range(ROWS)]
            expert_old = [pe.alloc_register(f"expert_old{r}") for r in range(2)]

            def load_experts(round_):
                pe.load(expert_now, experts_i[0:1, bass.ds(round_ * ROWS, ROWS)])

            def next_experts(round_):
                for old, now in zip(expert_old, expert_now[2:]):
                    pe.reg_mov(old, now)
                load_experts(round_)
                up = [pe.snap(reg, min_val=0, max_val=NE - 1) for reg in expert_now]
                return up, [pe.snap(reg, min_val=0, max_val=NE - 1) for reg in expert_old] + up[0:2]

            def expert_of(s):
                return pe.value_load(experts_i[0:1, s + 1:s + 2], min_val=0, max_val=NE - 1)

            def rows_T(s, r, round_):
                pe.wait_ge(row_loaded[r], round_ * 16 + 16)
                for dh in range(DH):
                    last = pe.transpose(bank[r % 2][:, dh * P:dh * P + P], row_in[:, r, dh * P:dh * P + P], ident[:, :])
                last.then_inc(rowT_done, 1)

            def gate_up(s, p, e):
                pe.wait_ge(rowT_copied, s + 1)
                for k in range(DH):
                    last = pe.matmul(bank[2 + p][:, 0:2 * HID], rowT[:, p, k, :], w_gu[:, bass.ds(e, 1), k, :].squeeze(1),
                                     start=k == 0, stop=k == DH - 1)
                last.then_inc(gu_done, 1)

            def hidden_T(s, p):
                pe.wait_ge(hid_ready, s + 1)
                pe.transpose(bank[4 + p][:, 0:P], hid[:, p, :], ident[:, :]).then_inc(hidT_done, 1)

            def back(s, p, e, first=False):
                pe.wait_ge(hidT_copied, s + 1)
                if not first:
                    pe.wait_ge(y_ready, s - 1)
                pe.matmul(bank[6 + p][:, 0:D], hidT[:, p, :], w_down[:, bass.ds(e, 1), :].squeeze(1), start=True, stop=True)\
                    .then_inc(down_done, 1)

            def turn(s, r, round_, ahead=True, back1=True, back2=True, back3=True, back5=True, experts=None):
                p = r % 2
                if ahead:
                    rows_T(s, r, round_)
                if back1:
                    gate_up(s - 1, 1 - p, experts[0][r] if experts else expert_of(s - 1))
                if back3:
                    back(s - 3, 1 - p, experts[1][r] if experts else expert_of(s - 3), first=not back5)
                if back2:
                    hidden_T(s - 2, p)

            pe.wait_ge(expert_step, 4)
            pe.wait_ge(experts_loaded, 16 * 3 * NE)
            pe.wait_ge(shared_added, NG)
            pe.wait_ge(place_ready, 1)
            for s in range(ROWS):
                turn(s, s, 0, True, s >= 1, s >= 2, s >= 3, False)
            turn(ROWS, 0, 1, back5=False)
            for s in range(ROWS + 1, 2 * ROWS):
                turn(s, s % ROWS, 1)
            load_experts(1)
            with pe.Fori(2, SLOTS // ROWS) as it:
                experts = next_experts(it)
                for r in range(ROWS):
                    turn(it * ROWS + r, r, it, experts=experts)
            for s in range(SLOTS // ROWS * ROWS, SLOTS + 3):
                turn(s, s % ROWS, s // ROWS, s < SLOTS, s < SLOTS + 1, s < SLOTS + 2)

        @block.vector
        def _(dve):
            def x_statistics(n):
                dve.wait_ge(x_loaded[n], 16)
                for a in range(4 * n, 4 * n + 4):
                    dve.bn_stats(x_stats[:, a, :], x_all[:, a, :]).then_inc(x_stat_ready, 1)
                for a in range(4 * n, 4 * n + 4):
                    dve.wait_ge(x_stat_ready, a + 1)
                    dve.bn_aggr(x_mv[:, a, :], x_stats[:, a, :]).then_inc(x_mv_ready, 1)

            def x_normed(n):
                dve.wait_ge(x_rstd_ready, n + 1)
                for a in range(4 * n, 4 * n + 4):
                    dve.tensor_scalar(xn_all[:, a, :], x_all[:, a, :], x_mv[:, a, 0:1], x_rstd[:, a:a + 1],
                                      ALU.subtract, ALU.mult).then_inc(xn_ready, 1)

            def small_operands():
                dve.wait_ge(prep_done, 1)
                dve.wait_ge(zeroed, 6)
                for b in range(GB):
                    mine = slice(NL * b, NL * b + NL)
                    dve.tensor_copy(w_pick[mine, b, :], T[0][mine, 300:300 + NP]).then_inc(smalls_ready, 1)
                    dve.tensor_copy(w_rep[mine, b, :, :], T[0][mine, 300:300 + NP].unsqueeze(1).broadcast_to([NL, HG, NP]))\
                        .then_inc(smalls_ready, 1)
                dve.tensor_copy(w_qT[:, :, :].rearrange("p a b -> p (a b)"), T[0][:, 0:DH * QD]).then_inc(smalls_ready, 1)
                dve.tensor_copy(router_T[:, :, 0:NE], T[0][:, 256:256 + DH * NE].rearrange("p (k e) -> p k e", k=DH))\
                    .then_inc(smalls_ready, 1)

            x_statistics(0)
            dve.wait_ge(qkb_loaded, 32)
            dve.tensor_copy(bk_rep[:, :, :], bk_col[:, :].unsqueeze(2).broadcast_to([P, DH, P])).then_inc(bk_rep_ready, 1)
            for n in range(1, 4):
                x_statistics(n)
                x_normed(n - 1)
            x_normed(3)
            dve.wait_ge(bk_row_copied, 1)

            def copy_out(i, use):
                dve.wait_ge(*done_of(use, i))
                dve.tensor_copy(*copy_of(use)).then_inc(count_of(use, i)[0], 1)

            def block_max(i, kb):
                dve.wait_ge(scores_done, i * KB + (kb + 1))
                dve.tensor_reduce(blockmax[:, kb:kb + 1], S[kb][:, 0:KW[kb]], AX.X, ALU.max).then_inc(blockmax_ready, 1)

            def row_max(i):
                dve.wait_ge(blockmax_ready, i * KB + KB)
                dve.tensor_reduce(rowmax[:, :], blockmax[:, :], AX.X, ALU.max).then_inc(rowmax_ready, 1)
                dve.wait_ge(rowmax_ready, i + 1)
                dve.tensor_tensor(topped[:, :], rowmax[:, :], shift[:, bass.ds(i, 1)], ALU.add).then_inc(topped_ready, 1)
                dve.wait_ge(topped_ready, i + 1)
                dve.tensor_tensor(negmax[:, :], shift[:, bass.ds(i, 1)], topped[:, :], ALU.subtract).then_inc(negmax_ready, 1)

            def row_sum(k):
                dve.wait_ge(exp_done, k * KB + KB)
                dve.tensor_reduce(rowsum[:, :], sums[:, :], AX.X, ALU.add).then_inc(rowsum_ready, 1)
                dve.wait_ge(rowsum_ready, k + 1)
                dve.reciprocal(rinv[:, :], rowsum[:, :]).then_inc(rinv_ready, 1)

            def normalise(k):
                dve.wait_ge(pv_done, k + 1)
                dve.wait_ge(rinv_ready, k + 1)
                dve.tensor_scalar(Un[:, :], U[:, 0:D], rinv[:, 0:1], None, ALU.mult).then_inc(Un_ready, 1)

            def residual(k):
                dve.wait_ge(res_done, k + 1)
                dve.wait_ge(xnb_ready, 2 * k + 2)
                dve.tensor_tensor(res[:, :], M[:, D:2 * D], xn_all[:, bass.ds(k, 1), :].squeeze(1), ALU.add).then_inc(res_ready, 1)
                dve.wait_ge(res_ready, k + 1)
                dve.bn_stats(stats[:, 0, :], res[:, :]).then_inc(stat_ready, 1)
                dve.wait_ge(stat_ready, 2 * k + 1)
                dve.tensor_copy(seen[:, :], stats[:, 0, 0:1])
                dve.bn_aggr(mv[:, 0, :], stats[:, 0, :]).then_inc(mv_ready, 1)
                dve.wait_ge(mv_ready, 2 * k + 1)
                dve.scalar_tensor_tensor(scaled[:, :], res[:, :], mv[:, 0, 0:1], gamma_b[:, :],
                                         ALU.subtract, ALU.mult).then_inc(scaled_ready, 1)

            def first_norm(k):
                dve.wait_ge(scaled_ready, k + 1)
                dve.wait_ge(rstd_ready, 2 * k + 1)
                dve.wait_ge(stored, k * 32 + 32)
                dve.scalar_tensor_tensor(stage[:, 0, :], scaled[:, :], rstd[:, 0:1], x_all[:, bass.ds(k, 1), :].squeeze(1),
                                         ALU.mult, ALU.add).then_inc(x1_ready, 1)
                dve.wait_ge(x1_ready, k + 1)
                dve.bn_stats(stats[:, 1, :], stage[:, 0, :]).then_inc(stat_ready, 1)
                dve.wait_ge(stat_ready, 2 * k + 2)
                dve.tensor_copy(seen[:, :], stats[:, 1, 0:1])
                dve.bn_aggr(mv[:, 1, :], stats[:, 1, :]).then_inc(mv_ready, 1)

            def second_norm(k):
                dve.wait_ge(rstd_ready, 2 * k + 2)
                dve.tensor_scalar(stage[:, 1, :], stage[:, 0, :], mv[:, 1, 0:1], rstd[:, 1:2],
                                  ALU.subtract, ALU.mult).then_inc(n1_ready, 1)

            def turn(i, ahead=True, back1=True, back2=True, back3=True):
                for use in range(1, len(USES), 2):
                    if ahead if USES[use][0] == "T" else back1:
                        copy_out(i, use)
                    if use == 3 and back3:
                        first_norm(i - 3)
                    if use == 5 and back2:
                        normalise(i - 2)
                    if use == 9:
                        if back1:
                            row_sum(i - 1)
                        if ahead:
                            block_max(i, 0)
                        if back3:
                            second_norm(i - 3)
                    if use == 13:
                        if ahead:
                            block_max(i, 1)
                        if back2:
                            residual(i - 2)
                if ahead:
                    block_max(i, 2)
                    block_max(i, 3)
                    row_max(i)

            for a in range(PAIRS):
                if a >= 1:
                    dve.wait_ge(dot_ready, a)
                dve.tensor_tensor_reduce(out=dotted[:, :], in0=xn_all[:, a, :], in1=bk_row[:, 0:D], scale=1.0,
                                         scalar=bk_row[:, D:D + 1], op0=ALU.mult, op1=ALU.add,
                                         accum_out=shift[:, a:a + 1]).then_inc(dot_ready, 1)
            dve.wait_ge(dot_ready, PAIRS)
            dve.sem_inc(shift_ready, PAIRS)
            turn(0, back1=False, back2=False, back3=False)
            turn(1, back2=False, back3=False)
            dve.wait_ge(rest_loaded, 112)
            turn(2, back3=False)
            with dve.Fori(3, PAIRS) as i:
                turn(i)
            turn(PAIRS, ahead=False)
            turn(PAIRS + 1, ahead=False, back1=False)
            turn(PAIRS + 2, ahead=False, back1=False, back2=False)
            small_operands()

            scores_ = bank[5][:, 0:HEADS * NP].rearrange("p (h n) -> p h n", h=HEADS)
            wide = [P, HEADS, NP]

            def shifted(k):
                dve.wait_ge(s2_done, k + 1)
                dve.tensor_reduce(head_max[:, :], scores_, AX.X, ALU.max).then_inc(head_max_ready, 1)
                dve.wait_ge(head_max_ready, k + 1)
                dve.tensor_tensor(attn, scores_, head_max[:, :].unsqueeze(2).broadcast_to(wide), ALU.subtract)\
                    .then_inc(shifted_ready, 1)

            def normed(k, first=False):
                dve.wait_ge(rstd2_ready, k + 1)
                if not first:
                    dve.wait_ge(n2T_done, k)
                    dve.wait_ge(n2a_ready, k)
                    dve.wait_ge(n2b_ready, k)
                dve.tensor_scalar(n2_now, x2_all[:, bass.ds(k, 1), :].squeeze(1),
                                  mv[:, 0, 0:1], rstd[:, 0:1], ALU.subtract, ALU.mult).then_inc(n2_ready, 1)

            def head_sums(k):
                dve.wait_ge(exp2_done, k + 1)
                dve.tensor_reduce(head_sum[:, :], attn, AX.X, ALU.add).then_inc(head_sum_ready, 1)

            def head_inverse(k):
                dve.wait_ge(head_sum_ready, k + 1)
                dve.wait_ge(o_copied, k)
                dve.reciprocal(head_inv[:, :], head_sum[:, :]).then_inc(head_inv_ready, 1)

            def divided(k):
                dve.wait_ge(pv2_done, k + 1)
                dve.wait_ge(head_inv_ready, k + 1)
                dve.tensor_tensor(o_sb.rearrange("p (v h) -> p h v", h=HEADS), bank[7][:, 0:D].rearrange("p (h v) -> p h v", v=DV),
                                  head_inv[:, :].unsqueeze(2).broadcast_to([P, HEADS, DV]), ALU.mult).then_inc(o_copied, 1)

            def values_by_head(i, p):
                rows = HG * NP
                dve.wait_ge(vrep_done, i + 1)
                for a in range(2):
                    dve.tensor_tensor(v_blk[p][0:rows, 2 * a:2 * a + 2],
                                      bank[2 + a][0:rows, :].rearrange("p (b h v) -> p b h v", b=2, h=HEADS),
                                      v_mask[0:rows, :].unsqueeze(1).unsqueeze(3).broadcast_to([rows, 2, HEADS, DV]),
                                      ALU.mult).then_inc(v_blk_ready, 1)

            def keys_out(i):
                dve.wait_ge(k2_done, i + 1)
                dve.tensor_copy(k_T, bank[1][:, QD:QD + GB * NP].rearrange("p (b n) -> p b n", b=GB)).then_inc(k2_copied, 1)

            def summed(k):
                dve.wait_ge(proj_done, k + 1)
                dve.wait_ge(x1b_ready, k + 1)
                dve.tensor_tensor(x2_all[:, bass.ds(k, 1), :].squeeze(1), bank[4][:, D:2 * D],
                                  x1_all[:, bass.ds(k, 1), :].squeeze(1), ALU.add).then_inc(x2_ready, 1)
                dve.wait_ge(x2_ready, k + 1)
                dve.tensor_copy(seen[:, :], mv[:, 0, 0:1])
                dve.bn_stats(stats[:, 0, :], x2_all[:, bass.ds(k, 1), :].squeeze(1)).then_inc(stat2_ready, 1)
                dve.wait_ge(stat2_ready, k + 1)
                dve.tensor_copy(seen[:, :], stats[:, 0, 0:1])
                dve.bn_aggr(mv[:, 0, :], stats[:, 0, :]).then_inc(mv2_ready, 1)

            def turn(i, p, ahead=True, back1=True, back2=True, back3=True, back4=True):
                if back4:
                    normed(i - 4, first=back4 == "first")
                if back1:
                    shifted(i - 1)
                if ahead:
                    if back2:
                        dve.wait_ge(pv2_done, i - 1)
                    values_by_head(i, p)
                    if back1:
                        dve.wait_ge(k_blk_ready, i)
                    keys_out(i)
                if back1:
                    head_sums(i - 1)
                if back2:
                    divided(i - 2)
                if back1:
                    if back2:
                        head_inverse(i - 1)
                    else:
                        dve.wait_ge(head_sum_ready, i)
                        dve.reciprocal(head_inv[:, :], head_sum[:, :]).then_inc(head_inv_ready, 1)
                if back3:
                    summed(i - 3)

            dve.wait_ge(masks_ready, 11)
            for i in range(4):
                turn(i, i % 2, True, i >= 1, i >= 2, i >= 3, False)
            turn(4, 0, back4="first")
            turn(5, 1)
            with dve.Fori(3, NG // 2) as it:
                for p in range(2):
                    turn(it * 2 + p, p)
            def top_values(n, first, size):
                dve.wait_ge(logits_done, n)
                by_block = [P, size, GB, NE]
                last = slice(first, first + size)
                dve.tensor_tensor(logits.rearrange("p (n a) e -> p n a e", n=4)[:, last],
                                  bank[7][:, :].rearrange("p (a n e) -> p n a e", a=4, e=NL)[:, last, :, 0:NE],
                                  rbias_b[:, :].unsqueeze(1).unsqueeze(1).broadcast_to(by_block), ALU.add).then_inc(logits_ready, 1)
                dve.wait_ge(logits_ready, n)
                for g in range(4 * first, 4 * (first + size)):
                    dve.max(best[:, g, :], logits[:, g, :]).then_inc(best_ready, 1)

            def top_places(first, size):
                for g in range(4 * first, 4 * (first + size)):
                    dve.wait_ge(best_ready, g + 1)
                    dve.max_index(best_at[:, g, :], best[:, g, :], logits[:, g, :]).then_inc(best_at_ready, 1)

            for i in range(NG, NG + 4):
                turn(i, i % 2, False, i < NG + 1, i < NG + 2, i < NG + 3)
                if i == NG + 2:
                    top_values(1, 0, 3)
            top_places(0, 3)

            def shared_hidden(q):
                for hc in range(DH):
                    dve.wait_ge(shared_silu, DH * q + hc + 1)
                    dve.wait_ge(shared_up_done, 2 * DH * q + DH + hc + 1)
                    if q >= 2:
                        dve.wait_ge(shared_done, 4 * (q - 1))
                    dve.tensor_tensor(sh_hid[:, q % 2, hc, :], bank[1 + DH + hc][:, :], sh_silu[:, hc, :], ALU.mult)\
                        .then_inc(shared_hid_ready, 1)

            def shared_add(q):
                for m in range(4 * q, 4 * q + 4):
                    dve.wait_ge(shared_done, m + 1)
                    dve.tensor_tensor(x2_all[:, m, :], x2_all[:, m, :], bank[5 + m % 2][:, 0:D], ALU.add).then_inc(shared_added, 1)

            top_values(2, 3, 1)
            top_places(3, 1)
            dve.wait_ge(best_at_ready, NG)
            dve.tensor_copy(best_f[:, :, :], best_at[:, :, 0:TOPK]).then_inc(best_f_ready, 1)
            dve.wait_ge(best_f_ready, 1)
            wide = [P, NE, NK]
            dve.tensor_tensor(chosen, best_f[:, :, :].rearrange("p g k -> p (g k)").unsqueeze(1).broadcast_to(wide),
                              lane[:, :].unsqueeze(2).broadcast_to(wide), ALU.is_equal).then_inc(chosen_ready, 1)
            dve.wait_ge(chosen_ready, 1)
            dve.wait_ge(dest_ready, TOPK + 2)
            dve.tensor_tensor_scan(counted.rearrange("p e c -> p (e c)"), keep.rearrange("p e c -> p (e c)"),
                                   chosen.rearrange("p e c -> p (e c)"), 0.0, ALU.mult, ALU.add).then_inc(chosen_ready, 1)
            dve.tensor_tensor(gap_w[:, :], best[:, :, 1], best[:, :, 0], ALU.subtract).then_inc(gap_ready, 1)
            shared_hidden(0)
            dve.wait_ge(before_done, 1)
            dve.tensor_scalar(tiles_i[:, :], bank[0][:, 0:NE], float(P - 1), None, ALU.add).then_inc(tiles_step, 1)
            dve.wait_ge(tiles_step, 1)
            dve.tensor_single_scalar(tiles_h[:, :], tiles_i[:, :], P.bit_length() - 1, ALU.logical_shift_right).then_inc(tiles_step, 1)
            dve.wait_ge(tiles_step, 2)
            dve.tensor_copy(tiles_n[:, :], tiles_h[:, :]).then_inc(tiles_step, 1)
            dve.wait_ge(tiles_step, 3)
            dve.tensor_tensor_scan(tiles_to[:, :], ones[:, 0:NE], tiles_n[:, :], 0.0, ALU.mult, ALU.add).then_inc(tiles_step, 1)
            dve.wait_ge(tiles_step, 4)
            dve.tensor_tensor(first_row[:, :], tiles_to[:, :], tiles_n[:, :], ALU.subtract).then_inc(first_ready, 1)
            dve.wait_ge(before_done, 2)
            dve.wait_ge(first_ready, 1)
            dve.scalar_tensor_tensor(place, first_row[:, :].unsqueeze(2).broadcast_to(wide), float(P),
                                     bank[7][:, :].rearrange("p (e c) -> p e c", e=NE), ALU.mult, ALU.add).then_inc(place_step, 1)
            dve.wait_ge(place_step, 1)
            dve.tensor_tensor(place, place, chosen, ALU.mult).then_inc(place_step, 1)
            dve.wait_ge(place_step, 2)
            dve.tensor_reduce(place_f[:, :], place.rearrange("p e c -> p c e"), AX.X, ALU.add).then_inc(place_step, 1)
            dve.wait_ge(place_step, 3)
            dve.tensor_copy(place_i[:, :], place_f[:, :]).then_inc(place_ready, 1)
            shared_hidden(1)
            shared_add(0)
            most = [1, SLOTS + 1, NE]
            dve.tensor_tensor(passed, tile_no[:, :].unsqueeze(2).broadcast_to(most),
                              tiles_to[0:1, :].unsqueeze(1).broadcast_to(most), ALU.is_ge).then_inc(expert_step, 1)
            dve.wait_ge(expert_step, 1)
            dve.tensor_reduce(expert_f[:, :], passed, AX.X, ALU.add).then_inc(expert_step, 1)
            dve.wait_ge(expert_step, 2)
            dve.tensor_scalar(expert_m[:, :], expert_f[:, :], float(NE - 1), None, ALU.min).then_inc(expert_step, 1)
            dve.wait_ge(expert_step, 3)
            dve.tensor_copy(experts_i[:, 1:SLOTS + 2], expert_m[:, :]).then_inc(expert_step, 1)
            for q in range(2, 4):
                shared_hidden(q)
                shared_add(q - 1)
            shared_add(3)
            dve.wait_ge(gap_exp, 1)
            dve.tensor_scalar(gap_s[:, :], gap_e[:, :], 1.0, None, ALU.add).then_inc(gap_sum_ready, 1)
            dve.wait_ge(gap_sum_ready, 1)
            dve.reciprocal(mix[:, 0, :], gap_s[:, :]).then_inc(mix_ready, 1)
            dve.wait_ge(mix_ready, 1)
            dve.tensor_tensor(mix[:, 1, :], gap_e[:, :], mix[:, 0, :], ALU.mult).then_inc(mix_ready, 1)

            def dest_of(s, r, round_):
                dve.wait_ge(row_loaded[r], round_ * 16 + 16)
                dve.tensor_copy(dest[:, bass.ds(s, 1)], row_in[:, r, D:ROW].bitcast(u32)).then_inc(dest_copied, 1)

            def hidden(s, p):
                dve.wait_ge(silu_done, s + 1)
                dve.tensor_tensor(hid[:, p, :], bank[2 + p][:, HID:2 * HID], silu_g[:, p, :], ALU.mult).then_inc(hid_ready, 1)

            def result(s, r, round_, first=False):
                if not first:
                    dve.wait_ge(y_sent[r], round_ * 16)
                dve.wait_ge(down_done, s + 1)
                dve.tensor_copy(y_sb[:, r, :], bank[6 + r % 2][:, 0:D]).then_inc(y_ready, 1)

            def turn(s, r, round_, first=False):
                dest_of(s, r, round_)
                hidden(s - 1, (r - 1) % 2)
                result(s - 3, (r - 3) % ROWS, round_ - (1 if r < 3 else 0), first)

            for s in range(ROWS):
                dest_of(s, s, 0)
                if s >= 1:
                    hidden(s - 1, (s - 1) % 2)
                if s >= 3:
                    result(s - 3, s - 3, 0, first=True)
            for s in range(ROWS, 2 * ROWS):
                turn(s, s % ROWS, 1, first=s < ROWS + 3)
            with dve.Fori(2, SLOTS // ROWS) as it:
                for r in range(ROWS):
                    turn(it * ROWS + r, r, it)
            for s in range(SLOTS // ROWS * ROWS, SLOTS):
                turn(s, s % ROWS, s // ROWS)
            for s in range(SLOTS, SLOTS + 3):
                if s == SLOTS:
                    hidden(s - 1, (s - 1) % 2)
                result(s - 3, (s - 3) % ROWS, (s - 3) // ROWS)

            for n, size in enumerate(CHUNKS):
                first = sum(CHUNKS[:n])
                dve.wait_ge(y_loaded[n], 16 * TOPK)
                dve.wait_ge(mix_ready, 2)
                for k in range(TOPK):
                    for a in range(size):
                        g = first + a
                        if k:
                            dve.wait_ge(mixed_ready, TOPK * first + a + 1)
                        dve.scalar_tensor_tensor(x2_all[:, g, :], y_all[k][:, g, :], mix[:, k, g:g + 1], x2_all[:, g, :],
                                                 ALU.mult, ALU.add).then_inc(mixed_ready, 1)


_INS = ["x", "ctx_1024", "L0_xattn_Wq", "L0_xattn_bq", "L0_xattn_Wk", "L0_xattn_bk", "L0_xattn_Wv", "L0_xattn_bv",
        "L0_xattn_gamma", "L0_xattn_beta", "L0_attn_w_kv", "L0_attn_w_q", "L0_attn_b_q", "L0_attn_w_out", "L0_attn_b_out",
        "L0_ffn_router_w", "L0_ffn_router_bias", "L0_ffn_up_proj", "L0_ffn_gate_proj", "L0_ffn_down_proj",
        "L0_ffn_sh_gate", "L0_ffn_sh_up", "L0_ffn_sh_down"]


def kernel(**inputs):
    import numpy as _np
    import concourse.bacc as _bacc
    from concourse import mybir as _mybir
    from concourse.bass_utils import run_bass_kernel_spmd as _run

    nc = _bacc.Bacc("TRN2", target_bir_lowering=False, num_devices=1)
    arrays, tensors = {}, {}
    for name in _INS:
        a = _np.ascontiguousarray(inputs[name])
        arrays[f"in_{name}_dram"] = a
        tensors[name] = nc.dram_tensor(f"in_{name}_dram", a.shape, _mybir.dt.from_np(a.dtype), kind="ExternalInput").ap()
    shape = inputs["x"].shape
    out = nc.dram_tensor("out_dram", shape, _mybir.dt.from_np(_np.dtype("float32")), kind="ExternalOutput").ap()
    perceiver_layer(nc, tensors, out)
    r = _run(nc, [arrays], core_ids=[0])
    return r.results[0]["out_dram"]
```
